# Optimizing a Trainium2 kernel written in Bass

```python
import numpy as np
import jax
import jax.numpy as jnp

def _softmax(x, axis=-1):
    return jax.nn.softmax(x, axis=axis)

def _gelu(x):
    return jax.nn.gelu(x, approximate=True)

def _silu(x):
    return jax.nn.silu(x)

def _sigmoid(x):
    return jax.nn.sigmoid(x)

def _layernorm(x, axis=-1, eps=1e-05):
    m = jnp.mean(x, axis=axis, keepdims=True)
    v = jnp.var(x, axis=axis, keepdims=True)
    return (x - m) / jnp.sqrt(v + eps)

def _scatter_add(tgt, idx, src, axis=0):
    return tgt.at[idx].add(src)

def _segment_sum(src, seg, n):
    return jax.ops.segment_sum(src, seg, n)
kernel_name = 'mk_gnn_preln_d4_gnn_r8_e10eb0'

def setup_inputs(seed: int=0):
    np.random.seed(seed)
    _w = jnp.asarray

    def _rec_inputs():
        import jax
        import jax.numpy as jnp
        _gk = jax.random.key(seed)
        x = -0.0005121 + 1.001 * jax.random.normal(jax.random.fold_in(_gk, 1), (6250, 64), jnp.float32)
        src = jax.random.randint(jax.random.fold_in(_gk, 2), (200000,), 0, 6250, jnp.int32)
        dst = jnp.minimum((6250 * jax.random.uniform(jax.random.fold_in(_gk, 3), (200000,)) ** 2.0).astype(jnp.int32), 49999)
        _o = jnp.argsort(dst, stable=True)
        src = src[_o]
        dst = dst[_o]
        edge_attr_64 = 1.36993e-05 + 0.999972 * jax.random.normal(jax.random.fold_in(_gk, 12), (200000, 64), jnp.float32)
        edge_attr_9 = 0.000739051 + 0.999958 * jax.random.normal(jax.random.fold_in(_gk, 13), (200000, 9), jnp.float32)
        edge_weight = jax.random.uniform(jax.random.fold_in(_gk, 15), (200000,), jnp.float32, 0.0, 1)
        return (x, src, dst, edge_attr_64, edge_attr_9, edge_weight)
    x, src, dst, edge_attr_64, edge_attr_9, edge_weight = _rec_inputs()

    def _L0_gnn_setup():
        import jax, jax.numpy as jnp
        import numpy as np
        N = 6250
        E = 150000
        D_IN = 64
        D_H = 64
        L = 3
        TAU = 1.0
        EPS = 1e-30
        LN_EPS = 1e-05
        ALPHA = 0.5

        def scatter_logsumexp(src, index, n, tau=TAU, eps=EPS):
            scaled = src.astype(jnp.float32) / tau
            max_val = jax.ops.segment_max(scaled, index, num_segments=n)
            exp_val = jnp.exp(scaled - max_val[index])
            sum_exp = jax.ops.segment_sum(exp_val, index, num_segments=n)
            deg = jnp.bincount(index, length=n)
            has_nbr = (deg > 0)[:, None]
            max_safe = jnp.where(has_nbr, max_val, 0.0)
            out = tau * (max_safe + jnp.log(jnp.maximum(sum_exp, eps)))
            return jnp.where(has_nbr, out, 0.0).astype(src.dtype)

        def layer_norm(h, gamma, beta):
            mu = jnp.mean(h, axis=-1, keepdims=True)
            var = jnp.var(h, axis=-1, keepdims=True)
            return (h - mu) * jax.lax.rsqrt(var + LN_EPS) * gamma + beta
        key = jax.random.key(seed)
        ks = jax.random.split(key, 8)
        x = jax.random.normal(ks[0], (N, D_IN), dtype=jnp.float32)
        edge_src = jax.random.randint(ks[1], (E,), 0, N)
        edge_dst = jax.random.randint(ks[2], (E,), 0, N)
        s_in = 1.0 / np.sqrt(D_IN)
        s_l = 1.0 / np.sqrt(2 * D_H)
        W_in = jax.random.uniform(ks[3], (D_H, D_IN), minval=-s_in, maxval=s_in, dtype=jnp.float32)
        b_in = jax.random.uniform(ks[4], (D_H,), minval=-s_in, maxval=s_in, dtype=jnp.float32)
        W_l = jax.random.uniform(ks[5], (L, D_H, 2 * D_H), minval=-s_l, maxval=s_l, dtype=jnp.float32)
        b_l = jax.random.uniform(ks[6], (L, D_H), minval=-s_l, maxval=s_l, dtype=jnp.float32)
        gamma_l = jnp.ones((L, D_H), dtype=jnp.float32)
        beta_l = jnp.zeros((L, D_H), dtype=jnp.float32)
        return {'x': x, 'edge_src': edge_src, 'edge_dst': edge_dst, 'W_in': W_in, 'b_in': b_in, 'W_l': W_l, 'b_l': b_l, 'gamma_l': gamma_l, 'beta_l': beta_l}
    _L0_gnn_all = _L0_gnn_setup()
    _L0_gnn_in = {k: v for k, v in _L0_gnn_all.items() if k in ('W_in', 'b_in', 'W_l', 'b_l', 'gamma_l', 'beta_l')}
    del _L0_gnn_all

    def _L1_gnn_setup():
        import jax, jax.numpy as jnp
        import numpy as np
        N_NODES = 12500
        N_EDGES = 200000
        D = 64
        BN_EPS = 1e-05

        def _bn(x, gamma, beta):
            mu = jnp.mean(x, axis=0)
            var = jnp.var(x, axis=0)
            return gamma * (x - mu) * jax.lax.rsqrt(var + BN_EPS) + beta
        key = jax.random.key(seed)
        ks = jax.random.split(key, 8)
        h = jax.random.normal(ks[0], (N_NODES, D), dtype=jnp.float32)
        edge_weight = jax.random.uniform(ks[1], (N_EDGES,), dtype=jnp.float32)
        src = jax.random.randint(ks[2], (N_EDGES,), 0, N_NODES)
        dst = jax.random.randint(ks[3], (N_EDGES,), 0, N_NODES)
        W1 = jax.random.normal(ks[4], (D, D), dtype=jnp.float32) * (1.0 / np.sqrt(D))
        W2 = jax.random.normal(ks[5], (D, D), dtype=jnp.float32) * (1.0 / np.sqrt(D))
        return {'h': h, 'edge_weight': edge_weight, 'src': src, 'dst': dst, 'W1': W1, 'b1': jnp.zeros((D,), jnp.float32), 'gamma1': jnp.ones((D,), jnp.float32), 'beta1': jnp.zeros((D,), jnp.float32), 'W2': W2, 'b2': jnp.zeros((D,), jnp.float32), 'gamma2': jnp.ones((D,), jnp.float32), 'beta2': jnp.zeros((D,), jnp.float32)}
    _L1_gnn_all = _L1_gnn_setup()
    _L1_gnn_in = {k: v for k, v in _L1_gnn_all.items() if k in ('W1', 'b1', 'gamma1', 'beta1', 'W2', 'b2', 'gamma2', 'beta2')}
    del _L1_gnn_all

    def _L2_gnn_setup():
        import jax, jax.numpy as jnp
        import numpy as np
        N, E = (1250, 40000)
        D, S, HE = (64, 9, 64)
        H, DQK, DV = (8, 16, 16)
        OK, OV = (H * DQK, H * DV)
        EPS_BN = 1e-05

        def tensor_product(x_e, sh, w, C):
            acc = sh[:, 0:1] * (x_e @ C[:, 0, :])
            for s in range(1, S):
                acc = acc + sh[:, s:s + 1] * (x_e @ C[:, s, :])
            return acc * w

        def mlp2(x, w1, b1, w2, b2):
            return jax.nn.relu(x @ w1 + b1) @ w2 + b2
        key = jax.random.key(seed)
        ks = jax.random.split(key, 20)
        g = lambda k, shape, fan: jax.random.normal(k, shape, jnp.float32) / np.float32(np.sqrt(fan))
        return {'tfn_features': jax.random.normal(ks[0], (N, D), jnp.float32), 'edge_features': jax.random.normal(ks[1], (E, HE), jnp.float32), 'edge_sh': jax.random.normal(ks[2], (E, S), jnp.float32), 'Wq': g(ks[3], (D, OK), D), 'Cqk': g(ks[4], (D, S, OK), D * S), 'Cv': g(ks[5], (D, S, OV), D * S), 'k_w1': g(ks[6], (HE, HE), HE), 'k_b1': jnp.zeros((HE,), jnp.float32), 'k_w2': g(ks[7], (HE, OK), HE), 'k_b2': jnp.zeros((OK,), jnp.float32), 'v_w1': g(ks[8], (HE, HE), HE), 'v_b1': jnp.zeros((HE,), jnp.float32), 'v_w2': g(ks[9], (HE, OV), HE), 'v_b2': jnp.zeros((OV,), jnp.float32), 'W_out': g(ks[10], (OV, D), OV), 'W_self': g(ks[11], (D, D), D), 'gamma': jnp.ones((D,), jnp.float32), 'beta': jnp.zeros((D,), jnp.float32), 'edge_index': jax.random.randint(ks[12], (2, E), 0, N, dtype=jnp.int32)}
    _L2_gnn_all = _L2_gnn_setup()
    _L2_gnn_in = {k: v for k, v in _L2_gnn_all.items() if k in ('Wq', 'Cqk', 'Cv', 'k_w1', 'k_b1', 'k_w2', 'k_b2', 'v_w1', 'v_b1', 'v_w2', 'v_b2', 'W_out', 'W_self', 'gamma', 'beta')}
    del _L2_gnn_all

    def _L3_gnn_setup():
        import jax, jax.numpy as jnp
        import numpy as np
        N_NODES = 6250
        N_EDGES = 100000
        D = 64
        NEG_SLOPE = 0.2

        def _gat_conv(x, src, dst, W, a_src, a_dst, b, n_nodes):
            h = x @ W
            alpha_s = h @ a_src
            alpha_d = h @ a_dst
            e = alpha_s[src] + alpha_d[dst]
            e = jnp.where(e > 0, e, NEG_SLOPE * e)
            m = jax.ops.segment_max(e, dst, num_segments=n_nodes)
            m = jnp.where(jnp.isfinite(m), m, 0.0)
            ex = jnp.exp(e - m[dst])
            s = jax.ops.segment_sum(ex, dst, num_segments=n_nodes)
            alpha = ex / (s[dst] + 1e-16)
            out = jax.ops.segment_sum(alpha[:, None] * h[src], dst, num_segments=n_nodes)
            return out + b

        def _add_self_loops(edge_index, n_nodes):
            loop = jnp.arange(n_nodes, dtype=edge_index.dtype)
            src = jnp.concatenate([edge_index[0], loop])
            dst = jnp.concatenate([edge_index[1], loop])
            return (src, dst)
        key = jax.random.key(seed)
        ks = jax.random.split(key, 16)
        x = jax.random.normal(ks[0], (N_NODES, D), dtype=jnp.float32)
        edge_index = jax.random.randint(ks[1], (2, N_EDGES), 0, N_NODES, dtype=jnp.int32)
        sc = 1.0 / np.sqrt(D)

        def lin(k):
            return jax.random.uniform(k, (D, D), jnp.float32, -sc, sc)

        def att(k):
            return jax.random.uniform(k, (D,), jnp.float32, -sc, sc)
        return {'x': x, 'edge_index': edge_index, 'W1': lin(ks[2]), 'a1s': att(ks[3]), 'a1d': att(ks[4]), 'b1': jnp.zeros((D,), jnp.float32), 'W2': lin(ks[5]), 'a2s': att(ks[6]), 'a2d': att(ks[7]), 'b2': jnp.zeros((D,), jnp.float32), 'W3': lin(ks[8]), 'a3s': att(ks[9]), 'a3d': att(ks[10]), 'b3': jnp.zeros((D,), jnp.float32)}
    _L3_gnn_all = _L3_gnn_setup()
    _L3_gnn_in = {k: v for k, v in _L3_gnn_all.items() if k in ('W1', 'a1s', 'a1d', 'b1', 'W2', 'a2s', 'a2d', 'b2', 'W3', 'a3s', 'a3d', 'b3')}
    del _L3_gnn_all
    return {'x': x, 'src': src, 'dst': dst, 'edge_attr_64': edge_attr_64, 'edge_attr_9': edge_attr_9, 'edge_weight': edge_weight, 'L0_gnn_W_in': _L0_gnn_in['W_in'], 'L0_gnn_b_in': _L0_gnn_in['b_in'], 'L0_gnn_W_l': _L0_gnn_in['W_l'], 'L0_gnn_b_l': _L0_gnn_in['b_l'], 'L0_gnn_gamma_l': _L0_gnn_in['gamma_l'], 'L0_gnn_beta_l': _L0_gnn_in['beta_l'], 'L1_gnn_W1': _L1_gnn_in['W1'], 'L1_gnn_b1': _L1_gnn_in['b1'], 'L1_gnn_gamma1': _L1_gnn_in['gamma1'], 'L1_gnn_beta1': _L1_gnn_in['beta1'], 'L1_gnn_W2': _L1_gnn_in['W2'], 'L1_gnn_b2': _L1_gnn_in['b2'], 'L1_gnn_gamma2': _L1_gnn_in['gamma2'], 'L1_gnn_beta2': _L1_gnn_in['beta2'], 'L2_gnn_Wq': _L2_gnn_in['Wq'], 'L2_gnn_Cqk': _L2_gnn_in['Cqk'], 'L2_gnn_Cv': _L2_gnn_in['Cv'], 'L2_gnn_k_w1': _L2_gnn_in['k_w1'], 'L2_gnn_k_b1': _L2_gnn_in['k_b1'], 'L2_gnn_k_w2': _L2_gnn_in['k_w2'], 'L2_gnn_k_b2': _L2_gnn_in['k_b2'], 'L2_gnn_v_w1': _L2_gnn_in['v_w1'], 'L2_gnn_v_b1': _L2_gnn_in['v_b1'], 'L2_gnn_v_w2': _L2_gnn_in['v_w2'], 'L2_gnn_v_b2': _L2_gnn_in['v_b2'], 'L2_gnn_W_out': _L2_gnn_in['W_out'], 'L2_gnn_W_self': _L2_gnn_in['W_self'], 'L2_gnn_gamma': _L2_gnn_in['gamma'], 'L2_gnn_beta': _L2_gnn_in['beta'], 'L3_gnn_W1': _L3_gnn_in['W1'], 'L3_gnn_a1s': _L3_gnn_in['a1s'], 'L3_gnn_a1d': _L3_gnn_in['a1d'], 'L3_gnn_b1': _L3_gnn_in['b1'], 'L3_gnn_W2': _L3_gnn_in['W2'], 'L3_gnn_a2s': _L3_gnn_in['a2s'], 'L3_gnn_a2d': _L3_gnn_in['a2d'], 'L3_gnn_b2': _L3_gnn_in['b2'], 'L3_gnn_W3': _L3_gnn_in['W3'], 'L3_gnn_a3s': _L3_gnn_in['a3s'], 'L3_gnn_a3d': _L3_gnn_in['a3d'], 'L3_gnn_b3': _L3_gnn_in['b3']}

def reference(x, src, dst, edge_attr_64, edge_attr_9, edge_weight, L0_gnn_W_in, L0_gnn_b_in, L0_gnn_W_l, L0_gnn_b_l, L0_gnn_gamma_l, L0_gnn_beta_l, L1_gnn_W1, L1_gnn_b1, L1_gnn_gamma1, L1_gnn_beta1, L1_gnn_W2, L1_gnn_b2, L1_gnn_gamma2, L1_gnn_beta2, L2_gnn_Wq, L2_gnn_Cqk, L2_gnn_Cv, L2_gnn_k_w1, L2_gnn_k_b1, L2_gnn_k_w2, L2_gnn_k_b2, L2_gnn_v_w1, L2_gnn_v_b1, L2_gnn_v_w2, L2_gnn_v_b2, L2_gnn_W_out, L2_gnn_W_self, L2_gnn_gamma, L2_gnn_beta, L3_gnn_W1, L3_gnn_a1s, L3_gnn_a1d, L3_gnn_b1, L3_gnn_W2, L3_gnn_a2s, L3_gnn_a2d, L3_gnn_b2, L3_gnn_W3, L3_gnn_a3s, L3_gnn_a3d, L3_gnn_b3):
    import jax
    import jax.numpy as jnp

    def _L0_gnn_ref(x, edge_src, edge_dst, W_in, b_in, W_l, b_l, gamma_l, beta_l):
        import jax, jax.numpy as jnp
        import numpy as np
        N = 6250
        E = 150000
        D_IN = 64
        D_H = 64
        L = 3
        TAU = 1.0
        EPS = 1e-30
        LN_EPS = 1e-05
        ALPHA = 0.5

        def scatter_logsumexp(src, index, n, tau=TAU, eps=EPS):
            scaled = src.astype(jnp.float32) / tau
            max_val = jax.ops.segment_max(scaled, index, num_segments=n)
            exp_val = jnp.exp(scaled - max_val[index])
            sum_exp = jax.ops.segment_sum(exp_val, index, num_segments=n)
            deg = jnp.bincount(index, length=n)
            has_nbr = (deg > 0)[:, None]
            max_safe = jnp.where(has_nbr, max_val, 0.0)
            out = tau * (max_safe + jnp.log(jnp.maximum(sum_exp, eps)))
            return jnp.where(has_nbr, out, 0.0).astype(src.dtype)

        def layer_norm(h, gamma, beta):
            mu = jnp.mean(h, axis=-1, keepdims=True)
            var = jnp.var(h, axis=-1, keepdims=True)
            return (h - mu) * jax.lax.rsqrt(var + LN_EPS) * gamma + beta
        h = x @ W_in.T + b_in
        for i in range(L):
            src_feat = h[edge_src]
            agg = scatter_logsumexp(src_feat, edge_dst, N)
            hc = jnp.concatenate([h, agg], axis=-1)
            h_new = hc @ W_l[i].T + b_l[i]
            h_new = jax.nn.relu(layer_norm(h_new, gamma_l[i], beta_l[i]))
            h = ALPHA * h + (1.0 - ALPHA) * h_new
        return h

    def _L1_gnn_ref(h, edge_weight, src, dst, W1, b1, gamma1, beta1, W2, b2, gamma2, beta2):
        import jax, jax.numpy as jnp
        import numpy as np
        N_NODES = 12500
        N_EDGES = 200000
        D = 64
        BN_EPS = 1e-05

        def _bn(x, gamma, beta):
            mu = jnp.mean(x, axis=0)
            var = jnp.var(x, axis=0)
            return gamma * (x - mu) * jax.lax.rsqrt(var + BN_EPS) + beta
        msg = h[src] * edge_weight[:, None]
        agg = jax.ops.segment_sum(msg, dst, num_segments=h.shape[0])
        x = agg + h
        x = jax.nn.relu(_bn(x @ W1 + b1, gamma1, beta1))
        x = jax.nn.relu(_bn(x @ W2 + b2, gamma2, beta2))
        return x

    def _L2_gnn_ref(tfn_features, edge_features, edge_sh, Wq, Cqk, Cv, k_w1, k_b1, k_w2, k_b2, v_w1, v_b1, v_w2, v_b2, W_out, W_self, gamma, beta, edge_index):
        import jax, jax.numpy as jnp
        import numpy as np
        N, E = (1250, 40000)
        D, S, HE = (64, 9, 64)
        H, DQK, DV = (8, 16, 16)
        OK, OV = (H * DQK, H * DV)
        EPS_BN = 1e-05

        def tensor_product(x_e, sh, w, C):
            acc = sh[:, 0:1] * (x_e @ C[:, 0, :])
            for s in range(1, S):
                acc = acc + sh[:, s:s + 1] * (x_e @ C[:, s, :])
            return acc * w

        def mlp2(x, w1, b1, w2, b2):
            return jax.nn.relu(x @ w1 + b1) @ w2 + b2
        edge_dst, edge_src = (edge_index[0], edge_index[1])
        n = tfn_features.shape[0]
        q = (tfn_features @ Wq).reshape(n, H, DQK)
        x_dst = tfn_features[edge_dst]
        wk = mlp2(edge_features, k_w1, k_b1, k_w2, k_b2)
        wv = mlp2(edge_features, v_w1, v_b1, v_w2, v_b2)
        k = tensor_product(x_dst, edge_sh, wk, Cqk).reshape(-1, H, DQK)
        v = tensor_product(x_dst, edge_sh, wv, Cv).reshape(-1, H, DV)
        attn = jnp.einsum('ehd,ehd->eh', q[edge_src], k)
        amax = jax.ops.segment_max(attn, edge_src, num_segments=n)
        ex = jnp.exp(attn - amax[edge_src])
        denom = jax.ops.segment_sum(ex, edge_src, num_segments=n)
        alpha = ex / (denom[edge_src] + 1e-16)
        upd = jax.ops.segment_sum(v * alpha[..., None], edge_src, num_segments=n)
        upd = upd.reshape(n, OV) @ W_out
        out = tfn_features @ W_self + upd
        mu = out.mean(axis=0)
        var = out.var(axis=0)
        return (out - mu) * jax.lax.rsqrt(var + EPS_BN) * gamma + beta

    def _L3_gnn_ref(x, edge_index, W1, a1s, a1d, b1, W2, a2s, a2d, b2, W3, a3s, a3d, b3):
        import jax, jax.numpy as jnp
        import numpy as np
        N_NODES = 6250
        N_EDGES = 100000
        D = 64
        NEG_SLOPE = 0.2

        def _gat_conv(x, src, dst, W, a_src, a_dst, b, n_nodes):
            h = x @ W
            alpha_s = h @ a_src
            alpha_d = h @ a_dst
            e = alpha_s[src] + alpha_d[dst]
            e = jnp.where(e > 0, e, NEG_SLOPE * e)
            m = jax.ops.segment_max(e, dst, num_segments=n_nodes)
            m = jnp.where(jnp.isfinite(m), m, 0.0)
            ex = jnp.exp(e - m[dst])
            s = jax.ops.segment_sum(ex, dst, num_segments=n_nodes)
            alpha = ex / (s[dst] + 1e-16)
            out = jax.ops.segment_sum(alpha[:, None] * h[src], dst, num_segments=n_nodes)
            return out + b

        def _add_self_loops(edge_index, n_nodes):
            loop = jnp.arange(n_nodes, dtype=edge_index.dtype)
            src = jnp.concatenate([edge_index[0], loop])
            dst = jnp.concatenate([edge_index[1], loop])
            return (src, dst)
        n = x.shape[0]
        src, dst = _add_self_loops(edge_index, n)
        h = _gat_conv(x, src, dst, W1, a1s, a1d, b1, n)
        h = jax.nn.relu(h)
        h = _gat_conv(h, src, dst, W2, a2s, a2d, b2, n)
        h = jax.nn.relu(h)
        return _gat_conv(h, src, dst, W3, a3s, a3d, b3, n)
    edge_index = jnp.stack([src, dst])
    h = jnp.maximum(_layernorm(x, axis=-1), 0.0)
    x = x + _L0_gnn_ref(h, src, dst, L0_gnn_W_in, L0_gnn_b_in, L0_gnn_W_l, L0_gnn_b_l, L0_gnn_gamma_l, L0_gnn_beta_l)
    h = jnp.maximum(_layernorm(x, axis=-1), 0.0)
    x = x + _L1_gnn_ref(h, edge_weight, src, dst, L1_gnn_W1, L1_gnn_b1, L1_gnn_gamma1, L1_gnn_beta1, L1_gnn_W2, L1_gnn_b2, L1_gnn_gamma2, L1_gnn_beta2)
    h = jnp.maximum(_layernorm(x, axis=-1), 0.0)
    x = x + _L2_gnn_ref(h, edge_attr_64, edge_attr_9, L2_gnn_Wq, L2_gnn_Cqk, L2_gnn_Cv, L2_gnn_k_w1, L2_gnn_k_b1, L2_gnn_k_w2, L2_gnn_k_b2, L2_gnn_v_w1, L2_gnn_v_b1, L2_gnn_v_w2, L2_gnn_v_b2, L2_gnn_W_out, L2_gnn_W_self, L2_gnn_gamma, L2_gnn_beta, edge_index)
    h = jnp.maximum(_layernorm(x, axis=-1), 0.0)
    x = x + _L3_gnn_ref(h, edge_index, L3_gnn_W1, L3_gnn_a1s, L3_gnn_a1d, L3_gnn_b1, L3_gnn_W2, L3_gnn_a2s, L3_gnn_a2d, L3_gnn_b2, L3_gnn_W3, L3_gnn_a3s, L3_gnn_a3d, L3_gnn_b3)
    return x

_drawn_inputs = setup_inputs


def setup_inputs(seed=0):
    import zlib

    import numpy as np

    out = dict(_drawn_inputs(seed))
    spreads = {'L0_gnn_gamma_l': (1.0, 0.2),
     'L0_gnn_beta_l': (0.0, 0.1),
     'L1_gnn_b1': (0.0, 2.0),
     'L1_gnn_gamma1': (1.0, 0.2),
     'L1_gnn_beta1': (0.0, 0.1),
     'L1_gnn_b2': (0.0, 2.0),
     'L1_gnn_gamma2': (1.0, 0.2),
     'L1_gnn_beta2': (0.0, 0.1),
     'L2_gnn_k_b1': (0.0, 0.1),
     'L2_gnn_k_b2': (0.0, 0.1),
     'L2_gnn_v_b1': (0.0, 0.281),
     'L2_gnn_v_b2': (0.0, 0.1),
     'L2_gnn_gamma': (1.0, 0.2),
     'L2_gnn_beta': (0.0, 0.1),
     'L3_gnn_b1': (0.0, 0.8),
     'L3_gnn_b2': (0.0, 0.423),
     'L3_gnn_b3': (0.0, 0.1)}
    factors = {'L0_gnn_b_in': 3.39,
     'L3_gnn_W1': 3.133,
     'L3_gnn_a1s': 8.0,
     'L3_gnn_a1d': 64.0,
     'L3_gnn_W2': 2.711,
     'L3_gnn_a2s': 8.0,
     'L3_gnn_a2d': 8.0,
     'L3_gnn_a3s': 8.0,
     'L3_gnn_a3d': 8.0}
    for name, (base, spread) in spreads.items():
        noise = np.random.default_rng([zlib.crc32(name.encode()), seed]).standard_normal(out[name].shape)
        drawn = base * np.exp(spread * noise) if base else spread * noise
        out[name] = jnp.asarray(drawn.astype(out[name].dtype))
    for name, factor in factors.items():
        out[name] = (out[name] * factor).astype(out[name].dtype)
    return out
```

```python
import concourse.bass as bass
from concourse import mybir
from contextlib import ExitStack

F32 = mybir.dt.float32
I32 = mybir.dt.int32
BF16 = mybir.dt.bfloat16
ALU = mybir.AluOpType
ACT = mybir.ActivationFunctionType
X = mybir.AxisListType.X

LAYERS = (0, 1, 2, 3)
P = 128
N, E, D = 6250, 200000, 64
NT = -(-N // P)
NP = NT * P
LAST = N - (NT - 1) * P
T = 49
PAIRS = -(-E // (P * 2 * T))
CHUNK = PAIRS * 2 * T
EP = P * CHUNK
T2 = T * 4 // 7
PAIRS2 = CHUNK // (2 * T2)
S, O, H, DH = 9, 128, 8, 16
NEG = -1.0e37
GROUPS = [(g, min(4, NT - g)) for g in range(0, NT, 4)]


class Signal:

    def __init__(self, ctx, nc, name):
        self.sem = ctx.enter_context(nc.semaphore(name))
        self.base = 0


def build_program(nc, a, out):
    ctx = ExitStack()
    with ctx:
        used_names = {}

        def sb(stack, name, shape, dt=F32):
            used_names[name] = used_names.get(name, 0) + 1
            return stack.enter_context(nc.sbuf_tensor(f"{name}_{used_names[name]}", shape, dt))

        def dram(name, shape, dt=F32):
            return nc.dram_tensor(name, shape, dt, kind="Internal").ap()

        def signal(name):
            return Signal(ctx, nc, name)

        vec = signal("vec_done")
        act = signal("act_done")
        mm = signal("pe_done")
        mm2 = signal("pe_products_done")
        pool = signal("pool_done")
        loaded = signal("loaded")
        stored = signal("stored")
        rows = signal("rows_gathered")
        chunk_rows = signal("chunk_rows_gathered")

        bank = [ctx.enter_context(nc.psum_tensor(f"bank{k}", [P, 512], F32)) for k in range(8)]

        x_sb = sb(ctx, "x_sb", [P, NT, D])
        hc = sb(ctx, "hc", [P, NT, 2 * D])
        h_sb = hc[:, :, 0:D]
        agg = hc[:, :, D:2 * D]
        ident = sb(ctx, "ident", [P, P])
        ones = sb(ctx, "ones", [P, P])
        ones_last = sb(ctx, "ones_last", [P, P])
        src_i = sb(ctx, "src_i", [P, CHUNK], I32)
        dst_i = sb(ctx, "dst_i", [P, CHUNK], I32)
        neg = sb(ctx, "neg", [P, CHUNK])
        negrow = sb(ctx, "negrow", [P, P])
        controw = sb(ctx, "controw", [P, P])
        has = sb(ctx, "has", [P, NT])
        nocarry = sb(ctx, "nocarry", [P, NT])
        last_i = sb(ctx, "last_i", [P, NT], I32)
        last144_i = sb(ctx, "last144_i", [P, NT], I32)
        first_i = sb(ctx, "first_i", [P, NT], I32)
        holder = sb(ctx, "holder", [P, 2])
        chunk_dst = sb(ctx, "chunk_dst", [P, 1], I32)

        table = dram("table", [NP, D])
        table_q = dram("table_q", [NP, O])
        table_a = dram("table_a", [NP, D + 2])
        record128 = dram("record128", [EP, 2 * D])
        record64 = dram("record64", [EP, D])
        record144 = dram("record144", [P * (CHUNK + T2), O + 2 * H])
        record66 = dram("record66", [EP, D + 2])
        selection = dram("selection", [P, NP])
        spare = dram("spare", [2, P, 1])
        by_first = dram("by_first", [EP + NP, 1])

        def nodes(t):
            return t.rearrange("(j p) f -> p j f", p=P)

        def edges(t):
            return t.rearrange("(c t) f -> c t f", c=P)

        def over(ap, n):
            return ap.unsqueeze(2).to_broadcast([ap.shape[0], ap.shape[1], n])

        def along(ap, n):
            return ap.unsqueeze(1).to_broadcast([ap.shape[0], n, ap.shape[1]])

        def step(eng, ins, sig, k):
            ins.then_inc(sig.sem, 1)
            eng.wait_ge(sig.sem, sig.base + k)

        def load_and_flags():
            with ExitStack() as st:
                prev_i = sb(st, "prev_i", [P, CHUNK], I32)
                dstf = sb(st, "dstf", [P, 2, CHUNK])
                anystart = sb(st, "anystart", [P, 1])
                anyrow = sb(st, "anyrow", [P, P])
                with nc.Block() as block:
                    @block.sync
                    def _(sp):
                        sp.dma_start(dst_i[:, :], a["dst_ext"][1:1 + EP].rearrange("(c t) -> c t", c=P)).then_inc(loaded.sem, 16)
                        sp.dma_start(prev_i[:, :], a["dst_ext"][0:EP].rearrange("(c t) -> c t", c=P)).then_inc(loaded.sem, 16)
                        sp.dma_start(src_i[:, :], a["src_pad"].rearrange("(c t) -> c t", c=P)).then_inc(loaded.sem, 16)
                        sp.wait_ge(vec.sem, vec.base + 1)
                        sp.dma_start(x_sb[:, 0:NT - 1, :], a["x"][0:P * (NT - 1), :].rearrange("(j p) f -> p j f", p=P)).then_inc(loaded.sem, 16)
                        sp.dma_start(x_sb[0:LAST, NT - 1, :], a["x"][P * (NT - 1):N, :]).then_inc(loaded.sem, 16)

                    @block.gpsimd
                    def _(g):
                        g.memset(holder[:, :], 0.0)
                        step(g, g.memset(ident[:, :], 0.0), pool, 1)
                        step(g, g.affine_select(out=ident[:, :], in_=ident[:, :], compare_op=ALU.not_equal, fill=1.0,
                                                base=0, pattern=[[-1, P]], channel_multiplier=1), pool, 2)
                        step(g, g.memset(ones[:, :], 1.0), pool, 3)
                        g.affine_select(out=ones_last[:, :], in_=ones[:, :], compare_op=ALU.is_gt, fill=0.0,
                                        base=LAST, pattern=[[0, P]], channel_multiplier=-1).then_inc(pool.sem, 1)

                    @block.vector
                    def _(v):
                        v.memset(x_sb[:, NT - 1, :], 0.0).then_inc(vec.sem, 1)
                        v.wait_ge(loaded.sem, loaded.base + 5 * 16)
                        v.tensor_copy(dstf[:, 0, :], dst_i[:, :])
                        v.tensor_copy(chunk_dst[:, :], dst_i[:, 0:1])
                        step(v, v.tensor_copy(dstf[:, 1, :], prev_i[:, :]), vec, 2)
                        step(v, v.tensor_tensor(neg[:, :], dstf[:, 0, :], dstf[:, 1, :], ALU.is_equal), vec, 3)
                        step(v, v.tensor_scalar(neg[:, :], neg[:, :], -1.0, -NEG, ALU.add, ALU.mult), vec, 4)
                        step(v, v.tensor_reduce(anystart[:, :], neg[:, :], X, ALU.min), vec, 5)
                        v.wait_ge(pool.sem, pool.base + 3)
                        v.memset(neg[:, 0:1], NEG)
                        v.tensor_scalar(anyrow[:, :], ones[:, :], anystart[:, 0:1], None, ALU.mult).then_inc(vec.sem, 1)
                        v.wait_ge(mm.sem, mm.base + 1)
                        step(v, v.tensor_copy(negrow[:, :], bank[0][:, 0:P]), vec, 7)
                        v.tensor_scalar(controw[:, :], negrow[:, :], 0.0, None, ALU.is_equal)

                    @block.tensor
                    def _(pe):
                        pe.wait_ge(vec.sem, vec.base + 6)
                        pe.wait_ge(pool.sem, pool.base + 2)
                        nc.tensor.matmul(bank[0][:, 0:P], anyrow[:, :], ident[:, :], start=True, stop=True).then_inc(mm.sem, 1)
                loaded.base += 5 * 16
                vec.base += 7
                pool.base += 4
                mm.base += 1

        def count_edges():
            with ExitStack() as st:
                HI, LO = NT, P
                hi_i = sb(st, "hi_i", [P, CHUNK], I32)
                lo_i = sb(st, "lo_i", [P, CHUNK], I32)
                select = sb(st, "select", [P, NP])
                hi_f = sb(st, "hi_f", [P, CHUNK])
                lo_f = sb(st, "lo_f", [P, CHUNK])
                hi_t = sb(st, "hi_t", [P, T])
                lo_t = sb(st, "lo_t", [P, T])
                iota_i = sb(st, "iota_i", [P, P], I32)
                iota_f = sb(st, "iota_f", [P, P])
                chan_i = sb(st, "chan_i", [P, 1], I32)
                chan_f = sb(st, "chan_f", [P, 1])
                hot_hi = sb(st, "hot_hi", [P, 2, T, HI], BF16)
                hot_lo = sb(st, "hot_lo", [P, 2, T, LO], BF16)
                zero = sb(st, "zero", [P, P], BF16)
                upper = sb(st, "upper", [P, P])
                cnt = sb(st, "cnt", [HI, LO])
                cum = sb(st, "cum", [HI, LO])
                before = sb(st, "before", [HI, 1])
                node_id = sb(st, "node_id", [HI, LO])
                node_i = sb(st, "node_i", [HI, LO], I32)
                q = sb(st, "q", [HI, 8, LO])
                hot = [signal("hot_ready0"), signal("hot_ready1")]
                used = [signal("hot_used0"), signal("hot_used1")]
                counts = bank[0][0:HI, 0:LO]
                with nc.Block() as block:
                    @block.sync
                    def _(sp):
                        sp.wait_ge(vec.sem, vec.base + 3 + 2 * PAIRS + 18 + len(GROUPS))
                        sp.dma_start(selection[:, :], select[:, :]).then_inc(stored.sem, 16)
                        sp.wait_ge(stored.sem, stored.base + 16)

                    @block.gpsimd
                    def _(g):
                        g.iota(iota_i[:, :], pattern=[[1, P]], base=0, channel_multiplier=0)
                        g.iota(chan_i[:, :], pattern=[[0, 1]], base=0, channel_multiplier=1)
                        g.iota(node_i[:, :], pattern=[[1, LO]], base=EP, channel_multiplier=LO)
                        g.affine_select(out=upper[:, :], in_=ones[:, :], compare_op=ALU.is_gt, fill=0.0,
                                        base=0, pattern=[[1, P]], channel_multiplier=-1).then_inc(pool.sem, 1)

                    @block.vector
                    def _(v):
                        v.memset(zero[:, :], 0.0).then_inc(vec.sem, 1)
                        v.wait_ge(pool.sem, pool.base + 1)
                        v.tensor_copy(iota_f[:, :], iota_i[:, :])
                        v.tensor_copy(chan_f[:, :], chan_i[:, :])
                        v.tensor_copy(node_id[:, :], node_i[:, :])
                        v.tensor_scalar(hi_i[:, :], dst_i[:, :], 7, None, ALU.logical_shift_right)
                        step(v, v.tensor_scalar(lo_i[:, :], dst_i[:, :], P - 1, None, ALU.bitwise_and), vec, 2)
                        v.tensor_copy(hi_f[:, :], hi_i[:, :])
                        step(v, v.tensor_copy(lo_f[:, :], lo_i[:, :]), vec, 3)
                        for b in range(2):
                            v.memset((hi_t, lo_t)[b][:, :], 0.0).then_inc(hot[b].sem, 1)
                        vec.base += 3
                        with v.Fori(0, PAIRS) as i:
                            for b in range(2):
                                v.wait_ge(hot[1 - b].sem, i + b + 1)
                                v.tensor_copy(hi_t[:, :], hi_f[:, bass.ds((i * 2 + b) * T, T)])
                                v.tensor_copy(lo_t[:, :], lo_f[:, bass.ds((i * 2 + b) * T, T)]).then_inc(vec.sem, 1)
                                v.wait_ge(vec.sem, vec.base + 2 * i + b + 1)
                                v.wait_ge(used[b].sem, i + 1)
                                v.tensor_tensor(hot_hi[:, b, :, :], over(hi_t[:, :], HI), along(iota_f[:, 0:HI], T), ALU.is_equal)
                                v.tensor_tensor(hot_lo[:, b, :, :], over(lo_t[:, :], LO), along(iota_f[:, :], T), ALU.is_equal).then_inc(hot[b].sem, 1)
                        vec.base += 2 * PAIRS
                        v.wait_ge(mm.sem, mm.base + 1)
                        step(v, v.tensor_copy(cnt[:, :], counts), vec, 1)
                        step(v, v.tensor_tensor_scan(cum[:, :], ones[0:HI, :], cnt[:, :], 0.0, ALU.mult, ALU.add), vec, 2)
                        v.wait_ge(mm.sem, mm.base + 2)
                        step(v, v.tensor_copy(before[:, :], bank[1][0:HI, 0:1]), vec, 3)
                        step(v, v.tensor_scalar(cum[:, :], cum[:, :], before[:, 0:1], None, ALU.add), vec, 4)
                        v.tensor_scalar(q[:, 0, :], cum[:, :], -1.0, 0.0, ALU.add, ALU.max)
                        v.tensor_scalar(q[:, 2, :], cnt[:, :], 0.0, None, ALU.is_gt)
                        step(v, v.tensor_tensor(q[:, 1, :], cum[:, :], cnt[:, :], ALU.subtract), vec, 5)
                        step(v, v.tensor_scalar(q[:, 3, :], q[:, 0, :], 0.5, 1.0 / CHUNK, ALU.add, ALU.mult), vec, 6)
                        step(v, v.tensor_scalar(q[:, 3, :], q[:, 3, :], -0.5, 12582912.0, ALU.add, ALU.add), vec, 7)
                        step(v, v.tensor_scalar(q[:, 3, :], q[:, 3, :], -12582912.0, None, ALU.add), vec, 8)
                        step(v, v.scalar_tensor_tensor(q[:, 4, :], q[:, 3, :], float(CHUNK), q[:, 1, :], ALU.mult, ALU.is_gt), vec, 9)
                        step(v, v.tensor_tensor(q[:, 4, :], q[:, 4, :], q[:, 2, :], ALU.mult), vec, 10)
                        step(v, v.tensor_tensor(q[:, 5, :], q[:, 4, :], q[:, 3, :], ALU.mult), vec, 11)
                        step(v, v.tensor_scalar(q[:, 5, :], q[:, 5, :], -1.0, None, ALU.add), vec, 12)
                        step(v, v.tensor_tensor(q[:, 6, :], q[:, 1, :], node_id[:, :], ALU.subtract), vec, 13)
                        step(v, v.tensor_tensor(q[:, 6, :], q[:, 6, :], q[:, 2, :], ALU.mult), vec, 14)
                        step(v, v.tensor_tensor(q[:, 6, :], q[:, 6, :], node_id[:, :], ALU.add), vec, 15)
                        step(v, v.tensor_scalar(q[:, 7, :], q[:, 3, :], 1.0, float(T2), ALU.add, ALU.mult), vec, 16)
                        step(v, v.tensor_tensor(q[:, 7, :], q[:, 7, :], q[:, 0, :], ALU.add), vec, 17)
                        v.wait_ge(mm.sem, mm.base + 3)
                        v.tensor_copy(last144_i[:, :], bank[1][:, 4 * HI:5 * HI])
                        v.tensor_copy(last_i[:, :], bank[1][:, 0:HI])
                        v.tensor_copy(first_i[:, :], bank[1][:, HI:2 * HI])
                        v.tensor_copy(has[:, :], bank[1][:, 2 * HI:3 * HI])
                        v.tensor_scalar(nocarry[:, :], bank[1][:, 3 * HI:4 * HI], 0.0, NEG, ALU.is_lt, ALU.mult).then_inc(vec.sem, 1)
                        for n, (g0, m) in enumerate(GROUPS):
                            v.wait_ge(mm2.sem, mm2.base + n + 1)
                            v.tensor_scalar(select[:, g0 * P:(g0 + m) * P], bank[2 + n % 2][:, 0:m * P], chan_f[:, 0:1], None,
                                            ALU.is_equal).then_inc(vec.sem, 1)

                    @block.tensor
                    def _(pe):
                        pe.wait_ge(vec.sem, vec.base - 2 * PAIRS - 3 + 1)
                        for b in range(2):
                            nc.tensor.matmul(counts, zero[:, 0:HI], zero[:, 0:LO], start=b == 0, stop=False).then_inc(used[b].sem, 1)
                        with pe.Fori(0, PAIRS) as i:
                            for b in range(2):
                                pe.wait_ge(hot[b].sem, i + 2)
                                for t in range(T):
                                    last = nc.tensor.matmul(counts, hot_hi[:, b, t, :], hot_lo[:, b, t, :], start=False, stop=False)
                                last.then_inc(used[b].sem, 1)
                        nc.tensor.matmul(counts, zero[:, 0:HI], zero[:, 0:LO], start=False, stop=True).then_inc(mm.sem, 1)
                        pe.wait_ge(vec.sem, vec.base + 2)
                        pe.wait_ge(pool.sem, pool.base + 1)
                        nc.tensor.matmul(bank[1][0:HI, 0:1], upper[0:HI, 0:HI], cum[:, LO - 1:LO], start=True, stop=True).then_inc(mm.sem, 1)
                        pe.wait_ge(vec.sem, vec.base + 17)
                        for k, which in enumerate((0, 6, 2, 5, 7)):
                            last = nc.tensor.transpose(bank[1][:, k * HI:(k + 1) * HI], q[:, which, :], ident[0:HI, 0:HI])
                        last.then_inc(mm.sem, 1)
                        for n, (g0, m) in enumerate(GROUPS):
                            if n >= 2:
                                pe.wait_ge(vec.sem, vec.base + 18 + n - 1)
                            for j in range(m):
                                last = nc.tensor.matmul(bank[2 + n % 2][:, j * P:(j + 1) * P],
                                                        ident[0:HI, g0 + j:g0 + j + 1].to_broadcast([HI, P]),
                                                        q[:, 5, :], start=True, stop=True)
                            last.then_inc(mm2.sem, 1)
                stored.base += 16
                pool.base += 1
                vec.base += 18 + len(GROUPS)
                mm.base += 3
                mm2.base += len(GROUPS)

        def clear_by_first():
            with ExitStack() as st:
                z = sb(st, "z", [P, CHUNK + NT])
                with nc.Block() as block:
                    @block.vector
                    def _(v):
                        v.memset(z[:, :], 0.0).then_inc(vec.sem, 1)

                    @block.sync
                    def _(sp):
                        sp.wait_ge(vec.sem, vec.base + 1)
                        sp.dma_start(by_first.rearrange("(p f) o -> p (f o)", p=P), z[:, :]).then_inc(stored.sem, 16)
                        sp.wait_ge(stored.sem, stored.base + 16)
                vec.base += 1
                stored.base += 16

        def load_weights(parts):
            with nc.Block() as block:
                @block.sync
                def _(sp):
                    for tile, source in parts:
                        sp.dma_start(tile, source).then_inc(loaded.sem, 16)
                    sp.wait_ge(loaded.sem, loaded.base + 16 * len(parts))
            loaded.base += 16 * len(parts)

        def spread(vector_ap):
            return vector_ap.unsqueeze(0).to_broadcast([P, vector_ap.shape[0]])

        def store_nodes(pairs):
            with nc.Block() as block:
                @block.sync
                def _(sp):
                    for t, tile in pairs:
                        sp.dma_start(nodes(t), tile).then_inc(stored.sem, 16)
                    sp.wait_ge(stored.sem, stored.base + 16 * len(pairs))
            stored.base += 16 * len(pairs)

        def layer_norm_relu(dst, src, tmp, stat, gamma=None, beta=None):
            affine = gamma is not None
            with nc.Block() as block:
                @block.vector
                def _(v):
                    step(v, v.tensor_reduce(stat[:, 0, :], src, X, ALU.add), vec, 1)
                    step(v, v.tensor_scalar(stat[:, 0, :], stat[:, 0, :], 1.0 / D, None, ALU.mult), vec, 2)
                    step(v, v.tensor_tensor(tmp, src, over(stat[:, 0, :], D), ALU.subtract), vec, 3)
                    step(v, v.tensor_tensor(dst, tmp, tmp, ALU.mult), vec, 4)
                    step(v, v.tensor_reduce(stat[:, 1, :], dst, X, ALU.add), vec, 5)
                    v.tensor_scalar(stat[:, 1, :], stat[:, 1, :], 1.0 / D, 1e-5, ALU.mult, ALU.add).then_inc(vec.sem, 1)
                    v.wait_ge(act.sem, act.base + 1)
                    step(v, v.reciprocal(stat[:, 1, :], stat[:, 0, :]), vec, 7)
                    step(v, v.tensor_tensor(tmp, tmp, over(stat[:, 1, :], D), ALU.mult), vec, 8)
                    if affine:
                        step(v, v.tensor_tensor(tmp, tmp, along(gamma[:, :], NT), ALU.mult), vec, 9)
                        step(v, v.tensor_tensor(tmp, tmp, along(beta[:, :], NT), ALU.add), vec, 10)
                    v.tensor_scalar(dst, tmp, 0.0, None, ALU.max)

                @block.scalar
                def _(s):
                    s.wait_ge(vec.sem, vec.base + 6)
                    s.activation(stat[:, 0, :], stat[:, 1, :], ACT.Sqrt).then_inc(act.sem, 1)
            vec.base += 10 if affine else 8
            act.base += 1

        def linear(dst, src, weight, K, M, bias=None, add_to=None):
            with ExitStack() as st:
                turned = sb(st, "turned", [P, 2, 512])
                t_ready = [bank[0], bank[1]]
                products = [bank[2], bank[3]]
                with nc.Block() as block:
                    @block.tensor
                    def _(pe):
                        for n in range(len(GROUPS) + 1):
                            if n < len(GROUPS):
                                g0, m = GROUPS[n]
                                if n >= 2:
                                    pe.wait_ge(act.sem, act.base + n - 1)
                                for j in range(m):
                                    last = nc.tensor.transpose(t_ready[n % 2][0:K, j * P:(j + 1) * P], src[:, g0 + j, :], ident[:, :])
                                last.then_inc(mm.sem, 1)
                            if n >= 1:
                                k = n - 1
                                g0, m = GROUPS[k]
                                pe.wait_ge(act.sem, act.base + k + 1)
                                if k >= 2:
                                    pe.wait_ge(vec.sem, vec.base + k - 1)
                                for j in range(m):
                                    last = nc.tensor.matmul(products[k % 2][:, j * M:(j + 1) * M], turned[0:K, k % 2, j * P:(j + 1) * P],
                                                            weight, start=True, stop=True)
                                last.then_inc(mm2.sem, 1)

                    @block.scalar
                    def _(s):
                        for n, (g0, m) in enumerate(GROUPS):
                            s.wait_ge(mm.sem, mm.base + n + 1)
                            if n >= 2:
                                s.wait_ge(mm2.sem, mm2.base + n - 1)
                            s.activation(turned[0:K, n % 2, 0:m * P], t_ready[n % 2][0:K, 0:m * P], ACT.Copy).then_inc(act.sem, 1)

                    @block.vector
                    def _(v):
                        for n, (g0, m) in enumerate(GROUPS):
                            v.wait_ge(mm2.sem, mm2.base + n + 1)
                            got = products[n % 2][:, 0:m * M].rearrange("p (j f) -> p j f", f=M)
                            if bias is not None:
                                v.tensor_tensor(dst[:, g0:g0 + m, :], got, along(bias, m), ALU.add).then_inc(vec.sem, 1)
                            elif add_to is not None:
                                v.tensor_tensor(dst[:, g0:g0 + m, :], got, add_to[:, g0:g0 + m, :], ALU.add).then_inc(vec.sem, 1)
                            else:
                                v.tensor_copy(dst[:, g0:g0 + m, :], got).then_inc(vec.sem, 1)
                n = len(GROUPS)
                mm.base += n
                mm2.base += n
                act.base += n
                vec.base += n

        def collect(width, tail_max, tail_sums, pieces, chain, carried, collected, record, at_last):
            k = len(tail_sums)
            online = tail_max is not None
            length = sum(p[3] for p in pieces)
            with ExitStack() as st:
                run = sb(st, "run", [width, k + 1, P])
                decay = sb(st, "decay", [width, P])
                weight = sb(st, "weight", [width, P])
                term = sb(st, "term", [width, k, P])
                select = sb(st, "select", [P, NP])
                with nc.Block() as block:
                    @block.sync
                    def _(sp):
                        sp.dma_start(select[:, :], selection[:, :]).then_inc(loaded.sem, 16)

                    @block.gpsimd
                    def _(g):
                        for j in range(NT):
                            nc.gpsimd.indirect_dma_start(collected[:, j, :], None, record,
                                                         bass.IndirectOffsetOnAxis(ap=at_last[:, j:j + 1], axis=0)).then_inc(rows.sem, 16)
                        g.wait_ge(rows.sem, rows.base + 16 * NT)

                    @block.tensor
                    def _(pe):
                        if online:
                            nc.tensor.transpose(bank[0][0:width, 0:P], tail_max, ident[:, :])
                        for n in range(k):
                            last = nc.tensor.transpose(bank[0][0:width, (n + 1) * P:(n + 2) * P], tail_sums[n], ident[:, :])
                        last.then_inc(mm.sem, 1)
                        pe.wait_ge(vec.sem, vec.base + (5 if online else 2))
                        for n in range(0 if online else 1, k + 1):
                            at = (n if online else n - 1) * width
                            last = nc.tensor.transpose(bank[1][:, at:at + width], run[:, n, :], ident[0:width, 0:width])
                        last.then_inc(mm.sem, 1)
                        pe.wait_ge(vec.sem, vec.base + (6 if online else 3))
                        pe.wait_ge(loaded.sem, loaded.base + 16)
                        for j in range(NT):
                            if j >= 4:
                                pe.wait_ge(act.sem, act.base + (1 if online else 0) + j - 3)
                            nc.tensor.matmul(bank[2 + j % 4][:, 0:length], select[:, j * P:(j + 1) * P], chain[:, 0:length],
                                             start=True, stop=True).then_inc(mm2.sem, 1)

                    @block.vector
                    def _(v):
                        v.wait_ge(mm.sem, mm.base + 1)
                        if online:
                            v.memset(decay[:, 0:1], NEG)
                            step(v, v.tensor_tensor_scan(run[:, 0, :], negrow[0:width, :], bank[0][0:width, 0:P], NEG, ALU.add, ALU.max), vec, 1)
                            v.tensor_tensor(decay[:, 1:P], run[:, 0, 0:P - 1], run[:, 0, 1:P], ALU.subtract)
                            step(v, v.tensor_tensor(weight[:, :], bank[0][0:width, 0:P], run[:, 0, :], ALU.subtract), vec, 2)
                            v.tensor_tensor(decay[:, :], decay[:, :], negrow[0:width, :], ALU.add).then_inc(vec.sem, 1)
                            v.wait_ge(act.sem, act.base + 1)
                            step(v, v.tensor_tensor(term[:, :, :], bank[0][0:width, P:(k + 1) * P].rearrange("p (n c) -> p n c", c=P),
                                                    along(weight[:, :], k), ALU.mult), vec, 4)
                            for n in range(k):
                                last = v.tensor_tensor_scan(run[:, n + 1, :], decay[:, :], term[:, n, :], 0.0, ALU.mult, ALU.add)
                            last.then_inc(vec.sem, 1)
                        else:
                            step(v, v.tensor_copy(term[:, 0, :], bank[0][0:width, P:2 * P]), vec, 1)
                            v.tensor_tensor_scan(run[:, 1, :], controw[0:width, :], term[:, 0, :], 0.0, ALU.mult, ALU.add).then_inc(vec.sem, 1)
                        v.wait_ge(mm.sem, mm.base + 2)
                        for to, first, every, count in pieces:
                            last = v.tensor_copy(chain[:, to:to + count], bank[1][:, first:first + (count - 1) * every + 1:every])
                        last.then_inc(vec.sem, 1)

                    @block.scalar
                    def _(s):
                        if online:
                            s.wait_ge(vec.sem, vec.base + 3)
                            s.activation(decay[:, :], decay[:, :], ACT.Exp)
                            s.activation(weight[:, :], weight[:, :], ACT.Exp).then_inc(act.sem, 1)
                        for j in range(NT):
                            s.wait_ge(mm2.sem, mm2.base + j + 1)
                            s.activation(carried[:, j, :], bank[2 + j % 4][:, 0:length], ACT.Copy).then_inc(act.sem, 1)
                mm.base += 2
                mm2.base += NT
                vec.base += 6 if online else 3
                act.base += NT + (1 if online else 0)
                loaded.base += 16
                rows.base += 16 * NT

        def start_count(sp, kept):
            for b in range(2):
                sp.dma_start(spare[b], holder[:, 0:1]).then_inc(kept[b].sem, 16)

        def hold(g):
            g.tensor_tensor(holder[:, 1:2], holder[:, 0:1], holder[:, 0:1], ALU.add)

        def gathers(g, index, where, filled, source):
            for t in range(where.shape[1]):
                nc.gpsimd.indirect_dma_start(where[:, t, :], None, source,
                                             bass.IndirectOffsetOnAxis(ap=index[:, t:t + 1], axis=0)).then_inc(filled, 16)

        def edges_logsumexp(tag, rec):
            with ExitStack() as st:
                got = [sb(st, f"got{b}", [P, T, D]) for b in range(2)]
                fall = sb(st, "fall", [P, T, D])
                index = sb(st, "index", [P, 2, T], I32)
                neg_t = sb(st, "neg_t", [P, T])
                filled = [signal(f"{tag}_rows_here{b}") for b in range(2)]
                done = [signal(f"{tag}_record_ready{b}") for b in range(2)]
                kept = [signal(f"{tag}_record_stored{b}") for b in range(2)]
                with nc.Block() as block:
                    @block.gpsimd
                    def _(g):
                        with g.Fori(0, PAIRS) as i:
                            for b in range(2):
                                g.wait_ge(done[b].sem, i + 1)
                                g.tensor_copy(index[:, b, :], src_i[:, bass.ds((i * 2 + b) * T, T)]).then_inc(pool.sem, 1)
                                g.wait_ge(pool.sem, pool.base + 2 * i + b + 1)
                                hold(g)
                                gathers(g, index[:, b, :], got[b], filled[b].sem, table)

                    @block.vector
                    def _(v):
                        v.memset(rec[1][:, T - 1, 0:D], 0.0).then_inc(done[0].sem, 1)
                        v.memset(rec[1][:, T - 1, D:2 * D], 0.0).then_inc(done[1].sem, 1)
                        with v.Fori(0, PAIRS) as i:
                            for b in range(2):
                                now, past = rec[b], rec[1 - b]
                                at = vec.base + 8 * i + 4 * b
                                v.wait_ge(done[1 - b].sem, i + b + 1)
                                v.tensor_copy(neg_t[:, :], neg[:, bass.ds((i * 2 + b) * T, T)]).then_inc(vec.sem, 1)
                                v.wait_ge(vec.sem, at + 1)
                                v.wait_ge(filled[b].sem, 16 * T * (i + 1))
                                v.wait_ge(kept[b].sem, 16 * i + 16)
                                for f in range(D):
                                    last = v.tensor_tensor_scan(now[:, :, f], neg_t[:, :], got[b][:, :, f], past[:, T - 1, f:f + 1], ALU.add, ALU.max)
                                last.then_inc(vec.sem, 1)
                                v.wait_ge(vec.sem, at + 2)
                                v.tensor_tensor(fall[:, 0, :], past[:, T - 1, 0:D], now[:, 0, 0:D], ALU.subtract)
                                v.tensor_tensor(fall[:, 1:T, :], now[:, 0:T - 1, 0:D], now[:, 1:T, 0:D], ALU.subtract)
                                v.tensor_tensor(got[b][:, :, :], got[b][:, :, :], now[:, :, 0:D], ALU.subtract).then_inc(vec.sem, 1)
                                v.wait_ge(vec.sem, at + 3)
                                v.tensor_tensor(fall[:, :, :], fall[:, :, :], over(neg_t[:, :], D), ALU.add).then_inc(vec.sem, 1)
                                v.wait_ge(act.sem, act.base + 2 * i + b + 1)
                                for f in range(D):
                                    last = v.tensor_tensor_scan(now[:, :, D + f], fall[:, :, f], got[b][:, :, f], past[:, T - 1, D + f:D + f + 1], ALU.mult, ALU.add)
                                last.then_inc(done[b].sem, 1)

                    @block.scalar
                    def _(s):
                        with s.Fori(0, PAIRS) as i:
                            for b in range(2):
                                s.wait_ge(vec.sem, vec.base + 8 * i + 4 * b + 4)
                                s.activation(fall[:, :, :], fall[:, :, :], ACT.Exp)
                                s.activation(got[b][:, :, :], got[b][:, :, :], ACT.Exp).then_inc(act.sem, 1)

                    @block.sync
                    def _(sp):
                        start_count(sp, kept)
                        with sp.Fori(0, PAIRS) as i:
                            for b in range(2):
                                sp.wait_ge(done[b].sem, i + 2)
                                sp.dma_start(edges(record128)[:, bass.ds((i * 2 + b) * T, T), :], rec[b][:, :, :]).then_inc(kept[b].sem, 16)
                        for b in range(2):
                            sp.wait_ge(kept[b].sem, 16 * PAIRS + 16)
                pool.base += 2 * PAIRS
                vec.base += 8 * PAIRS
                act.base += 2 * PAIRS

        def logsumexp_layers():
            with ExitStack() as st:
                w_in = sb(st, "w_in", [D, D])
                w_l = sb(st, "w_l", [2 * D, 3, D])
                vecs = sb(st, "vecs", [P, 10, D])
                load_weights([(w_in[:, :], a["L0_gnn_W_inT"]), (w_l[:, :, :], a["L0_gnn_W_lT"].rearrange("l k m -> k l m")),
                              (vecs[:, 0, :], spread(a["L0_gnn_b_in"]))]
                             + [(vecs[:, 1 + 3 * l + n, :], spread(a[name][l]))
                                for l in range(3) for n, name in enumerate(("L0_gnn_b_l", "L0_gnn_gamma_l", "L0_gnn_beta_l"))])
                with ExitStack() as s2:
                    tmp = sb(s2, "tmp", [P, NT, D])
                    stat = sb(s2, "stat", [P, 2, NT])
                    layer_norm_relu(agg, x_sb[:, :, :], tmp[:, :, :], stat)
                    linear(h_sb, agg, w_in[:, :], D, D, bias=vecs[:, 0, :])
                for l in range(3):
                    store_nodes([(table, h_sb)])
                    with ExitStack() as s2:
                        rec = [sb(s2, f"rec{b}", [P, T, 2 * D]) for b in range(2)]
                        edges_logsumexp(f"lse{l}", rec)
                        with ExitStack() as s3:
                            tail = rec[1][:, T - 1, :]
                            collected = sb(s3, "collected", [P, NT, 2 * D])
                            carried = sb(s3, "carried", [P, NT, 2 * D])
                            chain = sb(s3, "chain", [P, 2 * D])
                            collect(D, tail[:, 0:D], [tail[:, D:2 * D]], [(0, 0, 1, 2 * D)], chain, carried, collected, record128, last_i)
                            join_logsumexp(collected, carried)
                    with ExitStack() as s2:
                        new = sb(s2, "new", [P, NT, D])
                        tmp = sb(s2, "tmp2", [P, NT, D])
                        stat = sb(s2, "stat2", [P, 2, NT])
                        linear(new[:, :, :], hc, w_l[:, l, :], 2 * D, D, bias=vecs[:, 1 + 3 * l, :])
                        layer_norm_relu(agg, new[:, :, :], tmp[:, :, :], stat, vecs[:, 2 + 3 * l, :], vecs[:, 3 + 3 * l, :])
                        with nc.Block() as block:
                            @block.vector
                            def _(v):
                                step(v, v.tensor_tensor(tmp[:, :, :], h_sb, agg, ALU.add), vec, 1)
                                step(v, v.tensor_scalar(h_sb, tmp[:, :, :], 0.5, None, ALU.mult), vec, 2)
                                if l == 2:
                                    v.tensor_tensor(x_sb[:, :, :], x_sb[:, :, :], h_sb, ALU.add)
                        vec.base += 2

        def join_logsumexp(collected, carried):
            m1, s1 = collected[:, :, 0:D], collected[:, :, D:2 * D]
            m2, s2 = carried[:, :, 0:D], carried[:, :, D:2 * D]
            with nc.Block() as block:
                @block.vector
                def _(v):
                    step(v, v.tensor_tensor(m2, m2, over(nocarry[:, :], D), ALU.add), vec, 1)
                    step(v, v.tensor_tensor(agg, m1, m2, ALU.max), vec, 2)
                    v.tensor_tensor(m1, m1, agg, ALU.subtract)
                    v.tensor_tensor(m2, m2, agg, ALU.subtract).then_inc(vec.sem, 1)
                    v.wait_ge(act.sem, act.base + 1)
                    v.tensor_tensor(s1, s1, m1, ALU.mult)
                    step(v, v.tensor_tensor(s2, s2, m2, ALU.mult), vec, 4)
                    step(v, v.tensor_tensor(s1, s1, s2, ALU.add), vec, 5)
                    v.tensor_scalar(s1, s1, 1e-30, None, ALU.max).then_inc(vec.sem, 1)
                    v.wait_ge(act.sem, act.base + 2)
                    step(v, v.tensor_tensor(agg, agg, s1, ALU.add), vec, 7)
                    v.tensor_tensor(agg, agg, over(has[:, :], D), ALU.mult)

                @block.scalar
                def _(s):
                    s.wait_ge(vec.sem, vec.base + 3)
                    s.activation(m1, m1, ACT.Exp)
                    s.activation(m2, m2, ACT.Exp).then_inc(act.sem, 1)
                    s.wait_ge(vec.sem, vec.base + 6)
                    s.activation(s1, s1, ACT.Ln).then_inc(act.sem, 1)
            vec.base += 7
            act.base += 2

        def batch_norm(dst, src, tmp, gamma, beta, relu):
            with ExitStack() as st:
                mean = sb(st, "mean", [P, D])
                scale = sb(st, "scale", [P, 2, D])
                with nc.Block() as block:
                    @block.tensor
                    def _(pe):
                        for k, what in enumerate((src, dst)):
                            if k == 1:
                                pe.wait_ge(vec.sem, vec.base + 3)
                            for j in range(NT):
                                last = nc.tensor.matmul(bank[k][:, 0:D], (ones_last if j == NT - 1 else ones)[:, :], what[:, j, :],
                                                        start=j == 0, stop=j == NT - 1)
                            last.then_inc(mm.sem, 1)

                    @block.vector
                    def _(v):
                        v.wait_ge(mm.sem, mm.base + 1)
                        step(v, v.tensor_scalar(mean[:, :], bank[0][:, 0:D], 1.0 / N, None, ALU.mult), vec, 1)
                        step(v, v.tensor_tensor(tmp, src, along(mean[:, :], NT), ALU.subtract), vec, 2)
                        v.tensor_tensor(dst, tmp, tmp, ALU.mult).then_inc(vec.sem, 1)
                        v.wait_ge(mm.sem, mm.base + 2)
                        v.tensor_scalar(scale[:, 0, :], bank[1][:, 0:D], 1.0 / N, 1e-5, ALU.mult, ALU.add).then_inc(vec.sem, 1)
                        v.wait_ge(act.sem, act.base + 1)
                        step(v, v.reciprocal(scale[:, 0, :], scale[:, 1, :]), vec, 5)
                        step(v, v.tensor_tensor(scale[:, 0, :], scale[:, 0, :], gamma, ALU.mult), vec, 6)
                        step(v, v.tensor_tensor(tmp, tmp, along(scale[:, 0, :], NT), ALU.mult), vec, 7)
                        step(v, v.tensor_tensor(dst, tmp, along(beta, NT), ALU.add), vec, 8)
                        if relu:
                            v.tensor_scalar(dst, dst, 0.0, None, ALU.max)

                    @block.scalar
                    def _(s):
                        s.wait_ge(vec.sem, vec.base + 4)
                        s.activation(scale[:, 1, :], scale[:, 0, :], ACT.Sqrt).then_inc(act.sem, 1)
                mm.base += 2
                vec.base += 8
                act.base += 1

        def edges_weighted_sum(rec, weight):
            with ExitStack() as st:
                got = [sb(st, f"got{b}", [P, T, D]) for b in range(2)]
                index = sb(st, "index", [P, 2, T], I32)
                cont_t = sb(st, "cont_t", [P, T])
                filled = [signal(f"sum_rows_here{b}") for b in range(2)]
                done = [signal(f"sum_record_ready{b}") for b in range(2)]
                kept = [signal(f"sum_record_stored{b}") for b in range(2)]
                with nc.Block() as block:
                    @block.gpsimd
                    def _(g):
                        with g.Fori(0, PAIRS) as i:
                            for b in range(2):
                                g.wait_ge(done[b].sem, i + 1)
                                g.tensor_copy(index[:, b, :], src_i[:, bass.ds((i * 2 + b) * T, T)]).then_inc(pool.sem, 1)
                                g.wait_ge(pool.sem, pool.base + 2 * i + b + 1)
                                hold(g)
                                gathers(g, index[:, b, :], got[b], filled[b].sem, table)

                    @block.vector
                    def _(v):
                        v.memset(rec[1][:, T - 1, 0:D // 2], 0.0).then_inc(done[0].sem, 1)
                        v.memset(rec[1][:, T - 1, D // 2:D], 0.0).then_inc(done[1].sem, 1)
                        with v.Fori(0, PAIRS) as i:
                            for b in range(2):
                                v.wait_ge(done[1 - b].sem, i + b + 1)
                                v.tensor_scalar(cont_t[:, :], neg[:, bass.ds((i * 2 + b) * T, T)], 0.0, None, ALU.is_equal)
                                v.wait_ge(filled[b].sem, 16 * T * (i + 1))
                                v.tensor_tensor(got[b][:, :, :], got[b][:, :, :], over(weight[:, bass.ds((i * 2 + b) * T, T)], D), ALU.mult).then_inc(vec.sem, 1)
                                v.wait_ge(vec.sem, vec.base + 2 * i + b + 1)
                                v.wait_ge(kept[b].sem, 16 * i + 16)
                                for f in range(D):
                                    last = v.tensor_tensor_scan(rec[b][:, :, f], cont_t[:, :], got[b][:, :, f], rec[1 - b][:, T - 1, f:f + 1], ALU.mult, ALU.add)
                                last.then_inc(done[b].sem, 1)

                    @block.sync
                    def _(sp):
                        start_count(sp, kept)
                        with sp.Fori(0, PAIRS) as i:
                            for b in range(2):
                                sp.wait_ge(done[b].sem, i + 2)
                                sp.dma_start(edges(record64)[:, bass.ds((i * 2 + b) * T, T), :], rec[b][:, :, :]).then_inc(kept[b].sem, 16)
                        for b in range(2):
                            sp.wait_ge(kept[b].sem, 16 * PAIRS + 16)
                pool.base += 2 * PAIRS
                vec.base += 2 * PAIRS

        def weighted_sum_layer():
            with ExitStack() as st:
                w = sb(st, "w", [D, 2, D])
                vecs = sb(st, "vecs", [P, 6, D])
                weight = sb(st, "weight_e", [P, CHUNK])
                load_weights([(w[:, 0, :], a["L1_gnn_W1"]), (w[:, 1, :], a["L1_gnn_W2"]),
                              (weight[:, :], a["edge_weight"].rearrange("(c t) -> c t", c=P))]
                             + [(vecs[:, n, :], spread(a[f"L1_gnn_{name}"]))
                                for n, name in enumerate(("b1", "gamma1", "beta1", "b2", "gamma2", "beta2"))])
                with ExitStack() as s2:
                    tmp = sb(s2, "tmp", [P, NT, D])
                    stat = sb(s2, "stat", [P, 2, NT])
                    layer_norm_relu(h_sb, x_sb[:, :, :], tmp[:, :, :], stat)
                store_nodes([(table, h_sb)])
                with ExitStack() as s2:
                    rec = [sb(s2, f"rec{b}", [P, T, D]) for b in range(2)]
                    edges_weighted_sum(rec, weight)
                    collected = sb(s2, "collected", [P, NT, D])
                    carried = sb(s2, "carried", [P, NT, D])
                    chain = sb(s2, "chain", [P, D])
                    collect(D, None, [rec[1][:, T - 1, :]], [(0, 0, 1, D)], chain, carried, collected, record64, last_i)
                    with nc.Block() as block:
                        @block.vector
                        def _(v):
                            step(v, v.tensor_tensor(collected[:, :, :], collected[:, :, :], over(has[:, :], D), ALU.mult), vec, 1)
                            step(v, v.tensor_tensor(collected[:, :, :], collected[:, :, :], carried[:, :, :], ALU.add), vec, 2)
                            v.tensor_tensor(agg, collected[:, :, :], h_sb, ALU.add)
                    vec.base += 2
                with ExitStack() as s2:
                    mid = sb(s2, "mid", [P, NT, D])
                    tmp = sb(s2, "tmp", [P, NT, D])
                    for k in range(2):
                        linear(mid[:, :, :], agg, w[:, k, :], D, D, bias=vecs[:, 3 * k, :])
                        batch_norm(agg, mid[:, :, :], tmp[:, :, :], vecs[:, 3 * k + 1, :], vecs[:, 3 * k + 2, :], True)
                    with nc.Block() as block:
                        @block.vector
                        def _(v):
                            v.tensor_tensor(x_sb[:, :, :], x_sb[:, :, :], agg, ALU.add)

        def edges_attention(rec):
            C = 2 * T2
            W = O + 2 * H
            K5 = 5
            with ExitStack() as st:
                c_w = sb(st, "c_w", [P, K5, 2 * O])
                w1 = sb(st, "w1", [P, P])
                w2 = sb(st, "w2", [P, 2 * O])
                b1 = sb(st, "b1", [P, 1])
                b2 = sb(st, "b2", [P, 2 * O])
                xg = [sb(st, f"xg{b}", [P, T2, D]) for b in range(2)]
                qg = [sb(st, f"qg{b}", [P, T2, O]) for b in range(2)]
                ea = [sb(st, f"ea{b}", [P, T2, D]) for b in range(2)]
                sh = [sb(st, f"sh{b}", [P, T2, S]) for b in range(2)]
                vv = [sb(st, f"vv{b}", [P, T2, O]) for b in range(2)]
                logit = [sb(st, f"logit{b}", [P, T2, H]) for b in range(2)]
                neg_t = [sb(st, f"neg_t{b}", [P, T2]) for b in range(2)]
                fall = sb(st, "fall", [P, T2, H])
                z = [sb(st, f"z{k}", [P, K5 * P]) for k in range(3)]
                zt = [sb(st, f"zt{k}", [P, K5, P]) for k in range(2)]
                hid = [sb(st, f"hid{k}", [P, P]) for k in range(2)]
                wb = [sb(st, f"wb{k}", [P, 2 * O]) for k in range(2)]
                kk = [sb(st, f"kk{k}", [P, O]) for k in range(2)]
                index = sb(st, "index", [P, 2, 2, T2], I32)
                filled = [signal(f"att_rows_here{b}") for b in range(2)]
                inputs = [signal(f"att_edges_here{b}") for b in range(2)]
                kept = [signal(f"att_record_stored{b}") for b in range(2)]
                tails = [signal(f"att_record_ready{b}") for b in range(2)]
                left = [signal(f"att_rows_used{b}") for b in range(2)]
                primed = sb(st, "primed", [P, 32])
                z_ready, ea_ready, turned, evacuated = signal("z_ready"), signal("ea_ready"), signal("z_turned"), signal("zt_ready")
                hid_done, hid_ready, products, joined = signal("hid_done"), signal("hid_ready"), signal("products_done"), signal("kv_joined")
                tail_v, tail_a = signal("tail_vec"), signal("tail_exp")
                chain_v = signal("column_vec")

                def done(i, c):
                    return i * C + (c + 4)

                load_weights([(c_w[:, 0:4, 0:O], a["L2_gnn_Cqk_s"][0:512, :].rearrange("(k p) o -> p k o", p=P)),
                              (c_w[:, 0:4, O:2 * O], a["L2_gnn_Cv_s"][0:512, :].rearrange("(k p) o -> p k o", p=P)),
                              (c_w[0:D, 4, 0:O], a["L2_gnn_Cqk_s"][512:576, :]), (c_w[0:D, 4, O:2 * O], a["L2_gnn_Cv_s"][512:576, :]),
                              (w1[D:P, 0:D], a["L2_gnn_k_w1"]), (w1[D:P, D:P], a["L2_gnn_v_w1"]),
                              (b1[0:D, :], a["L2_gnn_k_b1"].unsqueeze(1)), (b1[D:P, :], a["L2_gnn_v_b1"].unsqueeze(1)),
                              (b2[:, 0:O], spread(a["L2_gnn_k_b2"])), (b2[:, O:2 * O], spread(a["L2_gnn_v_b2"])),
                              (w2[0:D, 0:O], a["L2_gnn_k_w2"]), (w2[D:P, O:2 * O], a["L2_gnn_v_w2"])])

                with nc.Block() as block:
                    @block.gpsimd
                    def _(g):
                        with g.Fori(0, PAIRS2) as i:
                            for b in range(2):
                                g.wait_ge(left[b].sem, i + 1)
                                g.tensor_copy(index[:, b, 0, :], src_i[:, bass.ds((i * 2 + b) * T2, T2)])
                                g.tensor_copy(index[:, b, 1, :], dst_i[:, bass.ds((i * 2 + b) * T2, T2)]).then_inc(pool.sem, 1)
                                g.wait_ge(pool.sem, pool.base + 2 * i + b + 1)
                                hold(g)
                                gathers(g, index[:, b, 0, :], xg[b], filled[b].sem, table)
                                gathers(g, index[:, b, 1, :], qg[b], filled[b].sem, table_q)

                    @block.sync
                    def _(sp):
                        def load(g, b, used):
                            sp.wait_ge(left[b].sem, used)
                            sp.dma_start(ea[b][:, :, :], edges(a["edge64"])[:, bass.ds(g * T2, T2), :]).then_inc(inputs[b].sem, 16)
                            sp.dma_start(sh[b][:, :, :], edges(a["edge9"])[:, bass.ds(g * T2, T2), :]).then_inc(inputs[b].sem, 16)

                        def store(g, b, ready):
                            sp.wait_ge(tails[b].sem, ready)
                            sp.dma_start(edges(record144)[:, bass.ds(g * T2, T2), :], rec[b][:, :, :]).then_inc(kept[b].sem, 16)

                        start_count(sp, kept)
                        load(0, 0, 1)
                        with sp.Fori(0, PAIRS2 - 1) as i:
                            load(i * 2 + 1, 1, i + 1)
                            store(i * 2, 1, i + 2)
                            load(i * 2 + 2, 0, i + 2)
                            store(i * 2 + 1, 0, i + 2)
                        load(2 * PAIRS2 - 1, 1, PAIRS2)
                        store(2 * PAIRS2 - 2, 1, PAIRS2 + 1)
                        store(2 * PAIRS2 - 1, 0, PAIRS2 + 1)
                        store(2 * PAIRS2, 1, PAIRS2 + 2)
                        sp.wait_ge(kept[0].sem, 16 * (PAIRS2 + 1))
                        sp.wait_ge(kept[1].sem, 16 * (PAIRS2 + 2))

                    @block.tensor
                    def _(pe):
                        for k in range(3):
                            for bk, sem in ((0, turned), (4, hid_done), (5, products)):
                                nc.tensor.matmul(bank[bk][:, 0:P], ident[:, :], ident[:, :], start=True, stop=True).then_inc(sem.sem, 1)

                        def turn(i, c):
                            pe.wait_ge(z_ready.sem, done(i, c))
                            pe.wait_ge(ea_ready.sem, done(i, c))
                            pe.wait_ge(evacuated.sem, done(i, c - 2))
                            for k in range(K5):
                                last = nc.tensor.transpose(bank[2 * (c % 2) + k // 4][:, (k % 4) * P:(k % 4 + 1) * P], z[c % 3][:, k * P:(k + 1) * P], ident[:, :])
                            last.then_inc(turned.sem, 1)

                        with pe.Fori(0, PAIRS2) as i:
                            for c in range(C):
                                if c == 0:
                                    turn(i, 0)
                                if c + 1 < C:
                                    turn(i, c + 1)
                                q = c % 2
                                pe.wait_ge(evacuated.sem, done(i, c))
                                pe.wait_ge(hid_ready.sem, done(i, c - 1))
                                nc.tensor.matmul(bank[4][:, 0:P], w1[D:P, :], zt[q][D:P, 4, :], start=True, stop=True).then_inc(hid_done.sem, 1)
                                pe.wait_ge(joined.sem, done(i, c - 2))
                                for k in range(K5):
                                    rows_k = D if k == 4 else P
                                    nc.tensor.matmul(bank[6 + q][:, 0:2 * O], zt[q][0:rows_k, k, :], c_w[0:rows_k, k, :], start=k == 0, stop=k == K5 - 1)
                                pe.wait_ge(hid_ready.sem, done(i, c))
                                pe.wait_ge(chain_v.sem, i * (3 * C) + (3 * c + 1))
                                nc.tensor.matmul(bank[5][:, 0:2 * O], hid[q][:, :], w2[:, :], start=True, stop=True).then_inc(products.sem, 1)

                    @block.scalar
                    def _(s):
                        for k in range(3):
                            for n, sem in enumerate((evacuated, hid_ready, ea_ready)):
                                s.activation(primed[:, 3 * k + n:3 * k + n + 1], holder[:, 0:1], ACT.Copy).then_inc(sem.sem, 1)

                        def place(i, c):
                            b, t = c // T2, c % T2
                            if t == 0:
                                s.wait_ge(inputs[b].sem, 32 * (i + 1))
                            s.wait_ge(turned.sem, done(i, c - 3))
                            s.activation(z[c % 3][:, S * D:], ea[b][:, t, :], ACT.Copy).then_inc(ea_ready.sem, 1)

                        with s.Fori(0, PAIRS2) as i:
                            for c in range(C):
                                b, t, q = c // T2, c % T2, c % 2
                                if c == 0:
                                    place(i, 0)
                                if c + 1 < C:
                                    place(i, c + 1)
                                s.wait_ge(turned.sem, done(i, c))
                                s.wait_ge(products.sem, done(i, c - 2))
                                s.activation(zt[q][:, 4, :], bank[2 * q + 1][:, 0:P], ACT.Copy)
                                s.activation(zt[q][:, 0:4, :], bank[2 * q][:, :].rearrange("p (k e) -> p k e", e=P), ACT.Copy).then_inc(evacuated.sem, 1)
                                s.wait_ge(hid_done.sem, done(i, c))
                                s.activation(hid[q][:, :], bank[4][:, 0:P], ACT.Relu, bias=b1[:, 0:1]).then_inc(hid_ready.sem, 1)
                                if t == 2:
                                    s.wait_ge(tail_v.sem, i * 8 + (4 * b + 3))
                                    s.activation(fall[:, :, :], fall[:, :, :], ACT.Exp)
                                    s.activation(logit[1 - b][:, :, :], logit[1 - b][:, :, :], ACT.Exp).then_inc(tail_a.sem, 1)
                        s.wait_ge(tail_v.sem, 4 * 2 * PAIRS2 + 3)
                        s.activation(fall[:, :, :], fall[:, :, :], ACT.Exp)
                        s.activation(logit[1][:, :, :], logit[1][:, :, :], ACT.Exp).then_inc(tail_a.sem, 1)

                    @block.vector
                    def _(v):
                        v.memset(vv[1][:, :, :], 0.0)
                        v.memset(logit[1][:, :, :], 0.0)
                        v.memset(neg_t[1][:, :], 0.0)
                        v.memset(rec[0][:, T2 - 1, :], 0.0).then_inc(tails[0].sem, 1)
                        v.memset(rec[1][:, T2 - 1, :], 0.0).then_inc(tails[1].sem, 1)
                        v.memset(w2[0:D, O:2 * O], 0.0)
                        v.memset(w2[D:P, 0:O], 0.0)
                        for k in range(3):
                            v.memset(primed[:, 16 + k:17 + k], 0.0).then_inc(z_ready.sem, 1)
                            v.memset(primed[:, 20 + k:21 + k], 0.0).then_inc(joined.sem, 1)
                            v.memset(primed[:, 28 + k:29 + k], 0.0).then_inc(chain_v.sem, 1)
                        for b in range(2):
                            v.memset(primed[:, 24 + b:25 + b], 0.0).then_inc(left[b].sem, 1)

                        def outer(i, c):
                            b, t = c // T2, c % T2
                            if t == 0:
                                v.wait_ge(filled[b].sem, 2 * 16 * T2 * (i + 1))
                                v.wait_ge(inputs[b].sem, 32 * (i + 1))
                            v.wait_ge(turned.sem, done(i, c - 3))
                            v.tensor_tensor(z[c % 3][:, 0:S * D].rearrange("p (s d) -> p s d", d=D), along(xg[b][:, t, :], S),
                                            over(sh[b][:, t, :], D), ALU.mult).then_inc(z_ready.sem, 1)

                        def tail(n, pb, t, before, free, columns):
                            now, past = rec[pb], rec[1 - pb]
                            p, m_now, m_past = logit[pb], now[:, :, O:O + H], past[:, T2 - 1, O:O + H]
                            if t == 0:
                                v.wait_ge(joined.sem, columns)
                                v.wait_ge(tails[1 - pb].sem, before)
                                v.wait_ge(kept[pb].sem, free)
                                for h in range(H):
                                    last = v.tensor_tensor_scan(now[:, :, O + h], neg_t[pb][:, :], p[:, :, h], past[:, T2 - 1, O + h:O + h + 1], ALU.add, ALU.max)
                                last.then_inc(tail_v.sem, 1)
                            elif t == 1:
                                v.wait_ge(tail_v.sem, n * 4 + 1)
                                v.tensor_tensor(fall[:, 0, :], m_past, now[:, 0, O:O + H], ALU.subtract)
                                v.tensor_tensor(fall[:, 1:T2, :], now[:, 0:T2 - 1, O:O + H], now[:, 1:T2, O:O + H], ALU.subtract)
                                v.tensor_tensor(p[:, :, :], p[:, :, :], m_now, ALU.subtract).then_inc(tail_v.sem, 1)
                                v.wait_ge(tail_v.sem, n * 4 + 2)
                                v.tensor_tensor(fall[:, :, :], fall[:, :, :], over(neg_t[pb][:, :], H), ALU.add).then_inc(tail_v.sem, 1)
                            elif t == 4:
                                v.wait_ge(tail_a.sem, n + 1)
                                for h in range(H):
                                    v.tensor_tensor_scan(now[:, :, O + H + h], fall[:, :, h], p[:, :, h], past[:, T2 - 1, O + H + h:O + H + h + 1], ALU.mult, ALU.add)
                            elif 5 <= t < 9:
                                t0 = (t - 5) * (T2 // 4)
                                part = vv[pb][:, t0:t0 + T2 // 4, :].rearrange("p t (h d) -> p t h d", d=DH)
                                pr = p[:, t0:t0 + T2 // 4, :]
                                last = v.tensor_tensor(part, part, pr.unsqueeze(3).to_broadcast([P, T2 // 4, H, DH]), ALU.mult)
                                if t == 8:
                                    last.then_inc(tail_v.sem, 1)
                            elif t >= 10:
                                if t == 10:
                                    v.wait_ge(tail_v.sem, n * 4 + 4)
                                slots = T2 - 10
                                for o in range((t - 10) * O // slots, (t - 9) * O // slots):
                                    last = v.tensor_tensor_scan(now[:, :, o], fall[:, :, o // DH], vv[pb][:, :, o], past[:, T2 - 1, o:o + 1], ALU.mult, ALU.add)
                                if t == T2 - 1:
                                    last.then_inc(tails[pb].sem, 1)

                        with v.Fori(0, PAIRS2) as i:
                            for c in range(C):
                                b, t, q = c // T2, c % T2, c % 2
                                if c == 0:
                                    outer(i, 0)
                                if c + 1 < C:
                                    outer(i, c + 1)
                                tail(i * 2 + b, 1 - b, t, i + (b + 1), i * 16 + 16, i * C + (b * T2 + 3))
                                if t == 0:
                                    v.tensor_copy(neg_t[b][:, :], neg[:, bass.ds((i * 2 + b) * T2, T2)])
                                v.wait_ge(products.sem, done(i, c))
                                v.tensor_tensor(wb[q][:, :], bank[5][:, 0:2 * O], b2[:, :], ALU.add).then_inc(chain_v.sem, 1)
                                v.wait_ge(chain_v.sem, i * (3 * C) + (3 * c + 4))
                                v.tensor_tensor(kk[q][:, :], bank[6 + q][:, 0:O], wb[q][:, 0:O], ALU.mult).then_inc(chain_v.sem, 1)
                                v.wait_ge(chain_v.sem, i * (3 * C) + (3 * c + 5))
                                v.tensor_tensor(kk[q][:, :], kk[q][:, :], qg[b][:, t, :], ALU.mult).then_inc(chain_v.sem, 1)
                                last = v.tensor_tensor(vv[b][:, t, :], bank[6 + q][:, O:2 * O], wb[q][:, O:2 * O], ALU.mult)
                                if t == T2 - 1:
                                    last.then_inc(left[b].sem, 1)
                                v.wait_ge(chain_v.sem, i * (3 * C) + (3 * c + 6))
                                v.tensor_reduce(logit[b][:, t, :], kk[q][:, :].rearrange("p (h d) -> p h d", d=DH), X, ALU.add).then_inc(joined.sem, 1)
                        for t in range(T2):
                            tail(2 * PAIRS2, 1, t, PAIRS2 + 1, 16 * (PAIRS2 + 1), PAIRS2 * C + 3)
                pool.base += 2 * PAIRS2

        def join_softmax(u1, m1, s1, u2, m2, s2, heads, width, own=None):
            parts = [(u1, m1, s1), (u2, m2, s2)] + ([own] if own is not None else [])
            with ExitStack() as st:
                top = sb(st, "top", [P, NT, heads])
                with nc.Block() as block:
                    @block.vector
                    def _(v):
                        step(v, v.tensor_tensor(m2, m2, over(nocarry[:, :], heads), ALU.add), vec, 1)
                        step(v, v.tensor_scalar(top[:, :, :], over(has[:, :], heads), 0.0, NEG, ALU.is_equal, ALU.mult), vec, 2)
                        step(v, v.tensor_tensor(m1, m1, over(has[:, :], heads), ALU.mult), vec, 3)
                        step(v, v.tensor_tensor(m1, m1, top[:, :, :], ALU.add), vec, 4)
                        step(v, v.tensor_tensor(top[:, :, :], m1, m2, ALU.max), vec, 5)
                        if own is None:
                            step(v, v.tensor_copy(top[:, :, :], top[:, :, :]), vec, 6)
                        else:
                            step(v, v.tensor_tensor(top[:, :, :], top[:, :, :], own[1], ALU.max), vec, 6)
                        for _, m, _ in parts:
                            last = v.tensor_tensor(m, m, top[:, :, :], ALU.subtract)
                        last.then_inc(vec.sem, 1)
                        v.wait_ge(act.sem, act.base + 1)
                        for u, m, s in parts:
                            v.tensor_tensor(s, s, m, ALU.mult)
                            uh = u.rearrange("p j (h d) -> p j h d", d=width)
                            last = v.tensor_tensor(uh, uh, m.unsqueeze(3).to_broadcast([P, NT, heads, width]), ALU.mult)
                        step(v, last, vec, 8)
                        for n, (u, _, s) in enumerate(parts[1:]):
                            v.tensor_tensor(s1, s1, s, ALU.add)
                            step(v, v.tensor_tensor(u1, u1, u, ALU.add), vec, 9 + n)

                    @block.scalar
                    def _(s):
                        s.wait_ge(vec.sem, vec.base + 7)
                        for _, m, _ in parts:
                            last = s.activation(m, m, ACT.Exp)
                        last.then_inc(act.sem, 1)
                vec.base += 7 + len(parts)
                act.base += 1

        def divide_softmax(u, s, m, heads, width):
            with nc.Block() as block:
                @block.vector
                def _(v):
                    step(v, v.tensor_scalar(s, s, 1e-16, None, ALU.add), vec, 1)
                    step(v, v.reciprocal(m, s), vec, 2)
                    uh = u.rearrange("p j (h d) -> p j h d", d=width)
                    v.tensor_tensor(uh, uh, m.unsqueeze(3).to_broadcast([P, NT, heads, width]), ALU.mult)
            vec.base += 2

        def attention_layer():
            W = O + 2 * H
            with ExitStack() as s2:
                tmp = sb(s2, "tmp", [P, NT, D])
                stat = sb(s2, "stat", [P, 2, NT])
                wq = sb(s2, "wq", [D, O])
                q = sb(s2, "q_nodes", [P, NT, O])
                load_weights([(wq[:, :], a["L2_gnn_Wq"])])
                layer_norm_relu(h_sb, x_sb[:, :, :], tmp[:, :, :], stat)
                linear(q[:, :, :], h_sb, wq[:, :], D, O)
                store_nodes([(table, h_sb), (table_q, q[:, :, :])])
            with ExitStack() as s1:
                last_rec = sb(s1, "last_rec", [P, W])
                with ExitStack() as s2:
                    rec = [sb(s2, f"rec{b}", [P, T2, W]) for b in range(2)]
                    edges_attention(rec)
                    with nc.Block() as block:
                        @block.vector
                        def _(v):
                            v.tensor_copy(last_rec[:, :], rec[1][:, T2 - 1, :])
                upd = sb(s1, "collected", [P, NT, W])
                with ExitStack() as s2:
                    tail_m = sb(s2, "tail_m", [P, O])
                    tail_s = sb(s2, "tail_s", [P, O])
                    chain = sb(s2, "chain", [P, W])
                    carried = sb(s2, "carried", [P, NT, W])
                    with nc.Block() as block:
                        @block.vector
                        def _(v):
                            v.tensor_copy(tail_m[:, :].rearrange("p (h d) -> p h d", d=DH), over(last_rec[:, O:O + H], DH))
                            v.tensor_copy(tail_s[:, :].rearrange("p (h d) -> p h d", d=DH), over(last_rec[:, O + H:W], DH))
                    collect(O, tail_m[:, :], [last_rec[:, 0:O], tail_s[:, :]],
                            [(0, O, 1, O), (O, 0, DH, H), (O + H, 2 * O, DH, H)], chain, carried, upd, record144, last144_i)
                    join_softmax(upd[:, :, 0:O], upd[:, :, O:O + H], upd[:, :, O + H:W],
                                 carried[:, :, 0:O], carried[:, :, O:O + H], carried[:, :, O + H:W], H, DH)
                divide_softmax(upd[:, :, 0:O], upd[:, :, O + H:W], upd[:, :, O:O + H], H, DH)
                w_out = sb(s1, "w_out", [O, D])
                w_self = sb(s1, "w_self", [D, D])
                vecs = sb(s1, "vecs", [P, 2, D])
                total = sb(s1, "total", [P, NT, D])
                tmp = sb(s1, "tmp", [P, NT, D])
                load_weights([(w_out[:, :], a["L2_gnn_W_out"]), (w_self[:, :], a["L2_gnn_W_self"]),
                              (vecs[:, 0, :], spread(a["L2_gnn_gamma"])), (vecs[:, 1, :], spread(a["L2_gnn_beta"]))])
                linear(tmp[:, :, :], upd[:, :, 0:O], w_out[:, :], O, D)
                linear(total[:, :, :], h_sb, w_self[:, :], D, D, add_to=tmp[:, :, :])
                batch_norm(agg, total[:, :, :], tmp[:, :, :], vecs[:, 0, :], vecs[:, 1, :], False)
                with nc.Block() as block:
                    @block.vector
                    def _(v):
                        v.tensor_tensor(x_sb[:, :, :], x_sb[:, :, :], agg, ALU.add)

        def spread_by_dst(ade, alpha_d):
            with ExitStack() as st:
                cont = sb(st, "cont", [P, CHUNK])
                firsts = sb(st, "firsts", [P, CHUNK])
                chunk_row = sb(st, "chunk_row", [P, D + 2])
                with nc.Block() as block:
                    @block.gpsimd
                    def _(g):
                        for j in range(NT):
                            nc.gpsimd.indirect_dma_start(by_first, bass.IndirectOffsetOnAxis(ap=first_i[:, j:j + 1], axis=0),
                                                         alpha_d[:, j:j + 1], None).then_inc(rows.sem, 16)
                        nc.gpsimd.indirect_dma_start(chunk_row[:, :], None, table_a,
                                                     bass.IndirectOffsetOnAxis(ap=chunk_dst[:, 0:1], axis=0)).then_inc(chunk_rows.sem, 16)
                        g.wait_ge(chunk_rows.sem, chunk_rows.base + 16)

                    @block.sync
                    def _(sp):
                        sp.wait_ge(rows.sem, rows.base + 16 * NT)
                        sp.dma_start(firsts[:, :], by_first[0:EP, :].rearrange("(c t) o -> c (t o)", c=P)).then_inc(loaded.sem, 16)

                    @block.vector
                    def _(v):
                        v.tensor_scalar(cont[:, :], neg[:, :], 0.0, None, ALU.is_equal).then_inc(vec.sem, 1)
                        v.wait_ge(chunk_rows.sem, chunk_rows.base + 16)
                        v.wait_ge(loaded.sem, loaded.base + 16)
                        v.tensor_copy(firsts[:, 0:1], chunk_row[:, D + 1:D + 2]).then_inc(vec.sem, 1)
                        v.wait_ge(vec.sem, vec.base + 2)
                        v.tensor_tensor_scan(ade[:, :], cont[:, :], firsts[:, :], 0.0, ALU.mult, ALU.add)
                vec.base += 2
                rows.base += 16 * NT
                loaded.base += 16
                chunk_rows.base += 16

        def edges_graph(tag, rec, ade):
            with ExitStack() as st:
                got = [sb(st, f"got{b}", [P, T, D + 2]) for b in range(2)]
                index = sb(st, "index", [P, 2, T], I32)
                neg_t = sb(st, "neg_t", [P, T])
                p = sb(st, "p", [P, T])
                raw = sb(st, "raw", [P, T])
                fall = sb(st, "fall", [P, T])
                M, Z = D, D + 1
                filled = [signal(f"{tag}_rows_here{b}") for b in range(2)]
                done = [signal(f"{tag}_record_ready{b}") for b in range(2)]
                kept = [signal(f"{tag}_record_stored{b}") for b in range(2)]
                with nc.Block() as block:
                    @block.gpsimd
                    def _(g):
                        with g.Fori(0, PAIRS) as i:
                            for b in range(2):
                                g.wait_ge(done[b].sem, i + 1)
                                g.tensor_copy(index[:, b, :], src_i[:, bass.ds((i * 2 + b) * T, T)]).then_inc(pool.sem, 1)
                                g.wait_ge(pool.sem, pool.base + 2 * i + b + 1)
                                hold(g)
                                gathers(g, index[:, b, :], got[b], filled[b].sem, table_a)

                    @block.vector
                    def _(v):
                        v.memset(rec[1][:, T - 1, 0:D], 0.0).then_inc(done[0].sem, 1)
                        v.memset(rec[1][:, T - 1, D:D + 2], 0.0).then_inc(done[1].sem, 1)
                        with v.Fori(0, PAIRS) as i:
                            for b in range(2):
                                now, past = rec[b], rec[1 - b]

                                def link(k, ins):
                                    ins.then_inc(vec.sem, 1)
                                    v.wait_ge(vec.sem, i * 14 + (vec.base + 7 * b + k))

                                v.wait_ge(done[1 - b].sem, i + b + 1)
                                v.tensor_copy(neg_t[:, :], neg[:, bass.ds((i * 2 + b) * T, T)])
                                v.wait_ge(filled[b].sem, 16 * T * (i + 1))
                                link(1, v.tensor_tensor(raw[:, :], got[b][:, :, D], ade[:, bass.ds((i * 2 + b) * T, T)], ALU.add))
                                link(2, v.scalar_tensor_tensor(p[:, :], raw[:, :], 0.2, raw[:, :], ALU.mult, ALU.max))
                                v.wait_ge(kept[b].sem, 16 * i + 16)
                                link(3, v.tensor_tensor_scan(now[:, :, M], neg_t[:, :], p[:, :], past[:, T - 1, M:M + 1], ALU.add, ALU.max))
                                v.tensor_tensor(fall[:, 0:1], past[:, T - 1, M:M + 1], now[:, 0, M:M + 1], ALU.subtract)
                                v.tensor_tensor(fall[:, 1:T], now[:, 0:T - 1, M], now[:, 1:T, M], ALU.subtract)
                                link(4, v.tensor_tensor(p[:, :], p[:, :], now[:, :, M], ALU.subtract))
                                link(5, v.tensor_tensor(fall[:, :], fall[:, :], neg_t[:, :], ALU.add))
                                v.wait_ge(act.sem, act.base + 2 * i + b + 1)
                                link(6, v.tensor_tensor(got[b][:, :, 0:D], got[b][:, :, 0:D], over(p[:, :], D), ALU.mult))
                                link(7, v.tensor_tensor_scan(now[:, :, Z], fall[:, :], p[:, :], past[:, T - 1, Z:Z + 1], ALU.mult, ALU.add))
                                for f in range(D):
                                    last = v.tensor_tensor_scan(now[:, :, f], fall[:, :], got[b][:, :, f], past[:, T - 1, f:f + 1], ALU.mult, ALU.add)
                                last.then_inc(done[b].sem, 1)

                    @block.scalar
                    def _(s):
                        with s.Fori(0, PAIRS) as i:
                            for b in range(2):
                                s.wait_ge(vec.sem, i * 14 + (vec.base + 7 * b + 5))
                                s.activation(fall[:, :], fall[:, :], ACT.Exp)
                                s.activation(p[:, :], p[:, :], ACT.Exp).then_inc(act.sem, 1)

                    @block.sync
                    def _(sp):
                        start_count(sp, kept)
                        with sp.Fori(0, PAIRS) as i:
                            for b in range(2):
                                sp.wait_ge(done[b].sem, i + 2)
                                sp.dma_start(edges(record66)[:, bass.ds((i * 2 + b) * T, T), :], rec[b][:, :, :]).then_inc(kept[b].sem, 16)
                        for b in range(2):
                            sp.wait_ge(kept[b].sem, 16 * PAIRS + 16)
                pool.base += 2 * PAIRS
                vec.base += 14 * PAIRS
                act.base += 2 * PAIRS

        def graph_attention_layers():
            W = D + 2
            with ExitStack() as st:
                w = sb(st, "w", [D, 3, D])
                vecs = sb(st, "vecs", [P, 9, D])
                alphas = sb(st, "alphas", [P, 3, NT])
                own = sb(st, "own", [P, NT, W])
                load_weights([(w[:, l, :], a[f"L3_gnn_W{l + 1}"]) for l in range(3)]
                             + [(vecs[:, 3 * l + n, :], spread(a[f"L3_gnn_{name}"]))
                                for l in range(3) for n, name in enumerate((f"a{l + 1}s", f"a{l + 1}d", f"b{l + 1}"))])
                with ExitStack() as s2:
                    tmp = sb(s2, "tmp", [P, NT, D])
                    stat = sb(s2, "stat", [P, 2, NT])
                    layer_norm_relu(h_sb, x_sb[:, :, :], tmp[:, :, :], stat)
                for l in range(3):
                    hw = own[:, :, 0:D]
                    linear(hw, h_sb, w[:, l, :], D, D)
                    with nc.Block() as block:
                        @block.vector
                        def _(v):
                            for n in range(2):
                                step(v, v.tensor_tensor(agg, hw, along(vecs[:, 3 * l + n, :], NT), ALU.mult), vec, 2 * n + 1)
                                step(v, v.tensor_reduce(alphas[:, n, :], agg, X, ALU.add), vec, 2 * n + 2)
                            step(v, v.tensor_tensor(alphas[:, 2, :], alphas[:, 0, :], alphas[:, 1, :], ALU.add), vec, 5)
                            v.tensor_copy(own[:, :, D], alphas[:, 0, :])
                            v.tensor_copy(own[:, :, D + 1], alphas[:, 1, :])
                    vec.base += 5
                    store_nodes([(table_a, own[:, :, :])])
                    with nc.Block() as block:
                        @block.vector
                        def _(v):
                            v.scalar_tensor_tensor(own[:, :, D], alphas[:, 2, :], 0.2, alphas[:, 2, :], ALU.mult, ALU.max)
                            v.memset(own[:, :, D + 1], 1.0)
                    with ExitStack() as s2:
                        ade = sb(s2, "ade", [P, CHUNK])
                        spread_by_dst(ade, alphas[:, 1, :])
                        rec = [sb(s2, f"rec{b}", [P, T, W]) for b in range(2)]
                        edges_graph(f"gat{l}", rec, ade)
                        collected = sb(s2, "collected", [P, NT, W])
                        carried = sb(s2, "carried", [P, NT, W])
                        chain = sb(s2, "chain", [P, W])
                        tail_m = sb(s2, "tail_m", [P, D])
                        tail_s = sb(s2, "tail_s", [P, D])
                        with nc.Block() as block:
                            @block.vector
                            def _(v):
                                v.tensor_copy(tail_m[:, :], rec[1][:, T - 1, D:D + 1].to_broadcast([P, D]))
                                v.tensor_copy(tail_s[:, :], rec[1][:, T - 1, D + 1:D + 2].to_broadcast([P, D]))
                        collect(D, tail_m[:, :], [rec[1][:, T - 1, 0:D], tail_s[:, :]],
                                [(0, D, 1, D), (D, 0, 1, 1), (D + 1, 2 * D, 1, 1)], chain, carried, collected, record66, last_i)

                        def fields(t):
                            return t[:, :, 0:D], t[:, :, D:D + 1], t[:, :, D + 1:D + 2]

                        u, m, s = fields(collected)
                        join_softmax(u, m, s, *fields(carried), 1, D, own=fields(own))
                        divide_softmax(u, s, m, 1, D)
                        with nc.Block() as block:
                            @block.vector
                            def _(v):
                                if l < 2:
                                    step(v, v.tensor_tensor(u, u, along(vecs[:, 3 * l + 2, :], NT), ALU.add), vec, 1)
                                    v.tensor_scalar(h_sb, u, 0.0, None, ALU.max)
                                else:
                                    step(v, v.tensor_tensor(u, u, along(vecs[:, 3 * l + 2, :], NT), ALU.add), vec, 1)
                                    v.tensor_tensor(x_sb[:, :, :], x_sb[:, :, :], u, ALU.add)
                        vec.base += 1

        load_and_flags()
        count_edges()
        if 0 in LAYERS:
            logsumexp_layers()
        if 1 in LAYERS:
            weighted_sum_layer()
        if 2 in LAYERS:
            attention_layer()
        if 3 in LAYERS:
            clear_by_first()
            graph_attention_layers()

        with nc.Block() as block:
            @block.sync
            def _(sp):
                sp.dma_start(out[0:P * (NT - 1), :].rearrange("(j p) f -> p j f", p=P), x_sb[:, 0:NT - 1, :]).then_inc(stored.sem, 16)
                sp.dma_start(out[P * (NT - 1):N, :], x_sb[0:LAST, NT - 1, :]).then_inc(stored.sem, 16)
                sp.wait_ge(stored.sem, stored.base + 32)


def kernel(**inputs):
    import numpy as np
    import concourse.bacc as bacc
    from concourse.bass_utils import run_bass_kernel_spmd as run

    def padded(v, length, value, front=0):
        r = np.full((length,) + v.shape[1:], value, v.dtype)
        r[front:front + v.shape[0]] = v
        return r

    lay = {k: np.ascontiguousarray(v) for k, v in inputs.items()}
    arrays = {
        "x": lay["x"],
        "src_pad": padded(lay["src"], EP, 0),
        "dst_ext": padded(lay["dst"], EP + 1, N, front=1),
        "edge64": padded(lay["edge_attr_64"], EP, 0),
        "edge9": padded(lay["edge_attr_9"], EP, 0),
        "edge_weight": padded(lay["edge_weight"], EP, 0),
        "L0_gnn_W_inT": np.ascontiguousarray(lay["L0_gnn_W_in"].T),
        "L0_gnn_W_lT": np.ascontiguousarray(lay["L0_gnn_W_l"].transpose(0, 2, 1)),
    }
    for name in ("Cqk", "Cv"):
        arrays[f"L2_gnn_{name}_s"] = np.ascontiguousarray(lay[f"L2_gnn_{name}"].transpose(1, 0, 2).reshape(S * D, O))
    arrays["dst_ext"][0] = -1
    for name, v in lay.items():
        if name[:3] in ("L0_", "L1_", "L2_", "L3_") and name not in ("L0_gnn_W_in", "L0_gnn_W_l", "L2_gnn_Cqk", "L2_gnn_Cv"):
            arrays[name] = v
    nc = bacc.Bacc("TRN2", target_bir_lowering=False, num_devices=1)
    aps = {name: nc.dram_tensor(f"in_{name}", v.shape, mybir.dt.from_np(v.dtype), kind="ExternalInput").ap()
           for name, v in arrays.items()}
    out = nc.dram_tensor("out_0", (N, D), F32, kind="ExternalOutput").ap()
    build_program(nc, aps, out)
    r = run(nc, [{f"in_{name}": v for name, v in arrays.items()}], core_ids=[0])
    return r.results[0]["out_0"]
```

```python
import concourse.bass as bass
from concourse import mybir
from contextlib import ExitStack

F32 = mybir.dt.float32
I32 = mybir.dt.int32
BF16 = mybir.dt.bfloat16
ALU = mybir.AluOpType
ACT = mybir.ActivationFunctionType
X = mybir.AxisListType.X

LAYERS = (0, 1, 2, 3)
P = 128
N, E, D = 6250, 200000, 64
NT = -(-N // P)
NP = NT * P
LAST = N - (NT - 1) * P
T = 49
PAIRS = -(-E // (P * 2 * T))
CHUNK = PAIRS * 2 * T
EP = P * CHUNK
T2 = T * 4 // 7
PAIRS2 = CHUNK // (2 * T2)
NET_COLUMNS = [(0, 16), (16, 33), (33, T)]
G = T2 // 2
S, O, H, DH = 9, 128, 8, 16
NEG = -1.0e37
GROUPS = [(g, min(4, NT - g)) for g in range(0, NT, 4)]


class Signal:

    def __init__(self, ctx, nc, name):
        self.sem = ctx.enter_context(nc.semaphore(name))
        self.base = 0


def build_program(nc, a, out):
    ctx = ExitStack()
    with ctx:
        used_names = {}

        def sb(stack, name, shape, dt=F32):
            used_names[name] = used_names.get(name, 0) + 1
            return stack.enter_context(nc.sbuf_tensor(f"{name}_{used_names[name]}", shape, dt))

        def dram(name, shape, dt=F32):
            return nc.dram_tensor(name, shape, dt, kind="Internal").ap()

        def signal(name):
            return Signal(ctx, nc, name)

        vec = signal("vec_done")
        act = signal("act_done")
        mm = signal("pe_done")
        mm2 = signal("pe_products_done")
        pool = signal("pool_done")
        loaded = signal("loaded")
        stored = signal("stored")
        rows = signal("rows_gathered")
        chunk_rows = signal("chunk_rows_gathered")

        wide = [ctx.enter_context(nc.psum_tensor(f"banks{k}", [P, 1024], F32)) for k in range(4)]
        net_here = signal("net_edges_here")
        net_hid = signal("net_hidden_done")
        net_relu = signal("net_hidden_ready")
        net_done = signal("net_product_done")
        net_out_ready = signal("net_out_ready")
        net_kept = signal("net_out_stored")
        hot = signal("one_hots_ready")
        digit = signal("digits_ready")
        counted = signal("one_hots_counted")

        bank = [wide[k // 2][:, 512 * (k % 2):512 * (k % 2 + 1)] for k in range(8)]

        x_sb = sb(ctx, "x_sb", [P, NT, D])
        hc = sb(ctx, "hc", [P, NT, 2 * D])
        h_sb = hc[:, :, 0:D]
        agg = hc[:, :, D:2 * D]
        ident = sb(ctx, "ident", [P, P])
        ones = sb(ctx, "ones", [P, P])
        ones_last = sb(ctx, "ones_last", [P, P])
        src_i = sb(ctx, "src_i", [P, CHUNK], I32)
        dst_i = sb(ctx, "dst_i", [P, CHUNK], I32)
        neg = sb(ctx, "neg", [P, CHUNK])
        negrow = sb(ctx, "negrow", [P, P])
        controw = sb(ctx, "controw", [P, P])
        has = sb(ctx, "has", [P, NT])
        nocarry = sb(ctx, "nocarry", [P, NT])
        last_i = sb(ctx, "last_i", [P, NT], I32)
        last144_i = sb(ctx, "last144_i", [P, NT], I32)
        first_i = sb(ctx, "first_i", [P, NT], I32)
        holder = sb(ctx, "holder", [P, 2])
        net_ones = sb(ctx, "net_ones", [1, P], BF16)
        primes = sb(ctx, "primes", [P, 8])
        chunk_dst = sb(ctx, "chunk_dst", [P, 1], I32)

        table = dram("table", [NP, D])
        table_hh = dram("table_hh", [NP, 2 * D])
        table_q = dram("table_q", [NP, O])
        edge_net = dram("edge_net", [EP, 2 * O])
        spare_net = dram("spare_net", [P, 1])
        sh_parts = dram("sh_parts", [3, S, CHUNK, P], BF16)
        table_a = dram("table_a", [NP, D + 2])
        record128 = dram("record128", [EP, 2 * D])
        record64 = dram("record64", [EP, D])
        record144 = dram("record144", [P * (CHUNK + T2), O + 2 * H])
        record66 = dram("record66", [EP, D + 2])
        selection = dram("selection", [P, NP])
        spare = dram("spare", [2, P, 1])
        by_first = dram("by_first", [EP + NP, 1])

        def nodes(t):
            return t.rearrange("(j p) f -> p j f", p=P)

        def edges(t):
            return t.rearrange("(c t) f -> c t f", c=P)

        def over(ap, n):
            return ap.unsqueeze(2).to_broadcast([ap.shape[0], ap.shape[1], n])

        def along(ap, n):
            return ap.unsqueeze(1).to_broadcast([ap.shape[0], n, ap.shape[1]])

        def step(eng, ins, sig, k):
            ins.then_inc(sig.sem, 1)
            eng.wait_ge(sig.sem, sig.base + k)

        def load_and_flags():
            with ExitStack() as st:
                prev_i = sb(st, "prev_i", [P, CHUNK], I32)
                dstf = sb(st, "dstf", [P, 2, CHUNK])
                anystart = sb(st, "anystart", [P, 1])
                anyrow = sb(st, "anyrow", [P, P])
                with nc.Block() as block:
                    @block.sync
                    def _(sp):
                        sp.dma_start(dst_i[:, :], a["dst_ext"][1:1 + EP].rearrange("(c t) -> c t", c=P)).then_inc(loaded.sem, 16)
                        sp.dma_start(prev_i[:, :], a["dst_ext"][0:EP].rearrange("(c t) -> c t", c=P)).then_inc(loaded.sem, 16)
                        sp.dma_start(src_i[:, :], a["src_pad"].rearrange("(c t) -> c t", c=P)).then_inc(loaded.sem, 16)
                        sp.wait_ge(vec.sem, vec.base + 1)
                        sp.dma_start(x_sb[:, 0:NT - 1, :], a["x"][0:P * (NT - 1), :].rearrange("(j p) f -> p j f", p=P)).then_inc(loaded.sem, 16)
                        sp.dma_start(x_sb[0:LAST, NT - 1, :], a["x"][P * (NT - 1):N, :]).then_inc(loaded.sem, 16)

                    @block.gpsimd
                    def _(g):
                        g.memset(holder[:, :], 0.0)
                        step(g, g.memset(ident[:, :], 0.0), pool, 1)
                        step(g, g.affine_select(out=ident[:, :], in_=ident[:, :], compare_op=ALU.not_equal, fill=1.0,
                                                base=0, pattern=[[-1, P]], channel_multiplier=1), pool, 2)
                        step(g, g.memset(ones[:, :], 1.0), pool, 3)
                        g.affine_select(out=ones_last[:, :], in_=ones[:, :], compare_op=ALU.is_gt, fill=0.0,
                                        base=LAST, pattern=[[0, P]], channel_multiplier=-1).then_inc(pool.sem, 1)

                    @block.vector
                    def _(v):
                        v.memset(x_sb[:, NT - 1, :], 0.0).then_inc(vec.sem, 1)
                        v.wait_ge(loaded.sem, loaded.base + 5 * 16)
                        v.tensor_copy(dstf[:, 0, :], dst_i[:, :])
                        v.tensor_copy(chunk_dst[:, :], dst_i[:, 0:1])
                        step(v, v.tensor_copy(dstf[:, 1, :], prev_i[:, :]), vec, 2)
                        step(v, v.tensor_tensor(neg[:, :], dstf[:, 0, :], dstf[:, 1, :], ALU.is_equal), vec, 3)
                        step(v, v.tensor_scalar(neg[:, :], neg[:, :], -1.0, -NEG, ALU.add, ALU.mult), vec, 4)
                        step(v, v.tensor_reduce(anystart[:, :], neg[:, :], X, ALU.min), vec, 5)
                        v.wait_ge(pool.sem, pool.base + 3)
                        v.memset(neg[:, 0:1], NEG)
                        v.tensor_scalar(anyrow[:, :], ones[:, :], anystart[:, 0:1], None, ALU.mult).then_inc(vec.sem, 1)
                        v.wait_ge(mm.sem, mm.base + 1)
                        step(v, v.tensor_copy(negrow[:, :], bank[0][:, 0:P]), vec, 7)
                        v.tensor_scalar(controw[:, :], negrow[:, :], 0.0, None, ALU.is_equal)

                    @block.tensor
                    def _(pe):
                        pe.wait_ge(vec.sem, vec.base + 6)
                        pe.wait_ge(pool.sem, pool.base + 2)
                        nc.tensor.matmul(bank[0][:, 0:P], anyrow[:, :], ident[:, :], start=True, stop=True).then_inc(mm.sem, 1)
                loaded.base += 5 * 16
                vec.base += 7
                pool.base += 4
                mm.base += 1

        def index_nodes():
            with ExitStack() as st:
                HI, LO = NT, P
                select = sb(st, "select", [P, NP])
                chan_i = sb(st, "chan_i", [P, 1], I32)
                chan_f = sb(st, "chan_f", [P, 1])
                upper = sb(st, "upper", [P, P])
                cnt = sb(st, "cnt", [HI, LO])
                cum = sb(st, "cum", [HI, LO])
                before = sb(st, "before", [HI, 1])
                node_id = sb(st, "node_id", [HI, LO])
                node_i = sb(st, "node_i", [HI, LO], I32)
                q = sb(st, "q", [HI, 8, LO])
                counts = bank[0][0:HI, 0:LO]
                with nc.Block() as block:
                    @block.sync
                    def _(sp):
                        sp.wait_ge(vec.sem, vec.base + 18 + len(GROUPS))
                        sp.dma_start(selection[:, :], select[:, :]).then_inc(stored.sem, 16)
                        sp.wait_ge(stored.sem, stored.base + 16)

                    @block.gpsimd
                    def _(g):
                        g.iota(chan_i[:, :], pattern=[[0, 1]], base=0, channel_multiplier=1)
                        g.iota(node_i[:, :], pattern=[[1, LO]], base=EP, channel_multiplier=LO)
                        g.affine_select(out=upper[:, :], in_=ones[:, :], compare_op=ALU.is_gt, fill=0.0,
                                        base=0, pattern=[[1, P]], channel_multiplier=-1).then_inc(pool.sem, 1)

                    @block.vector
                    def _(v):
                        v.wait_ge(pool.sem, pool.base + 1)
                        v.tensor_copy(chan_f[:, :], chan_i[:, :])
                        v.tensor_copy(node_id[:, :], node_i[:, :])
                        step(v, v.tensor_copy(cnt[:, :], counts), vec, 1)
                        step(v, v.tensor_tensor_scan(cum[:, :], ones[0:HI, :], cnt[:, :], 0.0, ALU.mult, ALU.add), vec, 2)
                        v.wait_ge(mm.sem, mm.base + 1)
                        step(v, v.tensor_copy(before[:, :], bank[1][0:HI, 0:1]), vec, 3)
                        step(v, v.tensor_scalar(cum[:, :], cum[:, :], before[:, 0:1], None, ALU.add), vec, 4)
                        v.tensor_scalar(q[:, 0, :], cum[:, :], -1.0, 0.0, ALU.add, ALU.max)
                        v.tensor_scalar(q[:, 2, :], cnt[:, :], 0.0, None, ALU.is_gt)
                        step(v, v.tensor_tensor(q[:, 1, :], cum[:, :], cnt[:, :], ALU.subtract), vec, 5)
                        step(v, v.tensor_scalar(q[:, 3, :], q[:, 0, :], 0.5, 1.0 / CHUNK, ALU.add, ALU.mult), vec, 6)
                        step(v, v.tensor_scalar(q[:, 3, :], q[:, 3, :], -0.5, 12582912.0, ALU.add, ALU.add), vec, 7)
                        step(v, v.tensor_scalar(q[:, 3, :], q[:, 3, :], -12582912.0, None, ALU.add), vec, 8)
                        step(v, v.scalar_tensor_tensor(q[:, 4, :], q[:, 3, :], float(CHUNK), q[:, 1, :], ALU.mult, ALU.is_gt), vec, 9)
                        step(v, v.tensor_tensor(q[:, 4, :], q[:, 4, :], q[:, 2, :], ALU.mult), vec, 10)
                        step(v, v.tensor_tensor(q[:, 5, :], q[:, 4, :], q[:, 3, :], ALU.mult), vec, 11)
                        step(v, v.tensor_scalar(q[:, 5, :], q[:, 5, :], -1.0, None, ALU.add), vec, 12)
                        step(v, v.tensor_tensor(q[:, 6, :], q[:, 1, :], node_id[:, :], ALU.subtract), vec, 13)
                        step(v, v.tensor_tensor(q[:, 6, :], q[:, 6, :], q[:, 2, :], ALU.mult), vec, 14)
                        step(v, v.tensor_tensor(q[:, 6, :], q[:, 6, :], node_id[:, :], ALU.add), vec, 15)
                        step(v, v.tensor_scalar(q[:, 7, :], q[:, 3, :], 1.0, float(T2), ALU.add, ALU.mult), vec, 16)
                        step(v, v.tensor_tensor(q[:, 7, :], q[:, 7, :], q[:, 0, :], ALU.add), vec, 17)
                        v.wait_ge(mm.sem, mm.base + 2)
                        v.tensor_copy(last144_i[:, :], bank[1][:, 4 * HI:5 * HI])
                        v.tensor_copy(last_i[:, :], bank[1][:, 0:HI])
                        v.tensor_copy(first_i[:, :], bank[1][:, HI:2 * HI])
                        v.tensor_copy(has[:, :], bank[1][:, 2 * HI:3 * HI])
                        v.tensor_scalar(nocarry[:, :], bank[1][:, 3 * HI:4 * HI], 0.0, NEG, ALU.is_lt, ALU.mult).then_inc(vec.sem, 1)
                        for n, (g0, m) in enumerate(GROUPS):
                            v.wait_ge(mm2.sem, mm2.base + n + 1)
                            v.tensor_scalar(select[:, g0 * P:(g0 + m) * P], bank[2 + n % 2][:, 0:m * P], chan_f[:, 0:1], None,
                                            ALU.is_equal).then_inc(vec.sem, 1)

                    @block.tensor
                    def _(pe):
                        pe.wait_ge(vec.sem, vec.base + 2)
                        pe.wait_ge(pool.sem, pool.base + 1)
                        nc.tensor.matmul(bank[1][0:HI, 0:1], upper[0:HI, 0:HI], cum[:, LO - 1:LO], start=True, stop=True).then_inc(mm.sem, 1)
                        pe.wait_ge(vec.sem, vec.base + 17)
                        for k, which in enumerate((0, 6, 2, 5, 7)):
                            last = nc.tensor.transpose(bank[1][:, k * HI:(k + 1) * HI], q[:, which, :], ident[0:HI, 0:HI])
                        last.then_inc(mm.sem, 1)
                        for n, (g0, m) in enumerate(GROUPS):
                            if n >= 2:
                                pe.wait_ge(vec.sem, vec.base + 18 + n - 1)
                            for j in range(m):
                                last = nc.tensor.matmul(bank[2 + n % 2][:, j * P:(j + 1) * P],
                                                        ident[0:HI, g0 + j:g0 + j + 1].to_broadcast([HI, P]),
                                                        q[:, 5, :], start=True, stop=True)
                            last.then_inc(mm2.sem, 1)
                stored.base += 16
                pool.base += 1
                vec.base += 18 + len(GROUPS)
                mm.base += 2
                mm2.base += len(GROUPS)

        def clear_by_first():
            with ExitStack() as st:
                z = sb(st, "z", [P, CHUNK + NT])
                with nc.Block() as block:
                    @block.vector
                    def _(v):
                        v.memset(z[:, :], 0.0).then_inc(vec.sem, 1)

                    @block.sync
                    def _(sp):
                        sp.wait_ge(vec.sem, vec.base + 1)
                        sp.dma_start(by_first.rearrange("(p f) o -> p (f o)", p=P), z[:, :]).then_inc(stored.sem, 16)
                        sp.wait_ge(stored.sem, stored.base + 16)
                vec.base += 1
                stored.base += 16

        def load_weights(parts):
            with nc.Block() as block:
                @block.sync
                def _(sp):
                    for tile, source in parts:
                        sp.dma_start(tile, source).then_inc(loaded.sem, 16)
                    sp.wait_ge(loaded.sem, loaded.base + 16 * len(parts))
            loaded.base += 16 * len(parts)

        def spread(vector_ap):
            return vector_ap.unsqueeze(0).to_broadcast([P, vector_ap.shape[0]])

        def store_nodes(pairs):
            with nc.Block() as block:
                @block.sync
                def _(sp):
                    for t, tile in pairs:
                        sp.dma_start(nodes(t), tile).then_inc(stored.sem, 16)
                    sp.wait_ge(stored.sem, stored.base + 16 * len(pairs))
            stored.base += 16 * len(pairs)

        def layer_norm_relu(dst, src, tmp, stat, gamma=None, beta=None):
            affine = gamma is not None
            with nc.Block() as block:
                @block.vector
                def _(v):
                    step(v, v.tensor_reduce(stat[:, 0, :], src, X, ALU.add), vec, 1)
                    step(v, v.tensor_scalar(stat[:, 0, :], stat[:, 0, :], 1.0 / D, None, ALU.mult), vec, 2)
                    step(v, v.tensor_tensor(tmp, src, over(stat[:, 0, :], D), ALU.subtract), vec, 3)
                    step(v, v.tensor_tensor(dst, tmp, tmp, ALU.mult), vec, 4)
                    step(v, v.tensor_reduce(stat[:, 1, :], dst, X, ALU.add), vec, 5)
                    v.tensor_scalar(stat[:, 1, :], stat[:, 1, :], 1.0 / D, 1e-5, ALU.mult, ALU.add).then_inc(vec.sem, 1)
                    v.wait_ge(act.sem, act.base + 1)
                    step(v, v.reciprocal(stat[:, 1, :], stat[:, 0, :]), vec, 7)
                    step(v, v.tensor_tensor(tmp, tmp, over(stat[:, 1, :], D), ALU.mult), vec, 8)
                    if affine:
                        step(v, v.tensor_tensor(tmp, tmp, along(gamma[:, :], NT), ALU.mult), vec, 9)
                        step(v, v.tensor_tensor(tmp, tmp, along(beta[:, :], NT), ALU.add), vec, 10)
                    v.tensor_scalar(dst, tmp, 0.0, None, ALU.max)

                @block.scalar
                def _(s):
                    s.wait_ge(vec.sem, vec.base + 6)
                    s.activation(stat[:, 0, :], stat[:, 1, :], ACT.Sqrt).then_inc(act.sem, 1)
            vec.base += 10 if affine else 8
            act.base += 1

        def linear(dst, src, weight, K, M, bias=None, add_to=None):
            with ExitStack() as st:
                turned = sb(st, "turned", [P, 2, 512])
                t_ready = [bank[0], bank[1]]
                products = [bank[2], bank[3]]
                with nc.Block() as block:
                    @block.tensor
                    def _(pe):
                        for n in range(len(GROUPS) + 1):
                            if n < len(GROUPS):
                                g0, m = GROUPS[n]
                                if n >= 2:
                                    pe.wait_ge(act.sem, act.base + n - 1)
                                for j in range(m):
                                    last = nc.tensor.transpose(t_ready[n % 2][0:K, j * P:(j + 1) * P], src[:, g0 + j, :], ident[:, :])
                                last.then_inc(mm.sem, 1)
                            if n >= 1:
                                k = n - 1
                                g0, m = GROUPS[k]
                                pe.wait_ge(act.sem, act.base + k + 1)
                                if k >= 2:
                                    pe.wait_ge(vec.sem, vec.base + k - 1)
                                for j in range(m):
                                    last = nc.tensor.matmul(products[k % 2][:, j * M:(j + 1) * M], turned[0:K, k % 2, j * P:(j + 1) * P],
                                                            weight, start=True, stop=True)
                                last.then_inc(mm2.sem, 1)

                    @block.scalar
                    def _(s):
                        for n, (g0, m) in enumerate(GROUPS):
                            s.wait_ge(mm.sem, mm.base + n + 1)
                            if n >= 2:
                                s.wait_ge(mm2.sem, mm2.base + n - 1)
                            s.activation(turned[0:K, n % 2, 0:m * P], t_ready[n % 2][0:K, 0:m * P], ACT.Copy).then_inc(act.sem, 1)

                    @block.vector
                    def _(v):
                        for n, (g0, m) in enumerate(GROUPS):
                            v.wait_ge(mm2.sem, mm2.base + n + 1)
                            got = products[n % 2][:, 0:m * M].rearrange("p (j f) -> p j f", f=M)
                            if bias is not None:
                                v.tensor_tensor(dst[:, g0:g0 + m, :], got, along(bias, m), ALU.add).then_inc(vec.sem, 1)
                            elif add_to is not None:
                                v.tensor_tensor(dst[:, g0:g0 + m, :], got, add_to[:, g0:g0 + m, :], ALU.add).then_inc(vec.sem, 1)
                            else:
                                v.tensor_copy(dst[:, g0:g0 + m, :], got).then_inc(vec.sem, 1)
                n = len(GROUPS)
                mm.base += n
                mm2.base += n
                act.base += n
                vec.base += n

        def collect(width, tail_max, tail_sums, pieces, chain, carried, collected, record, at_last):
            k = len(tail_sums)
            online = tail_max is not None
            length = sum(p[3] for p in pieces)
            with ExitStack() as st:
                run = sb(st, "run", [width, k + 1, P])
                decay = sb(st, "decay", [width, P])
                weight = sb(st, "weight", [width, P])
                term = sb(st, "term", [width, k, P])
                select = sb(st, "select", [P, NP])
                with nc.Block() as block:
                    @block.sync
                    def _(sp):
                        sp.dma_start(select[:, :], selection[:, :]).then_inc(loaded.sem, 16)

                    @block.gpsimd
                    def _(g):
                        for j in range(NT):
                            nc.gpsimd.indirect_dma_start(collected[:, j, :], None, record,
                                                         bass.IndirectOffsetOnAxis(ap=at_last[:, j:j + 1], axis=0)).then_inc(rows.sem, 16)
                        g.wait_ge(rows.sem, rows.base + 16 * NT)

                    @block.tensor
                    def _(pe):
                        if online:
                            nc.tensor.transpose(bank[0][0:width, 0:P], tail_max, ident[:, :])
                        for n in range(k):
                            last = nc.tensor.transpose(bank[0][0:width, (n + 1) * P:(n + 2) * P], tail_sums[n], ident[:, :])
                        last.then_inc(mm.sem, 1)
                        pe.wait_ge(vec.sem, vec.base + (5 if online else 2))
                        for n in range(0 if online else 1, k + 1):
                            at = (n if online else n - 1) * width
                            last = nc.tensor.transpose(bank[1][:, at:at + width], run[:, n, :], ident[0:width, 0:width])
                        last.then_inc(mm.sem, 1)
                        pe.wait_ge(vec.sem, vec.base + (6 if online else 3))
                        pe.wait_ge(loaded.sem, loaded.base + 16)
                        for j in range(NT):
                            if j >= 4:
                                pe.wait_ge(act.sem, act.base + (1 if online else 0) + j - 3)
                            nc.tensor.matmul(bank[2 + j % 4][:, 0:length], select[:, j * P:(j + 1) * P], chain[:, 0:length],
                                             start=True, stop=True).then_inc(mm2.sem, 1)

                    @block.vector
                    def _(v):
                        v.wait_ge(mm.sem, mm.base + 1)
                        if online:
                            v.memset(decay[:, 0:1], NEG)
                            step(v, v.tensor_tensor_scan(run[:, 0, :], negrow[0:width, :], bank[0][0:width, 0:P], NEG, ALU.add, ALU.max), vec, 1)
                            v.tensor_tensor(decay[:, 1:P], run[:, 0, 0:P - 1], run[:, 0, 1:P], ALU.subtract)
                            step(v, v.tensor_tensor(weight[:, :], bank[0][0:width, 0:P], run[:, 0, :], ALU.subtract), vec, 2)
                            v.tensor_tensor(decay[:, :], decay[:, :], negrow[0:width, :], ALU.add).then_inc(vec.sem, 1)
                            v.wait_ge(act.sem, act.base + 1)
                            step(v, v.tensor_tensor(term[:, :, :], bank[0][0:width, P:(k + 1) * P].rearrange("p (n c) -> p n c", c=P),
                                                    along(weight[:, :], k), ALU.mult), vec, 4)
                            for n in range(k):
                                last = v.tensor_tensor_scan(run[:, n + 1, :], decay[:, :], term[:, n, :], 0.0, ALU.mult, ALU.add)
                            last.then_inc(vec.sem, 1)
                        else:
                            step(v, v.tensor_copy(term[:, 0, :], bank[0][0:width, P:2 * P]), vec, 1)
                            v.tensor_tensor_scan(run[:, 1, :], controw[0:width, :], term[:, 0, :], 0.0, ALU.mult, ALU.add).then_inc(vec.sem, 1)
                        v.wait_ge(mm.sem, mm.base + 2)
                        for to, first, every, count in pieces:
                            last = v.tensor_copy(chain[:, to:to + count], bank[1][:, first:first + (count - 1) * every + 1:every])
                        last.then_inc(vec.sem, 1)

                    @block.scalar
                    def _(s):
                        if online:
                            s.wait_ge(vec.sem, vec.base + 3)
                            s.activation(decay[:, :], decay[:, :], ACT.Exp)
                            s.activation(weight[:, :], weight[:, :], ACT.Exp).then_inc(act.sem, 1)
                        for j in range(NT):
                            s.wait_ge(mm2.sem, mm2.base + j + 1)
                            s.activation(carried[:, j, :], bank[2 + j % 4][:, 0:length], ACT.Copy).then_inc(act.sem, 1)
                mm.base += 2
                mm2.base += NT
                vec.base += 6 if online else 3
                act.base += NT + (1 if online else 0)
                loaded.base += 16
                rows.base += 16 * NT

        def start_count(sp, kept):
            for b in range(2):
                sp.dma_start(spare[b], holder[:, 0:1]).then_inc(kept[b].sem, 16)

        def hold(g):
            g.tensor_tensor(holder[:, 1:2], holder[:, 0:1], holder[:, 0:1], ALU.add)

        def gathers(g, index, where, filled, source):
            for t in range(where.shape[1]):
                nc.gpsimd.indirect_dma_start(where[:, t, :], None, source,
                                             bass.IndirectOffsetOnAxis(ap=index[:, t:t + 1], axis=0)).then_inc(filled, 16)

        def edges_logsumexp(l, rec, net):
            tag = f"lse{l}"
            c0, c1 = NET_COLUMNS[l]
            n_net = c1 - c0
            w1, w2, b1, b2 = net
            HI, LO = NT, P
            counts = bank[0][0:HI, 0:LO]
            n_cols = 2 * PAIRS * n_net
            with ExitStack() as st:
                ea = sb(st, "ea", [D, n_net, P])
                hid = [sb(st, f"hid{k}", [P, P]) for k in range(2)]
                net_out = sb(st, "net_out", [P, n_net, 2 * O])
                if l == 0:
                    iota_i = sb(st, "iota_i", [P, P], I32)
                    iota_f = sb(st, "iota_f", [P, P])
                    digits_i = sb(st, "digits_i", [P, 2, T], I32)
                    digits = sb(st, "digits", [P, 2, T])
                    hot_hi = sb(st, "hot_hi", [P, T, HI], BF16)
                    hot_lo = sb(st, "hot_lo", [P, T, LO], BF16)
                    zero = sb(st, "zero", [P, P], BF16)
                got = [sb(st, f"got{b}", [P, T, D]) for b in range(2)]
                fall = sb(st, "fall", [P, T, D])
                index = sb(st, "index", [P, 2, T], I32)
                neg_t = sb(st, "neg_t", [P, T])
                filled = [signal(f"{tag}_rows_here{b}") for b in range(2)]
                done = [signal(f"{tag}_record_ready{b}") for b in range(2)]
                kept = [signal(f"{tag}_record_stored{b}") for b in range(2)]

                def column(i, b, c):
                    return i * (2 * n_net) + (b * n_net + c + 4)

                with nc.Block() as block:
                    @block.gpsimd
                    def _(g):
                        if l == 0:
                            step(g, g.iota(iota_i[:, :], pattern=[[1, P]], base=0, channel_multiplier=0), pool, 1)
                            pool.base += 1
                        with g.Fori(0, PAIRS) as i:
                            for b in range(2):
                                g.wait_ge(done[b].sem, i + 1)
                                g.tensor_copy(index[:, b, :], src_i[:, bass.ds((i * 2 + b) * T, T)]).then_inc(pool.sem, 1)
                                g.wait_ge(pool.sem, pool.base + 2 * i + b + 1)
                                hold(g)
                                gathers(g, index[:, b, :], got[b], filled[b].sem, table)

                    @block.tensor
                    def _(pe):
                        pe.wait_ge(hot.sem, hot.base + 1)
                        for k in range(3):
                            for bk, sig in ((1, net_hid), (3, net_done)):
                                nc.tensor.matmul(bank[bk][:, 0:P], ident[:, :], ident[:, :], start=True, stop=True).then_inc(sig.sem, 1)
                        if l == 0:
                            nc.tensor.matmul(counts, zero[:, 0:HI], zero[:, 0:LO], start=True, stop=False).then_inc(counted.sem, 1)

                        def hidden(i, b, c):
                            if c == 0:
                                pe.wait_ge(net_here.sem, i * 32 + (net_here.base + 16 * (b + 1)))
                            pe.wait_ge(net_relu.sem, column(i, b, c - 2) + net_relu.base)
                            nc.tensor.matmul(bank[1 + c % 2][:, 0:P], w1[:, :], ea[:, c, :], start=True, stop=True).then_inc(net_hid.sem, 1)

                        with pe.Fori(0, PAIRS) as i:
                            for b in range(2):
                                if l == 0:
                                    pe.wait_ge(hot.sem, i * 2 + (b + 2))
                                    for t in range(T):
                                        last = nc.tensor.matmul(counts, hot_hi[:, t, :], hot_lo[:, t, :], start=False, stop=False)
                                    last.then_inc(counted.sem, 1)
                                hidden(i, b, 0)
                                for c in range(n_net):
                                    if c + 1 < n_net:
                                        hidden(i, b, c + 1)
                                    pe.wait_ge(net_relu.sem, column(i, b, c) + net_relu.base)
                                    pe.wait_ge(net_out_ready.sem, column(i, b, c - 2) + net_out_ready.base)
                                    to = bank[3 + c % 2][:, 0:2 * O]
                                    for m in range(3):
                                        nc.tensor.matmul(to, net_ones[:, :], b2[:, m, :], start=m == 0, stop=False)
                                    nc.tensor.matmul(to, hid[c % 2][:, :], w2[:, :], start=False, stop=True).then_inc(net_done.sem, 1)
                        if l == 0:
                            nc.tensor.matmul(counts, zero[:, 0:HI], zero[:, 0:LO], start=False, stop=True)

                    @block.vector
                    def _(v):
                        if l == 0:
                            v.memset(zero[:, :], 0.0)
                            v.wait_ge(pool.sem, pool.base)
                            v.tensor_copy(iota_f[:, :], iota_i[:, :])
                        v.memset(fall[:, 0, 0:1], 0.0).then_inc(hot.sem, 1)
                        v.memset(rec[1][:, T - 1, 0:D], 0.0).then_inc(done[0].sem, 1)
                        v.memset(rec[1][:, T - 1, D:2 * D], 0.0).then_inc(done[1].sem, 1)
                        with v.Fori(0, PAIRS) as i:
                            for b in range(2):
                                now, past = rec[b], rec[1 - b]
                                at = vec.base + 8 * i + 4 * b
                                v.wait_ge(done[1 - b].sem, i + b + 1)
                                v.tensor_copy(neg_t[:, :], neg[:, bass.ds((i * 2 + b) * T, T)]).then_inc(vec.sem, 1)
                                v.wait_ge(vec.sem, at + 1)
                                if l == 0:
                                    some = dst_i[:, bass.ds((i * 2 + b) * T, T)]
                                    v.tensor_scalar(digits_i[:, 0, :], some, 7, None, ALU.logical_shift_right)
                                    v.tensor_scalar(digits_i[:, 1, :], some, P - 1, None, ALU.bitwise_and).then_inc(digit.sem, 1)
                                    v.wait_ge(digit.sem, i * 4 + (2 * b + 1))
                                    v.tensor_copy(digits[:, :, :], digits_i[:, :, :]).then_inc(digit.sem, 1)
                                    v.wait_ge(digit.sem, i * 4 + (2 * b + 2))
                                    v.wait_ge(counted.sem, i * 2 + (b + 1))
                                    v.tensor_tensor(hot_hi[:, :, :], over(digits[:, 0, :], HI), along(iota_f[:, 0:HI], T), ALU.is_equal)
                                    v.tensor_tensor(hot_lo[:, :, :], over(digits[:, 1, :], LO), along(iota_f[:, :], T), ALU.is_equal).then_inc(hot.sem, 1)
                                v.wait_ge(filled[b].sem, 16 * T * (i + 1))
                                v.wait_ge(kept[b].sem, 16 * i + 16)
                                for f in range(D):
                                    last = v.tensor_tensor_scan(now[:, :, f], neg_t[:, :], got[b][:, :, f], past[:, T - 1, f:f + 1], ALU.add, ALU.max)
                                last.then_inc(vec.sem, 1)
                                v.wait_ge(vec.sem, at + 2)
                                v.tensor_tensor(fall[:, 0, :], past[:, T - 1, 0:D], now[:, 0, 0:D], ALU.subtract)
                                v.tensor_tensor(fall[:, 1:T, :], now[:, 0:T - 1, 0:D], now[:, 1:T, 0:D], ALU.subtract)
                                v.tensor_tensor(got[b][:, :, :], got[b][:, :, :], now[:, :, 0:D], ALU.subtract).then_inc(vec.sem, 1)
                                v.wait_ge(vec.sem, at + 3)
                                v.tensor_tensor(fall[:, :, :], fall[:, :, :], over(neg_t[:, :], D), ALU.add).then_inc(vec.sem, 1)
                                v.wait_ge(act.sem, act.base + 2 * i + b + 1)
                                for f in range(D):
                                    last = v.tensor_tensor_scan(now[:, :, D + f], fall[:, :, f], got[b][:, :, f], past[:, T - 1, D + f:D + f + 1], ALU.mult, ALU.add)
                                last.then_inc(done[b].sem, 1)

                    @block.scalar
                    def _(s):
                        for k in range(3):
                            for m, sig in enumerate((net_relu, net_out_ready)):
                                s.activation(primes[:, 2 * k + m:2 * k + m + 1], holder[:, 0:1], ACT.Copy).then_inc(sig.sem, 1)
                        s.dma_start(spare_net[:, :], holder[:, 0:1]).then_inc(net_kept.sem, 16)

                        def relu(i, b, c):
                            s.wait_ge(net_hid.sem, column(i, b, c) + net_hid.base)
                            s.wait_ge(net_done.sem, column(i, b, c - 2) + net_done.base)
                            s.activation(hid[c % 2][:, :], bank[1 + c % 2][:, 0:P], ACT.Relu, bias=b1[:, 0:1]).then_inc(net_relu.sem, 1)

                        with s.Fori(0, PAIRS) as i:
                            for b in range(2):
                                s.wait_ge(vec.sem, vec.base + 8 * i + 4 * b + 4)
                                s.activation(fall[:, :, :], fall[:, :, :], ACT.Exp)
                                s.activation(got[b][:, :, :], got[b][:, :, :], ACT.Exp).then_inc(act.sem, 1)
                                relu(i, b, 0)
                                s.wait_ge(net_kept.sem, i * 32 + (net_kept.base + 16 * (b + 1)))
                                for c in range(n_net):
                                    if c + 1 < n_net:
                                        relu(i, b, c + 1)
                                    s.wait_ge(net_done.sem, column(i, b, c) + net_done.base)
                                    s.activation(net_out[:, c, :], bank[3 + c % 2][:, 0:2 * O], ACT.Copy).then_inc(net_out_ready.sem, 1)
                                s.wait_ge(net_out_ready.sem, column(i, b, n_net - 1) + net_out_ready.base)
                                s.dma_start(edges(edge_net)[:, bass.ds((i * 2 + b) * T + c0, n_net), :], net_out[:, :, :]).then_inc(net_kept.sem, 16)
                        s.wait_ge(net_kept.sem, net_kept.base + 16 * (2 * PAIRS + 1))

                    @block.sync
                    def _(sp):
                        start_count(sp, kept)
                        sp.dma_start(ea[:, :, :], a["edge64"][:, c0:c1, :]).then_inc(net_here.sem, 16)
                        with sp.Fori(0, PAIRS) as i:
                            for b in range(2):
                                sp.wait_ge(net_hid.sem, column(i, b, n_net - 1) + net_hid.base)
                                sp.dma_start(ea[:, :, :], a["edge64"][:, bass.ds((i * 2 + b + 1) * T + c0, n_net), :]).then_inc(net_here.sem, 16)
                                sp.wait_ge(done[b].sem, i + 2)
                                sp.dma_start(edges(record128)[:, bass.ds((i * 2 + b) * T, T), :], rec[b][:, :, :]).then_inc(kept[b].sem, 16)
                        for b in range(2):
                            sp.wait_ge(kept[b].sem, 16 * PAIRS + 16)
                        sp.wait_ge(net_here.sem, net_here.base + 16 * (2 * PAIRS + 1))
                pool.base += 2 * PAIRS
                vec.base += 8 * PAIRS
                act.base += 2 * PAIRS
                hot.base += 1 + (2 * PAIRS if l == 0 else 0)
                for sig in (net_hid, net_done, net_relu, net_out_ready):
                    sig.base += 3 + n_cols
                net_here.base += 16 * (2 * PAIRS + 1)
                net_kept.base += 16 * (2 * PAIRS + 1)

        def logsumexp_layers():
            with ExitStack() as st:
                w_in = sb(st, "w_in", [D, D])
                w1 = sb(st, "w1", [D, P])
                w2 = sb(st, "w2", [P, 2 * O])
                b1 = sb(st, "b1", [P, 1])
                b2 = sb(st, "b2", [1, 2 * O])
                b2_parts = sb(st, "b2_parts", [1, 3, 2 * O], BF16)
                w_l = sb(st, "w_l", [2 * D, 3, D])
                vecs = sb(st, "vecs", [P, 10, D])
                with nc.Block() as block:
                    @block.vector
                    def _(v):
                        v.memset(w2[:, :], 0.0)
                        v.memset(net_ones[:, :], 1.0)
                load_weights([(w1[:, 0:D], a["L2_gnn_k_w1"]), (w1[:, D:P], a["L2_gnn_v_w1"]),
                              (b1[0:D, :], a["L2_gnn_k_b1"].unsqueeze(1)), (b1[D:P, :], a["L2_gnn_v_b1"].unsqueeze(1)),
                              (b2[:, 0:O], a["L2_gnn_k_b2"].unsqueeze(0)), (b2[:, O:2 * O], a["L2_gnn_v_b2"].unsqueeze(0)),
                              (w2[0:D, 0:O], a["L2_gnn_k_w2"]), (w2[D:P, O:2 * O], a["L2_gnn_v_w2"]),
                              (w_in[:, :], a["L0_gnn_W_inT"]), (w_l[:, :, :], a["L0_gnn_W_lT"].rearrange("l k m -> k l m")),
                              (vecs[:, 0, :], spread(a["L0_gnn_b_in"]))]
                             + [(vecs[:, 1 + 3 * l + n, :], spread(a[name][l]))
                                for l in range(3) for n, name in enumerate(("L0_gnn_b_l", "L0_gnn_gamma_l", "L0_gnn_beta_l"))])
                with nc.Block() as block:
                    @block.vector
                    def _(v):
                        step(v, v.tensor_copy(b2_parts[:, 0, :], b2[:, :]), vec, 1)
                        step(v, v.tensor_tensor(b2[:, :], b2[:, :], b2_parts[:, 0, :], ALU.subtract), vec, 2)
                        step(v, v.tensor_copy(b2_parts[:, 1, :], b2[:, :]), vec, 3)
                        step(v, v.tensor_tensor(b2[:, :], b2[:, :], b2_parts[:, 1, :], ALU.subtract), vec, 4)
                        v.tensor_copy(b2_parts[:, 2, :], b2[:, :])
                vec.base += 4
                with ExitStack() as s2:
                    tmp = sb(s2, "tmp", [P, NT, D])
                    stat = sb(s2, "stat", [P, 2, NT])
                    layer_norm_relu(agg, x_sb[:, :, :], tmp[:, :, :], stat)
                    linear(h_sb, agg, w_in[:, :], D, D, bias=vecs[:, 0, :])
                for l in range(3):
                    store_nodes([(table, h_sb)])
                    with ExitStack() as s2:
                        rec = [sb(s2, f"rec{b}", [P, T, 2 * D]) for b in range(2)]
                        edges_logsumexp(l, rec, (w1, w2, b1, b2_parts))
                        if l == 0:
                            index_nodes()
                        with ExitStack() as s3:
                            tail = rec[1][:, T - 1, :]
                            collected = sb(s3, "collected", [P, NT, 2 * D])
                            carried = sb(s3, "carried", [P, NT, 2 * D])
                            chain = sb(s3, "chain", [P, 2 * D])
                            collect(D, tail[:, 0:D], [tail[:, D:2 * D]], [(0, 0, 1, 2 * D)], chain, carried, collected, record128, last_i)
                            join_logsumexp(collected, carried)
                    with ExitStack() as s2:
                        new = sb(s2, "new", [P, NT, D])
                        tmp = sb(s2, "tmp2", [P, NT, D])
                        stat = sb(s2, "stat2", [P, 2, NT])
                        linear(new[:, :, :], hc, w_l[:, l, :], 2 * D, D, bias=vecs[:, 1 + 3 * l, :])
                        layer_norm_relu(agg, new[:, :, :], tmp[:, :, :], stat, vecs[:, 2 + 3 * l, :], vecs[:, 3 + 3 * l, :])
                        with nc.Block() as block:
                            @block.vector
                            def _(v):
                                step(v, v.tensor_tensor(tmp[:, :, :], h_sb, agg, ALU.add), vec, 1)
                                step(v, v.tensor_scalar(h_sb, tmp[:, :, :], 0.5, None, ALU.mult), vec, 2)
                                if l == 2:
                                    v.tensor_tensor(x_sb[:, :, :], x_sb[:, :, :], h_sb, ALU.add)
                        vec.base += 2

        def join_logsumexp(collected, carried):
            m1, s1 = collected[:, :, 0:D], collected[:, :, D:2 * D]
            m2, s2 = carried[:, :, 0:D], carried[:, :, D:2 * D]
            with nc.Block() as block:
                @block.vector
                def _(v):
                    step(v, v.tensor_tensor(m2, m2, over(nocarry[:, :], D), ALU.add), vec, 1)
                    step(v, v.tensor_tensor(agg, m1, m2, ALU.max), vec, 2)
                    v.tensor_tensor(m1, m1, agg, ALU.subtract)
                    v.tensor_tensor(m2, m2, agg, ALU.subtract).then_inc(vec.sem, 1)
                    v.wait_ge(act.sem, act.base + 1)
                    v.tensor_tensor(s1, s1, m1, ALU.mult)
                    step(v, v.tensor_tensor(s2, s2, m2, ALU.mult), vec, 4)
                    step(v, v.tensor_tensor(s1, s1, s2, ALU.add), vec, 5)
                    v.tensor_scalar(s1, s1, 1e-30, None, ALU.max).then_inc(vec.sem, 1)
                    v.wait_ge(act.sem, act.base + 2)
                    step(v, v.tensor_tensor(agg, agg, s1, ALU.add), vec, 7)
                    v.tensor_tensor(agg, agg, over(has[:, :], D), ALU.mult)

                @block.scalar
                def _(s):
                    s.wait_ge(vec.sem, vec.base + 3)
                    s.activation(m1, m1, ACT.Exp)
                    s.activation(m2, m2, ACT.Exp).then_inc(act.sem, 1)
                    s.wait_ge(vec.sem, vec.base + 6)
                    s.activation(s1, s1, ACT.Ln).then_inc(act.sem, 1)
            vec.base += 7
            act.base += 2

        def batch_norm(dst, src, tmp, gamma, beta, relu):
            with ExitStack() as st:
                mean = sb(st, "mean", [P, D])
                scale = sb(st, "scale", [P, 2, D])
                with nc.Block() as block:
                    @block.tensor
                    def _(pe):
                        for k, what in enumerate((src, dst)):
                            if k == 1:
                                pe.wait_ge(vec.sem, vec.base + 3)
                            for j in range(NT):
                                last = nc.tensor.matmul(bank[k][:, 0:D], (ones_last if j == NT - 1 else ones)[:, :], what[:, j, :],
                                                        start=j == 0, stop=j == NT - 1)
                            last.then_inc(mm.sem, 1)

                    @block.vector
                    def _(v):
                        v.wait_ge(mm.sem, mm.base + 1)
                        step(v, v.tensor_scalar(mean[:, :], bank[0][:, 0:D], 1.0 / N, None, ALU.mult), vec, 1)
                        step(v, v.tensor_tensor(tmp, src, along(mean[:, :], NT), ALU.subtract), vec, 2)
                        v.tensor_tensor(dst, tmp, tmp, ALU.mult).then_inc(vec.sem, 1)
                        v.wait_ge(mm.sem, mm.base + 2)
                        v.tensor_scalar(scale[:, 0, :], bank[1][:, 0:D], 1.0 / N, 1e-5, ALU.mult, ALU.add).then_inc(vec.sem, 1)
                        v.wait_ge(act.sem, act.base + 1)
                        step(v, v.reciprocal(scale[:, 0, :], scale[:, 1, :]), vec, 5)
                        step(v, v.tensor_tensor(scale[:, 0, :], scale[:, 0, :], gamma, ALU.mult), vec, 6)
                        step(v, v.tensor_tensor(tmp, tmp, along(scale[:, 0, :], NT), ALU.mult), vec, 7)
                        step(v, v.tensor_tensor(dst, tmp, along(beta, NT), ALU.add), vec, 8)
                        if relu:
                            v.tensor_scalar(dst, dst, 0.0, None, ALU.max)

                    @block.scalar
                    def _(s):
                        s.wait_ge(vec.sem, vec.base + 4)
                        s.activation(scale[:, 1, :], scale[:, 0, :], ACT.Sqrt).then_inc(act.sem, 1)
                mm.base += 2
                vec.base += 8
                act.base += 1

        def edges_weighted_sum(rec, weight):
            with ExitStack() as st:
                got = [sb(st, f"got{b}", [P, T, D]) for b in range(2)]
                index = sb(st, "index", [P, 2, T], I32)
                cont_t = sb(st, "cont_t", [P, T])
                filled = [signal(f"sum_rows_here{b}") for b in range(2)]
                done = [signal(f"sum_record_ready{b}") for b in range(2)]
                kept = [signal(f"sum_record_stored{b}") for b in range(2)]
                with nc.Block() as block:
                    @block.gpsimd
                    def _(g):
                        with g.Fori(0, PAIRS) as i:
                            for b in range(2):
                                g.wait_ge(done[b].sem, i + 1)
                                g.tensor_copy(index[:, b, :], src_i[:, bass.ds((i * 2 + b) * T, T)]).then_inc(pool.sem, 1)
                                g.wait_ge(pool.sem, pool.base + 2 * i + b + 1)
                                hold(g)
                                gathers(g, index[:, b, :], got[b], filled[b].sem, table)

                    @block.vector
                    def _(v):
                        v.memset(rec[1][:, T - 1, 0:D // 2], 0.0).then_inc(done[0].sem, 1)
                        v.memset(rec[1][:, T - 1, D // 2:D], 0.0).then_inc(done[1].sem, 1)
                        with v.Fori(0, PAIRS) as i:
                            for b in range(2):
                                v.wait_ge(done[1 - b].sem, i + b + 1)
                                v.tensor_scalar(cont_t[:, :], neg[:, bass.ds((i * 2 + b) * T, T)], 0.0, None, ALU.is_equal)
                                v.wait_ge(filled[b].sem, 16 * T * (i + 1))
                                v.tensor_tensor(got[b][:, :, :], got[b][:, :, :], over(weight[:, bass.ds((i * 2 + b) * T, T)], D), ALU.mult).then_inc(vec.sem, 1)
                                v.wait_ge(vec.sem, vec.base + 2 * i + b + 1)
                                v.wait_ge(kept[b].sem, 16 * i + 16)
                                for f in range(D):
                                    last = v.tensor_tensor_scan(rec[b][:, :, f], cont_t[:, :], got[b][:, :, f], rec[1 - b][:, T - 1, f:f + 1], ALU.mult, ALU.add)
                                last.then_inc(done[b].sem, 1)

                    @block.sync
                    def _(sp):
                        start_count(sp, kept)
                        with sp.Fori(0, PAIRS) as i:
                            for b in range(2):
                                sp.wait_ge(done[b].sem, i + 2)
                                sp.dma_start(edges(record64)[:, bass.ds((i * 2 + b) * T, T), :], rec[b][:, :, :]).then_inc(kept[b].sem, 16)
                        for b in range(2):
                            sp.wait_ge(kept[b].sem, 16 * PAIRS + 16)
                pool.base += 2 * PAIRS
                vec.base += 2 * PAIRS

        def weighted_sum_layer():
            with ExitStack() as st:
                w = sb(st, "w", [D, 2, D])
                vecs = sb(st, "vecs", [P, 6, D])
                weight = sb(st, "weight_e", [P, CHUNK])
                load_weights([(w[:, 0, :], a["L1_gnn_W1"]), (w[:, 1, :], a["L1_gnn_W2"]),
                              (weight[:, :], a["edge_weight"].rearrange("(c t) -> c t", c=P))]
                             + [(vecs[:, n, :], spread(a[f"L1_gnn_{name}"]))
                                for n, name in enumerate(("b1", "gamma1", "beta1", "b2", "gamma2", "beta2"))])
                with ExitStack() as s2:
                    tmp = sb(s2, "tmp", [P, NT, D])
                    stat = sb(s2, "stat", [P, 2, NT])
                    layer_norm_relu(h_sb, x_sb[:, :, :], tmp[:, :, :], stat)
                store_nodes([(table, h_sb)])
                with ExitStack() as s2:
                    rec = [sb(s2, f"rec{b}", [P, T, D]) for b in range(2)]
                    edges_weighted_sum(rec, weight)
                    collected = sb(s2, "collected", [P, NT, D])
                    carried = sb(s2, "carried", [P, NT, D])
                    chain = sb(s2, "chain", [P, D])
                    collect(D, None, [rec[1][:, T - 1, :]], [(0, 0, 1, D)], chain, carried, collected, record64, last_i)
                    with nc.Block() as block:
                        @block.vector
                        def _(v):
                            step(v, v.tensor_tensor(collected[:, :, :], collected[:, :, :], over(has[:, :], D), ALU.mult), vec, 1)
                            step(v, v.tensor_tensor(collected[:, :, :], collected[:, :, :], carried[:, :, :], ALU.add), vec, 2)
                            v.tensor_tensor(agg, collected[:, :, :], h_sb, ALU.add)
                    vec.base += 2
                with ExitStack() as s2:
                    mid = sb(s2, "mid", [P, NT, D])
                    tmp = sb(s2, "tmp", [P, NT, D])
                    for k in range(2):
                        linear(mid[:, :, :], agg, w[:, k, :], D, D, bias=vecs[:, 3 * k, :])
                        batch_norm(agg, mid[:, :, :], tmp[:, :, :], vecs[:, 3 * k + 1, :], vecs[:, 3 * k + 2, :], True)
                    with nc.Block() as block:
                        @block.vector
                        def _(v):
                            v.tensor_tensor(x_sb[:, :, :], x_sb[:, :, :], agg, ALU.add)

        def split_harmonics():
            PIECES = 7
            n = S * CHUNK // PIECES
            flat = a["edge9"].rearrange("s t c -> (s t c)").rearrange("(g p n) -> g p n", p=P, n=n)
            with ExitStack() as st:
                full = [sb(st, f"full{b}", [P, n]) for b in range(2)]
                parts = [sb(st, f"parts{b}", [P, 3, n], BF16) for b in range(2)]
                here = [signal("harmonics_here0"), signal("harmonics_here1")]
                ready = [signal("parts_ready0"), signal("parts_ready1")]
                kept = [signal("parts_stored0"), signal("parts_stored1")]
                with nc.Block() as block:
                    @block.scalar
                    def _(s):
                        for k in range(PIECES):
                            if k >= 2:
                                s.wait_ge(ready[k % 2].sem, k // 2)
                            s.dma_start(full[k % 2][:, :], flat[k]).then_inc(here[k % 2].sem, 16)

                    @block.sync
                    def _(sp):
                        for k in range(PIECES):
                            sp.wait_ge(ready[k % 2].sem, k // 2 + 1)
                            for m in range(3):
                                to = sh_parts[m].rearrange("s t c -> (s t c)").rearrange("(g p n) -> g p n", p=P, n=n)[k]
                                sp.dma_start(to, parts[k % 2][:, m, :]).then_inc(kept[k % 2].sem, 16)
                        for b in range(2):
                            sp.wait_ge(kept[b].sem, 48 * ((PIECES + 1 - b) // 2))

                    @block.vector
                    def _(v):
                        for k in range(PIECES):
                            f, p = full[k % 2], parts[k % 2]
                            v.wait_ge(here[k % 2].sem, 16 * (k // 2 + 1))
                            if k >= 2:
                                v.wait_ge(kept[k % 2].sem, 48 * (k // 2))
                            step(v, v.tensor_copy(p[:, 0, :], f[:, :]), vec, 4 * k + 1)
                            step(v, v.tensor_tensor(f[:, :], f[:, :], p[:, 0, :], ALU.subtract), vec, 4 * k + 2)
                            step(v, v.tensor_copy(p[:, 1, :], f[:, :]), vec, 4 * k + 3)
                            step(v, v.tensor_tensor(f[:, :], f[:, :], p[:, 1, :], ALU.subtract), vec, 4 * k + 4)
                            v.tensor_copy(p[:, 2, :], f[:, :]).then_inc(ready[k % 2].sem, 1)
                vec.base += 4 * PIECES

        def edges_attention(rec):
            C = 2 * T2
            W = O + 2 * H
            K5 = 5
            with ExitStack() as st:
                c_w = sb(st, "c_w", [P, K5, 2 * O])
                pick = sb(st, "pick", [3 * S, K5, 2, D], BF16)
                xg = [sb(st, f"xg{b}", [P, G, 2 * D]) for b in range(2)]
                qg = [sb(st, f"qg{b}", [P, G, O]) for b in range(2)]
                wg = [sb(st, f"wg{b}", [P, G, 2 * O]) for b in range(2)]
                sh = [sb(st, f"sh{b}", [3 * S, G, P], BF16) for b in range(2)]
                vv = [sb(st, f"vv{b}", [P, T2, O]) for b in range(2)]
                logit = [sb(st, f"logit{b}", [P, T2, H]) for b in range(2)]
                neg_t = [sb(st, f"neg_t{b}", [P, T2]) for b in range(2)]
                fall = sb(st, "fall", [P, T2, H])
                xt = [sb(st, f"xt{k}", [P, P]) for k in range(2)]
                zt = [sb(st, f"zt{k}", [P, K5, P]) for k in range(2)]
                kk = [sb(st, f"kk{k}", [P, O]) for k in range(2)]
                index = sb(st, "index", [P, 2, 2, G], I32)
                filled = [signal(f"att_rows_here{b}") for b in range(2)]
                inputs = [signal(f"att_edges_here{b}") for b in range(2)]
                kept = [signal(f"att_record_stored{b}") for b in range(2)]
                tails = [signal(f"att_record_ready{b}") for b in range(2)]
                left = [signal(f"att_rows_used{b}") for b in range(2)]
                primed = sb(st, "primed", [P, 32])
                turned, xt_ready, z_ready = signal("x_turned_sh_spread"), signal("xt_ready"), signal("z_ready")
                products, joined = signal("products_done"), signal("kv_joined")
                tail_v, tail_a = signal("tail_vec"), signal("tail_exp")
                chain_v = signal("column_vec")

                def done(i, c):
                    return i * C + (c + 4)

                load_weights([(c_w[:, 0:4, 0:O], a["L2_gnn_Cqk_s"][0:512, :].rearrange("(k p) o -> p k o", p=P)),
                              (c_w[:, 0:4, O:2 * O], a["L2_gnn_Cv_s"][0:512, :].rearrange("(k p) o -> p k o", p=P)),
                              (c_w[0:D, 4, 0:O], a["L2_gnn_Cqk_s"][512:576, :]), (c_w[0:D, 4, O:2 * O], a["L2_gnn_Cv_s"][512:576, :]),
                              ])

                with nc.Block() as block:
                    @block.gpsimd
                    def _(g):
                        step(g, g.memset(pick[:, :, :, :], 0.0), pool, 1)
                        for part in range(3):
                            step(g, g.affine_select(out=pick[:, :, :, :], in_=pick[:, :, :, :], compare_op=ALU.not_equal, fill=1.0,
                                                    base=-S * part, pattern=[[-2, K5], [-1, 2], [0, D]], channel_multiplier=1), pool, 2 + part)
                        pool.base += 4
                        with g.Fori(0, PAIRS2) as i:
                            for u in range(4):
                                b = u % 2
                                g.wait_ge(left[b].sem, i * 2 + (u // 2 + 1))
                                g.tensor_copy(index[:, b, 0, :], src_i[:, bass.ds((i * 4 + u) * G, G)])
                                g.tensor_copy(index[:, b, 1, :], dst_i[:, bass.ds((i * 4 + u) * G, G)]).then_inc(pool.sem, 1)
                                g.wait_ge(pool.sem, i * 4 + (pool.base + u + 1))
                                hold(g)
                                gathers(g, index[:, b, 0, :], xg[b], filled[b].sem, table_hh)
                                gathers(g, index[:, b, 1, :], qg[b], filled[b].sem, table_q)

                    @block.sync
                    def _(sp):
                        def load(g, b, used):
                            sp.wait_ge(left[b].sem, used)
                            sp.dma_start(wg[b][:, :, :], edges(edge_net)[:, bass.ds(g * G, G), :]).then_inc(inputs[b].sem, 16)
                            sp.dma_start(sh[b][:, :, :], sh_parts.rearrange("k s t c -> (k s) t c")[:, bass.ds(g * G, G), :]).then_inc(inputs[b].sem, 16)

                        def store(g, b, ready):
                            sp.wait_ge(tails[b].sem, ready)
                            sp.dma_start(edges(record144)[:, bass.ds(g * T2, T2), :], rec[b][:, :, :]).then_inc(kept[b].sem, 16)

                        def ahead(i, b, more):
                            for u in range(2 * more):
                                load(i * 4 + (2 * b + 2 + u), u, i * 2 + (b + 2))
                            store(i * 2 + b, 1 - b, i + 2)

                        start_count(sp, kept)
                        load(0, 0, 1)
                        load(1, 1, 1)
                        with sp.Fori(0, PAIRS2 - 1) as i:
                            ahead(i, 0, 1)
                            ahead(i, 1, 1)
                        ahead(PAIRS2 - 1, 0, 1)
                        ahead(PAIRS2 - 1, 1, 0)
                        store(2 * PAIRS2, 1, PAIRS2 + 2)
                        sp.wait_ge(kept[0].sem, 16 * (PAIRS2 + 1))
                        sp.wait_ge(kept[1].sem, 16 * (PAIRS2 + 2))

                    @block.tensor
                    def _(pe):
                        for k in range(3):
                            for bk, sem in ((0, turned), (6, products)):
                                nc.tensor.matmul(bank[bk][:, 0:P], ident[:, :], ident[:, :], start=True, stop=True).then_inc(sem.sem, 1)
                        pe.wait_ge(pool.sem, pool.base)

                        def turn(i, c):
                            u, t = c // G, c % G
                            b, w = u % 2, wide[c % 2]
                            if t == 0:
                                pe.wait_ge(filled[b].sem, i * (64 * G) + 32 * G * (u // 2 + 1))
                                pe.wait_ge(inputs[b].sem, i * 64 + 32 * (u // 2 + 1))
                            pe.wait_ge(z_ready.sem, done(i, c - 2))
                            for k in range(K5):
                                nc.tensor.matmul(w[:, k * P:(k + 1) * P], pick[:, k, :, :].rearrange("r a d -> r (a d)"), sh[b][:, t, :], start=True, stop=True)
                            nc.tensor.transpose(w[:, K5 * P:(K5 + 1) * P], xg[b][:, t, :], ident[:, :]).then_inc(turned.sem, 1)

                        with pe.Fori(0, PAIRS2) as i:
                            for c in range(C):
                                b, t, q = (c // G) % 2, c % G, c % 2
                                if c == 0:
                                    turn(i, 0)
                                if c + 1 < C:
                                    turn(i, c + 1)
                                pe.wait_ge(z_ready.sem, done(i, c))
                                pe.wait_ge(joined.sem, done(i, c - 2))
                                for k in range(K5):
                                    last = nc.tensor.matmul(bank[6 + q][:, 0:2 * O], zt[q][:, k, :], c_w[:, k, :], start=k == 0, stop=k == K5 - 1)
                                last.then_inc(products.sem, 1)

                    @block.scalar
                    def _(s):
                        for k in range(3):
                            s.activation(primed[:, k:k + 1], holder[:, 0:1], ACT.Copy).then_inc(xt_ready.sem, 1)

                        def keep_xt(i, c):
                            s.wait_ge(turned.sem, done(i, c))
                            s.wait_ge(z_ready.sem, done(i, c - 2))
                            s.activation(xt[c % 2][:, :], wide[c % 2][:, K5 * P:(K5 + 1) * P], ACT.Copy).then_inc(xt_ready.sem, 1)

                        with s.Fori(0, PAIRS2) as i:
                            for c in range(C):
                                b, t, q = c // T2, c % T2, c % 2
                                if c == 0:
                                    keep_xt(i, 0)
                                if c + 1 < C:
                                    keep_xt(i, c + 1)
                                if t == 2:
                                    s.wait_ge(tail_v.sem, i * 8 + (4 * b + 3))
                                    s.activation(fall[:, :, :], fall[:, :, :], ACT.Exp)
                                    s.activation(logit[1 - b][:, :, :], logit[1 - b][:, :, :], ACT.Exp).then_inc(tail_a.sem, 1)
                        s.wait_ge(tail_v.sem, 4 * 2 * PAIRS2 + 3)
                        s.activation(fall[:, :, :], fall[:, :, :], ACT.Exp)
                        s.activation(logit[1][:, :, :], logit[1][:, :, :], ACT.Exp).then_inc(tail_a.sem, 1)

                    @block.vector
                    def _(v):
                        v.memset(vv[1][:, :, :], 0.0)
                        v.memset(logit[1][:, :, :], 0.0)
                        v.memset(neg_t[1][:, :], 0.0)
                        v.memset(rec[0][:, T2 - 1, :], 0.0).then_inc(tails[0].sem, 1)
                        v.memset(rec[1][:, T2 - 1, :], 0.0).then_inc(tails[1].sem, 1)
                        v.memset(c_w[D:P, 4, :], 0.0)
                        for k in range(3):
                            v.memset(primed[:, 16 + k:17 + k], 0.0).then_inc(z_ready.sem, 1)
                            v.memset(primed[:, 20 + k:21 + k], 0.0).then_inc(joined.sem, 1)
                        for b in range(2):
                            v.memset(primed[:, 24 + b:25 + b], 0.0).then_inc(left[b].sem, 1)

                        def outer(i, c):
                            v.wait_ge(xt_ready.sem, done(i, c))
                            v.wait_ge(products.sem, done(i, c - 2))
                            v.tensor_tensor(zt[c % 2][:, :, :], wide[c % 2][:, 0:K5 * P].rearrange("p (k e) -> p k e", e=P),
                                            along(xt[c % 2][:, :], K5), ALU.mult).then_inc(z_ready.sem, 1)

                        def tail(n, pb, t, before, free, columns):
                            now, past = rec[pb], rec[1 - pb]
                            p, m_now, m_past = logit[pb], now[:, :, O:O + H], past[:, T2 - 1, O:O + H]
                            if t == 0:
                                v.wait_ge(joined.sem, columns)
                                v.wait_ge(tails[1 - pb].sem, before)
                                v.wait_ge(kept[pb].sem, free)
                                for h in range(H):
                                    last = v.tensor_tensor_scan(now[:, :, O + h], neg_t[pb][:, :], p[:, :, h], past[:, T2 - 1, O + h:O + h + 1], ALU.add, ALU.max)
                                last.then_inc(tail_v.sem, 1)
                            elif t == 1:
                                v.wait_ge(tail_v.sem, n * 4 + 1)
                                v.tensor_tensor(fall[:, 0, :], m_past, now[:, 0, O:O + H], ALU.subtract)
                                v.tensor_tensor(fall[:, 1:T2, :], now[:, 0:T2 - 1, O:O + H], now[:, 1:T2, O:O + H], ALU.subtract)
                                v.tensor_tensor(p[:, :, :], p[:, :, :], m_now, ALU.subtract).then_inc(tail_v.sem, 1)
                                v.wait_ge(tail_v.sem, n * 4 + 2)
                                v.tensor_tensor(fall[:, :, :], fall[:, :, :], over(neg_t[pb][:, :], H), ALU.add).then_inc(tail_v.sem, 1)
                            elif t == 4:
                                v.wait_ge(tail_a.sem, n + 1)
                                for h in range(H):
                                    v.tensor_tensor_scan(now[:, :, O + H + h], fall[:, :, h], p[:, :, h], past[:, T2 - 1, O + H + h:O + H + h + 1], ALU.mult, ALU.add)
                            elif 5 <= t < 9:
                                t0 = (t - 5) * (T2 // 4)
                                part = vv[pb][:, t0:t0 + T2 // 4, :].rearrange("p t (h d) -> p t h d", d=DH)
                                pr = p[:, t0:t0 + T2 // 4, :]
                                last = v.tensor_tensor(part, part, pr.unsqueeze(3).to_broadcast([P, T2 // 4, H, DH]), ALU.mult)
                                if t == 8:
                                    last.then_inc(tail_v.sem, 1)
                            elif t >= 10:
                                if t == 10:
                                    v.wait_ge(tail_v.sem, n * 4 + 4)
                                slots = T2 - 10
                                for o in range((t - 10) * O // slots, (t - 9) * O // slots):
                                    last = v.tensor_tensor_scan(now[:, :, o], fall[:, :, o // DH], vv[pb][:, :, o], past[:, T2 - 1, o:o + 1], ALU.mult, ALU.add)
                                if t == T2 - 1:
                                    last.then_inc(tails[pb].sem, 1)

                        with v.Fori(0, PAIRS2) as i:
                            for c in range(C):
                                b, t, q = c // T2, c % T2, c % 2
                                if c == 0:
                                    outer(i, 0)
                                if c + 1 < C:
                                    outer(i, c + 1)
                                tail(i * 2 + b, 1 - b, t, i + (b + 1), i * 16 + 16, i * C + (b * T2 + 3))
                                if t == 0:
                                    v.tensor_copy(neg_t[b][:, :], neg[:, bass.ds((i * 2 + b) * T2, T2)])
                                v.wait_ge(products.sem, done(i, c))
                                u, w = (c // G) % 2, wg[(c // G) % 2][:, c % G, :]
                                v.tensor_tensor(kk[q][:, :], bank[6 + q][:, 0:O], w[:, 0:O], ALU.mult).then_inc(chain_v.sem, 1)
                                v.wait_ge(chain_v.sem, i * (2 * C) + (2 * c + 1))
                                v.tensor_tensor(kk[q][:, :], kk[q][:, :], qg[u][:, c % G, :], ALU.mult).then_inc(chain_v.sem, 1)
                                last = v.tensor_tensor(vv[b][:, t, :], bank[6 + q][:, O:2 * O], w[:, O:2 * O], ALU.mult)
                                if c % G == G - 1:
                                    last.then_inc(left[(c // G) % 2].sem, 1)
                                v.wait_ge(chain_v.sem, i * (2 * C) + (2 * c + 2))
                                v.tensor_reduce(logit[b][:, t, :], kk[q][:, :].rearrange("p (h d) -> p h d", d=DH), X, ALU.add).then_inc(joined.sem, 1)
                        for t in range(T2):
                            tail(2 * PAIRS2, 1, t, PAIRS2 + 1, 16 * (PAIRS2 + 1), PAIRS2 * C + 3)
                pool.base += 4 * PAIRS2

        def join_softmax(u1, m1, s1, u2, m2, s2, heads, width, own=None):
            parts = [(u1, m1, s1), (u2, m2, s2)] + ([own] if own is not None else [])
            with ExitStack() as st:
                top = sb(st, "top", [P, NT, heads])
                with nc.Block() as block:
                    @block.vector
                    def _(v):
                        step(v, v.tensor_tensor(m2, m2, over(nocarry[:, :], heads), ALU.add), vec, 1)
                        step(v, v.tensor_scalar(top[:, :, :], over(has[:, :], heads), 0.0, NEG, ALU.is_equal, ALU.mult), vec, 2)
                        step(v, v.tensor_tensor(m1, m1, over(has[:, :], heads), ALU.mult), vec, 3)
                        step(v, v.tensor_tensor(m1, m1, top[:, :, :], ALU.add), vec, 4)
                        step(v, v.tensor_tensor(top[:, :, :], m1, m2, ALU.max), vec, 5)
                        if own is None:
                            step(v, v.tensor_copy(top[:, :, :], top[:, :, :]), vec, 6)
                        else:
                            step(v, v.tensor_tensor(top[:, :, :], top[:, :, :], own[1], ALU.max), vec, 6)
                        for _, m, _ in parts:
                            last = v.tensor_tensor(m, m, top[:, :, :], ALU.subtract)
                        last.then_inc(vec.sem, 1)
                        v.wait_ge(act.sem, act.base + 1)
                        for u, m, s in parts:
                            v.tensor_tensor(s, s, m, ALU.mult)
                            uh = u.rearrange("p j (h d) -> p j h d", d=width)
                            last = v.tensor_tensor(uh, uh, m.unsqueeze(3).to_broadcast([P, NT, heads, width]), ALU.mult)
                        step(v, last, vec, 8)
                        for n, (u, _, s) in enumerate(parts[1:]):
                            v.tensor_tensor(s1, s1, s, ALU.add)
                            step(v, v.tensor_tensor(u1, u1, u, ALU.add), vec, 9 + n)

                    @block.scalar
                    def _(s):
                        s.wait_ge(vec.sem, vec.base + 7)
                        for _, m, _ in parts:
                            last = s.activation(m, m, ACT.Exp)
                        last.then_inc(act.sem, 1)
                vec.base += 7 + len(parts)
                act.base += 1

        def divide_softmax(u, s, m, heads, width):
            with nc.Block() as block:
                @block.vector
                def _(v):
                    step(v, v.tensor_scalar(s, s, 1e-16, None, ALU.add), vec, 1)
                    step(v, v.reciprocal(m, s), vec, 2)
                    uh = u.rearrange("p j (h d) -> p j h d", d=width)
                    v.tensor_tensor(uh, uh, m.unsqueeze(3).to_broadcast([P, NT, heads, width]), ALU.mult)
            vec.base += 2

        def attention_layer():
            W = O + 2 * H
            with ExitStack() as s2:
                tmp = sb(s2, "tmp", [P, NT, D])
                stat = sb(s2, "stat", [P, 2, NT])
                wq = sb(s2, "wq", [D, O])
                q = sb(s2, "q_nodes", [P, NT, O])
                load_weights([(wq[:, :], a["L2_gnn_Wq"])])
                layer_norm_relu(h_sb, x_sb[:, :, :], tmp[:, :, :], stat)
                linear(q[:, :, :], h_sb, wq[:, :], D, O)
                store_nodes([(table_hh[:, 0:D], h_sb), (table_hh[:, D:2 * D], h_sb), (table_q, q[:, :, :])])
            with ExitStack() as s1:
                last_rec = sb(s1, "last_rec", [P, W])
                with ExitStack() as s2:
                    rec = [sb(s2, f"rec{b}", [P, T2, W]) for b in range(2)]
                    edges_attention(rec)
                    with nc.Block() as block:
                        @block.vector
                        def _(v):
                            v.tensor_copy(last_rec[:, :], rec[1][:, T2 - 1, :])
                upd = sb(s1, "collected", [P, NT, W])
                with ExitStack() as s2:
                    tail_m = sb(s2, "tail_m", [P, O])
                    tail_s = sb(s2, "tail_s", [P, O])
                    chain = sb(s2, "chain", [P, W])
                    carried = sb(s2, "carried", [P, NT, W])
                    with nc.Block() as block:
                        @block.vector
                        def _(v):
                            v.tensor_copy(tail_m[:, :].rearrange("p (h d) -> p h d", d=DH), over(last_rec[:, O:O + H], DH))
                            v.tensor_copy(tail_s[:, :].rearrange("p (h d) -> p h d", d=DH), over(last_rec[:, O + H:W], DH))
                    collect(O, tail_m[:, :], [last_rec[:, 0:O], tail_s[:, :]],
                            [(0, O, 1, O), (O, 0, DH, H), (O + H, 2 * O, DH, H)], chain, carried, upd, record144, last144_i)
                    join_softmax(upd[:, :, 0:O], upd[:, :, O:O + H], upd[:, :, O + H:W],
                                 carried[:, :, 0:O], carried[:, :, O:O + H], carried[:, :, O + H:W], H, DH)
                divide_softmax(upd[:, :, 0:O], upd[:, :, O + H:W], upd[:, :, O:O + H], H, DH)
                w_out = sb(s1, "w_out", [O, D])
                w_self = sb(s1, "w_self", [D, D])
                vecs = sb(s1, "vecs", [P, 2, D])
                total = sb(s1, "total", [P, NT, D])
                tmp = sb(s1, "tmp", [P, NT, D])
                load_weights([(w_out[:, :], a["L2_gnn_W_out"]), (w_self[:, :], a["L2_gnn_W_self"]),
                              (vecs[:, 0, :], spread(a["L2_gnn_gamma"])), (vecs[:, 1, :], spread(a["L2_gnn_beta"]))])
                linear(tmp[:, :, :], upd[:, :, 0:O], w_out[:, :], O, D)
                linear(total[:, :, :], h_sb, w_self[:, :], D, D, add_to=tmp[:, :, :])
                batch_norm(agg, total[:, :, :], tmp[:, :, :], vecs[:, 0, :], vecs[:, 1, :], False)
                with nc.Block() as block:
                    @block.vector
                    def _(v):
                        v.tensor_tensor(x_sb[:, :, :], x_sb[:, :, :], agg, ALU.add)

        def spread_by_dst(ade, alpha_d):
            with ExitStack() as st:
                cont = sb(st, "cont", [P, CHUNK])
                firsts = sb(st, "firsts", [P, CHUNK])
                chunk_row = sb(st, "chunk_row", [P, D + 2])
                with nc.Block() as block:
                    @block.gpsimd
                    def _(g):
                        for j in range(NT):
                            nc.gpsimd.indirect_dma_start(by_first, bass.IndirectOffsetOnAxis(ap=first_i[:, j:j + 1], axis=0),
                                                         alpha_d[:, j:j + 1], None).then_inc(rows.sem, 16)
                        nc.gpsimd.indirect_dma_start(chunk_row[:, :], None, table_a,
                                                     bass.IndirectOffsetOnAxis(ap=chunk_dst[:, 0:1], axis=0)).then_inc(chunk_rows.sem, 16)
                        g.wait_ge(chunk_rows.sem, chunk_rows.base + 16)

                    @block.sync
                    def _(sp):
                        sp.wait_ge(rows.sem, rows.base + 16 * NT)
                        sp.dma_start(firsts[:, :], by_first[0:EP, :].rearrange("(c t) o -> c (t o)", c=P)).then_inc(loaded.sem, 16)

                    @block.vector
                    def _(v):
                        v.tensor_scalar(cont[:, :], neg[:, :], 0.0, None, ALU.is_equal).then_inc(vec.sem, 1)
                        v.wait_ge(chunk_rows.sem, chunk_rows.base + 16)
                        v.wait_ge(loaded.sem, loaded.base + 16)
                        v.tensor_copy(firsts[:, 0:1], chunk_row[:, D + 1:D + 2]).then_inc(vec.sem, 1)
                        v.wait_ge(vec.sem, vec.base + 2)
                        v.tensor_tensor_scan(ade[:, :], cont[:, :], firsts[:, :], 0.0, ALU.mult, ALU.add)
                vec.base += 2
                rows.base += 16 * NT
                loaded.base += 16
                chunk_rows.base += 16

        def edges_graph(tag, rec, ade):
            with ExitStack() as st:
                got = [sb(st, f"got{b}", [P, T, D + 2]) for b in range(2)]
                index = sb(st, "index", [P, 2, T], I32)
                neg_t = sb(st, "neg_t", [P, T])
                p = sb(st, "p", [P, T])
                raw = sb(st, "raw", [P, T])
                fall = sb(st, "fall", [P, T])
                M, Z = D, D + 1
                filled = [signal(f"{tag}_rows_here{b}") for b in range(2)]
                done = [signal(f"{tag}_record_ready{b}") for b in range(2)]
                kept = [signal(f"{tag}_record_stored{b}") for b in range(2)]
                with nc.Block() as block:
                    @block.gpsimd
                    def _(g):
                        with g.Fori(0, PAIRS) as i:
                            for b in range(2):
                                g.wait_ge(done[b].sem, i + 1)
                                g.tensor_copy(index[:, b, :], src_i[:, bass.ds((i * 2 + b) * T, T)]).then_inc(pool.sem, 1)
                                g.wait_ge(pool.sem, pool.base + 2 * i + b + 1)
                                hold(g)
                                gathers(g, index[:, b, :], got[b], filled[b].sem, table_a)

                    @block.vector
                    def _(v):
                        v.memset(rec[1][:, T - 1, 0:D], 0.0).then_inc(done[0].sem, 1)
                        v.memset(rec[1][:, T - 1, D:D + 2], 0.0).then_inc(done[1].sem, 1)
                        with v.Fori(0, PAIRS) as i:
                            for b in range(2):
                                now, past = rec[b], rec[1 - b]

                                def link(k, ins):
                                    ins.then_inc(vec.sem, 1)
                                    v.wait_ge(vec.sem, i * 14 + (vec.base + 7 * b + k))

                                v.wait_ge(done[1 - b].sem, i + b + 1)
                                v.tensor_copy(neg_t[:, :], neg[:, bass.ds((i * 2 + b) * T, T)])
                                v.wait_ge(filled[b].sem, 16 * T * (i + 1))
                                link(1, v.tensor_tensor(raw[:, :], got[b][:, :, D], ade[:, bass.ds((i * 2 + b) * T, T)], ALU.add))
                                link(2, v.scalar_tensor_tensor(p[:, :], raw[:, :], 0.2, raw[:, :], ALU.mult, ALU.max))
                                v.wait_ge(kept[b].sem, 16 * i + 16)
                                link(3, v.tensor_tensor_scan(now[:, :, M], neg_t[:, :], p[:, :], past[:, T - 1, M:M + 1], ALU.add, ALU.max))
                                v.tensor_tensor(fall[:, 0:1], past[:, T - 1, M:M + 1], now[:, 0, M:M + 1], ALU.subtract)
                                v.tensor_tensor(fall[:, 1:T], now[:, 0:T - 1, M], now[:, 1:T, M], ALU.subtract)
                                link(4, v.tensor_tensor(p[:, :], p[:, :], now[:, :, M], ALU.subtract))
                                link(5, v.tensor_tensor(fall[:, :], fall[:, :], neg_t[:, :], ALU.add))
                                v.wait_ge(act.sem, act.base + 2 * i + b + 1)
                                link(6, v.tensor_tensor(got[b][:, :, 0:D], got[b][:, :, 0:D], over(p[:, :], D), ALU.mult))
                                link(7, v.tensor_tensor_scan(now[:, :, Z], fall[:, :], p[:, :], past[:, T - 1, Z:Z + 1], ALU.mult, ALU.add))
                                for f in range(D):
                                    last = v.tensor_tensor_scan(now[:, :, f], fall[:, :], got[b][:, :, f], past[:, T - 1, f:f + 1], ALU.mult, ALU.add)
                                last.then_inc(done[b].sem, 1)

                    @block.scalar
                    def _(s):
                        with s.Fori(0, PAIRS) as i:
                            for b in range(2):
                                s.wait_ge(vec.sem, i * 14 + (vec.base + 7 * b + 5))
                                s.activation(fall[:, :], fall[:, :], ACT.Exp)
                                s.activation(p[:, :], p[:, :], ACT.Exp).then_inc(act.sem, 1)

                    @block.sync
                    def _(sp):
                        start_count(sp, kept)
                        with sp.Fori(0, PAIRS) as i:
                            for b in range(2):
                                sp.wait_ge(done[b].sem, i + 2)
                                sp.dma_start(edges(record66)[:, bass.ds((i * 2 + b) * T, T), :], rec[b][:, :, :]).then_inc(kept[b].sem, 16)
                        for b in range(2):
                            sp.wait_ge(kept[b].sem, 16 * PAIRS + 16)
                pool.base += 2 * PAIRS
                vec.base += 14 * PAIRS
                act.base += 2 * PAIRS

        def graph_attention_layers():
            W = D + 2
            with ExitStack() as st:
                w = sb(st, "w", [D, 3, D])
                vecs = sb(st, "vecs", [P, 9, D])
                alphas = sb(st, "alphas", [P, 3, NT])
                own = sb(st, "own", [P, NT, W])
                load_weights([(w[:, l, :], a[f"L3_gnn_W{l + 1}"]) for l in range(3)]
                             + [(vecs[:, 3 * l + n, :], spread(a[f"L3_gnn_{name}"]))
                                for l in range(3) for n, name in enumerate((f"a{l + 1}s", f"a{l + 1}d", f"b{l + 1}"))])
                with ExitStack() as s2:
                    tmp = sb(s2, "tmp", [P, NT, D])
                    stat = sb(s2, "stat", [P, 2, NT])
                    layer_norm_relu(h_sb, x_sb[:, :, :], tmp[:, :, :], stat)
                for l in range(3):
                    hw = own[:, :, 0:D]
                    linear(hw, h_sb, w[:, l, :], D, D)
                    with nc.Block() as block:
                        @block.vector
                        def _(v):
                            for n in range(2):
                                step(v, v.tensor_tensor(agg, hw, along(vecs[:, 3 * l + n, :], NT), ALU.mult), vec, 2 * n + 1)
                                step(v, v.tensor_reduce(alphas[:, n, :], agg, X, ALU.add), vec, 2 * n + 2)
                            step(v, v.tensor_tensor(alphas[:, 2, :], alphas[:, 0, :], alphas[:, 1, :], ALU.add), vec, 5)
                            v.tensor_copy(own[:, :, D], alphas[:, 0, :])
                            v.tensor_copy(own[:, :, D + 1], alphas[:, 1, :])
                    vec.base += 5
                    store_nodes([(table_a, own[:, :, :])])
                    with nc.Block() as block:
                        @block.vector
                        def _(v):
                            v.scalar_tensor_tensor(own[:, :, D], alphas[:, 2, :], 0.2, alphas[:, 2, :], ALU.mult, ALU.max)
                            v.memset(own[:, :, D + 1], 1.0)
                    with ExitStack() as s2:
                        ade = sb(s2, "ade", [P, CHUNK])
                        spread_by_dst(ade, alphas[:, 1, :])
                        rec = [sb(s2, f"rec{b}", [P, T, W]) for b in range(2)]
                        edges_graph(f"gat{l}", rec, ade)
                        collected = sb(s2, "collected", [P, NT, W])
                        carried = sb(s2, "carried", [P, NT, W])
                        chain = sb(s2, "chain", [P, W])
                        tail_m = sb(s2, "tail_m", [P, D])
                        tail_s = sb(s2, "tail_s", [P, D])
                        with nc.Block() as block:
                            @block.vector
                            def _(v):
                                v.tensor_copy(tail_m[:, :], rec[1][:, T - 1, D:D + 1].to_broadcast([P, D]))
                                v.tensor_copy(tail_s[:, :], rec[1][:, T - 1, D + 1:D + 2].to_broadcast([P, D]))
                        collect(D, tail_m[:, :], [rec[1][:, T - 1, 0:D], tail_s[:, :]],
                                [(0, D, 1, D), (D, 0, 1, 1), (D + 1, 2 * D, 1, 1)], chain, carried, collected, record66, last_i)

                        def fields(t):
                            return t[:, :, 0:D], t[:, :, D:D + 1], t[:, :, D + 1:D + 2]

                        u, m, s = fields(collected)
                        join_softmax(u, m, s, *fields(carried), 1, D, own=fields(own))
                        divide_softmax(u, s, m, 1, D)
                        with nc.Block() as block:
                            @block.vector
                            def _(v):
                                if l < 2:
                                    step(v, v.tensor_tensor(u, u, along(vecs[:, 3 * l + 2, :], NT), ALU.add), vec, 1)
                                    v.tensor_scalar(h_sb, u, 0.0, None, ALU.max)
                                else:
                                    step(v, v.tensor_tensor(u, u, along(vecs[:, 3 * l + 2, :], NT), ALU.add), vec, 1)
                                    v.tensor_tensor(x_sb[:, :, :], x_sb[:, :, :], u, ALU.add)
                        vec.base += 1

        load_and_flags()
        if 0 in LAYERS:
            logsumexp_layers()
        if 1 in LAYERS:
            weighted_sum_layer()
        if 2 in LAYERS:
            split_harmonics()
            attention_layer()
        if 3 in LAYERS:
            clear_by_first()
            graph_attention_layers()

        with nc.Block() as block:
            @block.sync
            def _(sp):
                sp.dma_start(out[0:P * (NT - 1), :].rearrange("(j p) f -> p j f", p=P), x_sb[:, 0:NT - 1, :]).then_inc(stored.sem, 16)
                sp.dma_start(out[P * (NT - 1):N, :], x_sb[0:LAST, NT - 1, :]).then_inc(stored.sem, 16)
                sp.wait_ge(stored.sem, stored.base + 32)


def kernel(**inputs):
    import numpy as np
    import concourse.bacc as bacc
    from concourse.bass_utils import run_bass_kernel_spmd as run

    def padded(v, length, value, front=0):
        r = np.full((length,) + v.shape[1:], value, v.dtype)
        r[front:front + v.shape[0]] = v
        return r

    lay = {k: np.ascontiguousarray(v) for k, v in inputs.items()}
    arrays = {
        "x": lay["x"],
        "src_pad": padded(lay["src"], EP, 0),
        "dst_ext": padded(lay["dst"], EP + 1, N, front=1),
        "edge64": padded(np.ascontiguousarray(padded(lay["edge_attr_64"], EP, 0).reshape(P, CHUNK, D).transpose(1, 2, 0)),
                         CHUNK + T, 0).transpose(1, 0, 2).copy(),
        "edge9": np.ascontiguousarray(padded(lay["edge_attr_9"], EP, 0).reshape(P, CHUNK, S).transpose(2, 1, 0)),
        "edge_weight": padded(lay["edge_weight"], EP, 0),
        "L0_gnn_W_inT": np.ascontiguousarray(lay["L0_gnn_W_in"].T),
        "L0_gnn_W_lT": np.ascontiguousarray(lay["L0_gnn_W_l"].transpose(0, 2, 1)),
    }
    for name in ("Cqk", "Cv"):
        arrays[f"L2_gnn_{name}_s"] = np.ascontiguousarray(lay[f"L2_gnn_{name}"].transpose(1, 0, 2).reshape(S * D, O))
    arrays["dst_ext"][0] = -1
    for name, v in lay.items():
        if name[:3] in ("L0_", "L1_", "L2_", "L3_") and name not in ("L0_gnn_W_in", "L0_gnn_W_l", "L2_gnn_Cqk", "L2_gnn_Cv"):
            arrays[name] = v
    nc = bacc.Bacc("TRN2", target_bir_lowering=False, num_devices=1)
    aps = {name: nc.dram_tensor(f"in_{name}", v.shape, mybir.dt.from_np(v.dtype), kind="ExternalInput").ap()
           for name, v in arrays.items()}
    out = nc.dram_tensor("out_0", (N, D), F32, kind="ExternalOutput").ap()
    build_program(nc, aps, out)
    r = run(nc, [{f"in_{name}": v for name, v in arrays.items()}], core_ids=[0])
    return r.results[0]["out_0"]
```

```python
import concourse.bass as bass
from concourse import mybir
from contextlib import ExitStack

F32 = mybir.dt.float32
I32 = mybir.dt.int32
BF16 = mybir.dt.bfloat16
ALU = mybir.AluOpType
ACT = mybir.ActivationFunctionType
X = mybir.AxisListType.X

P = 128
N, E, D = 6250, 200000, 64
NT = -(-N // P)
NP = NT * P
LAST = N - (NT - 1) * P
T = 49
PAIRS = -(-E // (P * 2 * T))
CHUNK = PAIRS * 2 * T
EP = P * CHUNK
T2 = T * 4 // 7
PAIRS2 = CHUNK // (2 * T2)
NET_COLUMNS = [(0, 13), (13, 31), (31, T)]
G = T2 // 2
S, O, H, DH = 9, 128, 8, 16
NEG = -1.0e37
SEVENTHS = [(j, min(j + 7, NT)) for j in range(0, NT, 7)]
GROUPS = [(g, min(4, NT - g)) for g in range(0, NT, 4)]


class Signal:

    def __init__(self, ctx, nc, name):
        self.sem = ctx.enter_context(nc.semaphore(name))
        self.base = 0


def build_program(nc, a, out):
    ctx = ExitStack()
    with ctx:
        used_names = {}

        def sb(stack, name, shape, dt=F32):
            used_names[name] = used_names.get(name, 0) + 1
            return stack.enter_context(nc.sbuf_tensor(f"{name}_{used_names[name]}", shape, dt))

        def dram(name, shape, dt=F32):
            return nc.dram_tensor(name, shape, dt, kind="Internal").ap()

        def signal(name):
            return Signal(ctx, nc, name)

        vec = signal("vec_done")
        act = signal("act_done")
        mm = signal("pe_done")
        mm2 = signal("pe_products_done")
        pool = signal("pool_done")
        loaded = signal("loaded")
        stored = signal("stored")
        rows = signal("firsts_scattered")
        records = [signal(f"records_gathered{k}") for k in range(len(SEVENTHS))]
        chunk_rows = signal("chunk_rows_gathered")

        wide = [ctx.enter_context(nc.psum_tensor(f"banks{k}", [P, 1024], F32)) for k in range(4)]
        net_here = signal("net_edges_here")
        net_hid = signal("net_hidden_done")
        net_relu = signal("net_hidden_ready")
        net_done = signal("net_product_done")
        net_out_ready = signal("net_out_ready")
        net_kept = signal("net_out_stored")
        hot = signal("one_hots_ready")
        digit = signal("digits_ready")
        counted = signal("one_hots_counted")

        bank = [wide[k // 2][:, 512 * (k % 2):512 * (k % 2 + 1)] for k in range(8)]

        x_sb = sb(ctx, "x_sb", [P, NT, D])
        hc = sb(ctx, "hc", [P, NT, 2 * D])
        h_sb = hc[:, :, 0:D]
        agg = hc[:, :, D:2 * D]
        ident = sb(ctx, "ident", [P, P])
        ones = sb(ctx, "ones", [P, P])
        ones_last = sb(ctx, "ones_last", [P, P])
        src_i = sb(ctx, "src_i", [P, CHUNK + 2 * T], I32)
        dst_i = sb(ctx, "dst_i", [P, CHUNK], I32)
        neg = sb(ctx, "neg", [P, CHUNK])
        negrow = sb(ctx, "negrow", [P, P])
        controw = sb(ctx, "controw", [P, P])
        has = sb(ctx, "has", [P, NT])
        nocarry = sb(ctx, "nocarry", [P, NT])
        last_i = sb(ctx, "last_i", [P, NT], I32)
        last144_i = sb(ctx, "last144_i", [P, NT], I32)
        first_i = sb(ctx, "first_i", [P, NT], I32)
        holder = sb(ctx, "holder", [P, 2])
        net_ones = sb(ctx, "net_ones", [1, P], BF16)
        primes = sb(ctx, "primes", [P, 8])
        chunk_dst = sb(ctx, "chunk_dst", [P, 1], I32)

        table = dram("table", [NP, D])
        table_hh = dram("table_hh", [NP, 2 * D])
        table_q = dram("table_q", [NP, O])
        edge_net = dram("edge_net", [EP, 2 * O])
        spare_net = dram("spare_net", [P, 1])
        sh_parts = dram("sh_parts", [3, S, CHUNK, P], BF16)
        table_a = dram("table_a", [NP, D + 2])
        record128 = dram("record128", [EP, 2 * D])
        record64 = dram("record64", [EP, D])
        record144 = dram("record144", [P * (CHUNK + T2), O + 2 * H])
        record66 = dram("record66", [EP, D + 2])
        selection = dram("selection", [P, NP])
        spare = dram("spare", [2, P, 1])
        by_first = dram("by_first", [EP + NP, 1])

        def nodes(t):
            return t.rearrange("(j p) f -> p j f", p=P)

        def edges(t):
            return t.rearrange("(c t) f -> c t f", c=P)

        def over(ap, n):
            return ap.unsqueeze(2).to_broadcast([ap.shape[0], ap.shape[1], n])

        def along(ap, n):
            return ap.unsqueeze(1).to_broadcast([ap.shape[0], n, ap.shape[1]])

        def step(eng, ins, sig, k):
            ins.then_inc(sig.sem, 1)
            eng.wait_ge(sig.sem, sig.base + k)

        def load_and_flags():
            with ExitStack() as st:
                prev_i = sb(st, "prev_i", [P, CHUNK], I32)
                dstf = sb(st, "dstf", [P, 2, CHUNK])
                anystart = sb(st, "anystart", [P, 1])
                anyrow = sb(st, "anyrow", [P, P])
                with nc.Block() as block:
                    @block.sync
                    def _(sp):
                        sp.dma_start(dst_i[:, :], a["dst_ext"][1:1 + EP].rearrange("(c t) -> c t", c=P)).then_inc(loaded.sem, 16)
                        sp.dma_start(prev_i[:, :], a["dst_ext"][0:EP].rearrange("(c t) -> c t", c=P)).then_inc(loaded.sem, 16)
                        sp.dma_start(src_i[:, 0:CHUNK], a["src_pad"].rearrange("(c t) -> c t", c=P)).then_inc(loaded.sem, 16)
                        sp.wait_ge(vec.sem, vec.base + 1)
                        sp.dma_start(x_sb[:, 0:NT - 1, :], a["x"][0:P * (NT - 1), :].rearrange("(j p) f -> p j f", p=P)).then_inc(loaded.sem, 16)
                        sp.dma_start(x_sb[0:LAST, NT - 1, :], a["x"][P * (NT - 1):N, :]).then_inc(loaded.sem, 16)

                    @block.gpsimd
                    def _(g):
                        g.memset(holder[:, :], 0.0)
                        step(g, g.memset(ident[:, :], 0.0), pool, 1)
                        step(g, g.affine_select(out=ident[:, :], in_=ident[:, :], compare_op=ALU.not_equal, fill=1.0,
                                                base=0, pattern=[[-1, P]], channel_multiplier=1), pool, 2)
                        step(g, g.memset(ones[:, :], 1.0), pool, 3)
                        g.affine_select(out=ones_last[:, :], in_=ones[:, :], compare_op=ALU.is_gt, fill=0.0,
                                        base=LAST, pattern=[[0, P]], channel_multiplier=-1).then_inc(pool.sem, 1)

                    @block.vector
                    def _(v):
                        v.memset(x_sb[:, NT - 1, :], 0.0).then_inc(vec.sem, 1)
                        v.wait_ge(loaded.sem, loaded.base + 5 * 16)
                        v.tensor_copy(dstf[:, 0, :], dst_i[:, :])
                        v.tensor_copy(chunk_dst[:, :], dst_i[:, 0:1])
                        v.tensor_copy(src_i[:, CHUNK:CHUNK + 2 * T], dst_i[:, 0:2 * T])
                        step(v, v.tensor_copy(dstf[:, 1, :], prev_i[:, :]), vec, 2)
                        step(v, v.tensor_tensor(neg[:, :], dstf[:, 0, :], dstf[:, 1, :], ALU.is_equal), vec, 3)
                        step(v, v.tensor_scalar(neg[:, :], neg[:, :], -1.0, -NEG, ALU.add, ALU.mult), vec, 4)
                        step(v, v.tensor_reduce(anystart[:, :], neg[:, :], X, ALU.min), vec, 5)
                        v.wait_ge(pool.sem, pool.base + 3)
                        v.memset(neg[:, 0:1], NEG)
                        v.tensor_scalar(anyrow[:, :], ones[:, :], anystart[:, 0:1], None, ALU.mult).then_inc(vec.sem, 1)
                        v.wait_ge(mm.sem, mm.base + 1)
                        step(v, v.tensor_copy(negrow[:, :], bank[0][:, 0:P]), vec, 7)
                        v.tensor_scalar(controw[:, :], negrow[:, :], 0.0, None, ALU.is_equal)

                    @block.tensor
                    def _(pe):
                        pe.wait_ge(vec.sem, vec.base + 6)
                        pe.wait_ge(pool.sem, pool.base + 2)
                        nc.tensor.matmul(bank[0][:, 0:P], anyrow[:, :], ident[:, :], start=True, stop=True).then_inc(mm.sem, 1)
                loaded.base += 5 * 16
                vec.base += 7
                pool.base += 4
                mm.base += 1

        def index_nodes():
            with ExitStack() as st:
                HI, LO = NT, P
                select = sb(st, "select", [P, NP])
                chan_i = sb(st, "chan_i", [P, 1], I32)
                chan_f = sb(st, "chan_f", [P, 1])
                upper = sb(st, "upper", [P, P])
                cnt = sb(st, "cnt", [HI, LO])
                cum = sb(st, "cum", [HI, LO])
                before = sb(st, "before", [HI, 1])
                node_id = sb(st, "node_id", [HI, LO])
                node_i = sb(st, "node_i", [HI, LO], I32)
                q = sb(st, "q", [HI, 8, LO])
                counts = bank[0][0:HI, 0:LO]
                with nc.Block() as block:
                    @block.sync
                    def _(sp):
                        sp.wait_ge(vec.sem, vec.base + 18 + len(GROUPS))
                        sp.dma_start(selection[:, :], select[:, :]).then_inc(stored.sem, 16)
                        sp.wait_ge(stored.sem, stored.base + 16)

                    @block.gpsimd
                    def _(g):
                        g.iota(chan_i[:, :], pattern=[[0, 1]], base=0, channel_multiplier=1)
                        g.iota(node_i[:, :], pattern=[[1, LO]], base=EP, channel_multiplier=LO)
                        g.affine_select(out=upper[:, :], in_=ones[:, :], compare_op=ALU.is_gt, fill=0.0,
                                        base=0, pattern=[[1, P]], channel_multiplier=-1).then_inc(pool.sem, 1)

                    @block.vector
                    def _(v):
                        v.wait_ge(pool.sem, pool.base + 1)
                        v.tensor_copy(chan_f[:, :], chan_i[:, :])
                        v.tensor_copy(node_id[:, :], node_i[:, :])
                        step(v, v.tensor_copy(cnt[:, :], counts), vec, 1)
                        step(v, v.tensor_tensor_scan(cum[:, :], ones[0:HI, :], cnt[:, :], 0.0, ALU.mult, ALU.add), vec, 2)
                        v.wait_ge(mm.sem, mm.base + 1)
                        step(v, v.tensor_copy(before[:, :], bank[1][0:HI, 0:1]), vec, 3)
                        step(v, v.tensor_scalar(cum[:, :], cum[:, :], before[:, 0:1], None, ALU.add), vec, 4)
                        v.tensor_scalar(q[:, 0, :], cum[:, :], -1.0, 0.0, ALU.add, ALU.max)
                        v.tensor_scalar(q[:, 2, :], cnt[:, :], 0.0, None, ALU.is_gt)
                        step(v, v.tensor_tensor(q[:, 1, :], cum[:, :], cnt[:, :], ALU.subtract), vec, 5)
                        step(v, v.tensor_scalar(q[:, 3, :], q[:, 0, :], 0.5, 1.0 / CHUNK, ALU.add, ALU.mult), vec, 6)
                        step(v, v.tensor_scalar(q[:, 3, :], q[:, 3, :], -0.5, 12582912.0, ALU.add, ALU.add), vec, 7)
                        step(v, v.tensor_scalar(q[:, 3, :], q[:, 3, :], -12582912.0, None, ALU.add), vec, 8)
                        step(v, v.scalar_tensor_tensor(q[:, 4, :], q[:, 3, :], float(CHUNK), q[:, 1, :], ALU.mult, ALU.is_gt), vec, 9)
                        step(v, v.tensor_tensor(q[:, 4, :], q[:, 4, :], q[:, 2, :], ALU.mult), vec, 10)
                        step(v, v.tensor_tensor(q[:, 5, :], q[:, 4, :], q[:, 3, :], ALU.mult), vec, 11)
                        step(v, v.tensor_scalar(q[:, 5, :], q[:, 5, :], -1.0, None, ALU.add), vec, 12)
                        step(v, v.tensor_tensor(q[:, 6, :], q[:, 1, :], node_id[:, :], ALU.subtract), vec, 13)
                        step(v, v.tensor_tensor(q[:, 6, :], q[:, 6, :], q[:, 2, :], ALU.mult), vec, 14)
                        step(v, v.tensor_tensor(q[:, 6, :], q[:, 6, :], node_id[:, :], ALU.add), vec, 15)
                        step(v, v.tensor_scalar(q[:, 7, :], q[:, 3, :], 1.0, float(T2), ALU.add, ALU.mult), vec, 16)
                        step(v, v.tensor_tensor(q[:, 7, :], q[:, 7, :], q[:, 0, :], ALU.add), vec, 17)
                        v.wait_ge(mm.sem, mm.base + 2)
                        v.tensor_copy(last144_i[:, :], bank[1][:, 4 * HI:5 * HI])
                        v.tensor_copy(last_i[:, :], bank[1][:, 0:HI])
                        v.tensor_copy(first_i[:, :], bank[1][:, HI:2 * HI])
                        v.tensor_copy(has[:, :], bank[1][:, 2 * HI:3 * HI])
                        v.tensor_scalar(nocarry[:, :], bank[1][:, 3 * HI:4 * HI], 0.0, NEG, ALU.is_lt, ALU.mult).then_inc(vec.sem, 1)
                        for n, (g0, m) in enumerate(GROUPS):
                            v.wait_ge(mm2.sem, mm2.base + n + 1)
                            v.tensor_scalar(select[:, g0 * P:(g0 + m) * P], bank[2 + n % 2][:, 0:m * P], chan_f[:, 0:1], None,
                                            ALU.is_equal).then_inc(vec.sem, 1)

                    @block.tensor
                    def _(pe):
                        pe.wait_ge(vec.sem, vec.base + 2)
                        pe.wait_ge(pool.sem, pool.base + 1)
                        nc.tensor.matmul(bank[1][0:HI, 0:1], upper[0:HI, 0:HI], cum[:, LO - 1:LO], start=True, stop=True).then_inc(mm.sem, 1)
                        pe.wait_ge(vec.sem, vec.base + 17)
                        for k, which in enumerate((0, 6, 2, 5, 7)):
                            last = nc.tensor.transpose(bank[1][:, k * HI:(k + 1) * HI], q[:, which, :], ident[0:HI, 0:HI])
                        last.then_inc(mm.sem, 1)
                        for n, (g0, m) in enumerate(GROUPS):
                            if n >= 2:
                                pe.wait_ge(vec.sem, vec.base + 18 + n - 1)
                            for j in range(m):
                                last = nc.tensor.matmul(bank[2 + n % 2][:, j * P:(j + 1) * P],
                                                        ident[0:HI, g0 + j:g0 + j + 1].to_broadcast([HI, P]),
                                                        q[:, 5, :], start=True, stop=True)
                            last.then_inc(mm2.sem, 1)
                stored.base += 16
                pool.base += 1
                vec.base += 18 + len(GROUPS)
                mm.base += 2
                mm2.base += len(GROUPS)

        def clear_by_first():
            with ExitStack() as st:
                z = sb(st, "z", [P, CHUNK + NT])
                with nc.Block() as block:
                    @block.vector
                    def _(v):
                        v.memset(z[:, :], 0.0).then_inc(vec.sem, 1)

                    @block.sync
                    def _(sp):
                        sp.wait_ge(vec.sem, vec.base + 1)
                        sp.dma_start(by_first.rearrange("(p f) o -> p (f o)", p=P), z[:, :]).then_inc(stored.sem, 16)
                        sp.wait_ge(stored.sem, stored.base + 16)
                vec.base += 1
                stored.base += 16

        def load_weights(parts):
            with nc.Block() as block:
                @block.sync
                def _(sp):
                    for tile, source in parts:
                        sp.dma_start(tile, source).then_inc(loaded.sem, 16)
                    sp.wait_ge(loaded.sem, loaded.base + 16 * len(parts))
            loaded.base += 16 * len(parts)

        def spread(vector_ap):
            return vector_ap.unsqueeze(0).to_broadcast([P, vector_ap.shape[0]])

        def store_nodes(pairs):
            with nc.Block() as block:
                @block.sync
                def _(sp):
                    for t, tile in pairs:
                        sp.dma_start(nodes(t), tile).then_inc(stored.sem, 16)
                    sp.wait_ge(stored.sem, stored.base + 16 * len(pairs))
            stored.base += 16 * len(pairs)

        def layer_norm_relu(dst, src, tmp, stat, gamma=None, beta=None, blend=None, add_to=None):
            affine = gamma is not None
            with nc.Block() as block:
                @block.vector
                def _(v):
                    step(v, v.tensor_reduce(stat[:, 0, :], src, X, ALU.add), vec, 1)
                    step(v, v.tensor_scalar(stat[:, 0, :], stat[:, 0, :], 1.0 / D, None, ALU.mult), vec, 2)
                    step(v, v.tensor_tensor(tmp, src, over(stat[:, 0, :], D), ALU.subtract), vec, 3)
                    step(v, v.tensor_tensor(dst, tmp, tmp, ALU.mult), vec, 4)
                    step(v, v.tensor_reduce(stat[:, 1, :], dst, X, ALU.add), vec, 5)
                    v.tensor_scalar(stat[:, 1, :], stat[:, 1, :], 1.0 / D, 1e-5, ALU.mult, ALU.add).then_inc(vec.sem, 1)
                    v.wait_ge(act.sem, act.base + 1)
                    step(v, v.reciprocal(stat[:, 1, :], stat[:, 0, :]), vec, 7)
                    step(v, v.tensor_tensor(tmp, tmp, over(stat[:, 1, :], D), ALU.mult), vec, 8)
                    if affine:
                        step(v, v.tensor_tensor(tmp, tmp, along(gamma[:, :], NT), ALU.mult), vec, 9)
                        step(v, v.tensor_tensor(tmp, tmp, along(beta[:, :], NT), ALU.add), vec, 10)
                    if blend is None:
                        v.tensor_scalar(dst, tmp, 0.0, None, ALU.max)
                    else:
                        step(v, v.scalar_tensor_tensor(tmp, tmp, 0.0, blend, ALU.max, ALU.add), vec, 11)
                        step(v, v.tensor_scalar(blend, tmp, 0.5, None, ALU.mult), vec, 12)
                        if add_to is not None:
                            v.tensor_tensor(add_to, add_to, blend, ALU.add)

                @block.scalar
                def _(s):
                    s.wait_ge(vec.sem, vec.base + 6)
                    s.activation(stat[:, 0, :], stat[:, 1, :], ACT.Sqrt).then_inc(act.sem, 1)
            vec.base += (10 if affine else 8) + (2 if blend is not None else 0)
            act.base += 1

        def linear(dst, src, weight, K, M, bias=None, add_to=None):
            with ExitStack() as st:
                turned = sb(st, "turned", [P, 2, 512])
                t_ready = [bank[0], bank[1]]
                products = [bank[2], bank[3]]
                with nc.Block() as block:
                    @block.tensor
                    def _(pe):
                        for n in range(len(GROUPS) + 1):
                            if n < len(GROUPS):
                                g0, m = GROUPS[n]
                                if n >= 2:
                                    pe.wait_ge(act.sem, act.base + n - 1)
                                for j in range(m):
                                    last = nc.tensor.transpose(t_ready[n % 2][0:K, j * P:(j + 1) * P], src[:, g0 + j, :], ident[:, :])
                                last.then_inc(mm.sem, 1)
                            if n >= 1:
                                k = n - 1
                                g0, m = GROUPS[k]
                                pe.wait_ge(act.sem, act.base + k + 1)
                                if k >= 2:
                                    pe.wait_ge(vec.sem, vec.base + k - 1)
                                for j in range(m):
                                    last = nc.tensor.matmul(products[k % 2][:, j * M:(j + 1) * M], turned[0:K, k % 2, j * P:(j + 1) * P],
                                                            weight, start=True, stop=True)
                                last.then_inc(mm2.sem, 1)

                    @block.scalar
                    def _(s):
                        for n, (g0, m) in enumerate(GROUPS):
                            s.wait_ge(mm.sem, mm.base + n + 1)
                            if n >= 2:
                                s.wait_ge(mm2.sem, mm2.base + n - 1)
                            s.activation(turned[0:K, n % 2, 0:m * P], t_ready[n % 2][0:K, 0:m * P], ACT.Copy).then_inc(act.sem, 1)

                    @block.vector
                    def _(v):
                        for n, (g0, m) in enumerate(GROUPS):
                            v.wait_ge(mm2.sem, mm2.base + n + 1)
                            got = products[n % 2][:, 0:m * M].rearrange("p (j f) -> p j f", f=M)
                            if bias is not None:
                                v.tensor_tensor(dst[:, g0:g0 + m, :], got, along(bias, m), ALU.add).then_inc(vec.sem, 1)
                            elif add_to is not None:
                                v.tensor_tensor(dst[:, g0:g0 + m, :], got, add_to[:, g0:g0 + m, :], ALU.add).then_inc(vec.sem, 1)
                            else:
                                v.tensor_copy(dst[:, g0:g0 + m, :], got).then_inc(vec.sem, 1)
                n = len(GROUPS)
                mm.base += n
                mm2.base += n
                act.base += n
                vec.base += n

        def collect(width, tail_max, tail_sums, pieces, chain, carried, collected, record, at_last, join):
            vec_steps, act_steps, join_vector, join_scalar = join
            k = len(tail_sums)
            online = tail_max is not None
            length = sum(p[3] for p in pieces)
            with ExitStack() as st:
                run = sb(st, "run", [width, k + 1, P])
                decay = sb(st, "decay", [width, P])
                weight = sb(st, "weight", [width, P])
                term = sb(st, "term", [width, k, P])
                select = sb(st, "select", [P, NP])
                with nc.Block() as block:
                    @block.sync
                    def _(sp):
                        sp.dma_start(select[:, :], selection[:, :]).then_inc(loaded.sem, 16)

                    @block.gpsimd
                    def _(g):
                        for j in range(NT):
                            nc.gpsimd.indirect_dma_start(collected[:, j, :], None, record,
                                                         bass.IndirectOffsetOnAxis(ap=at_last[:, j:j + 1], axis=0)).then_inc(records[j // 7].sem, 16)
                        for k, (j0, j1) in enumerate(SEVENTHS):
                            g.wait_ge(records[k].sem, records[k].base + 16 * (j1 - j0))

                    @block.tensor
                    def _(pe):
                        if online:
                            nc.tensor.transpose(bank[0][0:width, 0:P], tail_max, ident[:, :])
                        for n in range(k):
                            last = nc.tensor.transpose(bank[0][0:width, (n + 1) * P:(n + 2) * P], tail_sums[n], ident[:, :])
                        last.then_inc(mm.sem, 1)
                        pe.wait_ge(vec.sem, vec.base + (5 if online else 2))
                        for n in range(0 if online else 1, k + 1):
                            at = (n if online else n - 1) * width
                            last = nc.tensor.transpose(bank[1][:, at:at + width], run[:, n, :], ident[0:width, 0:width])
                        last.then_inc(mm.sem, 1)
                        pe.wait_ge(vec.sem, vec.base + (6 if online else 3))
                        pe.wait_ge(loaded.sem, loaded.base + 16)
                        for j in range(NT):
                            if j >= 4:
                                pe.wait_ge(act.sem, act.base + (1 if online else 0) + j - 3)
                            nc.tensor.matmul(bank[2 + j % 4][:, 0:length], select[:, j * P:(j + 1) * P], chain[:, 0:length],
                                             start=True, stop=True).then_inc(mm2.sem, 1)

                    @block.vector
                    def _(v):
                        v.wait_ge(mm.sem, mm.base + 1)
                        if online:
                            v.memset(decay[:, 0:1], NEG)
                            step(v, v.tensor_tensor_scan(run[:, 0, :], negrow[0:width, :], bank[0][0:width, 0:P], NEG, ALU.add, ALU.max), vec, 1)
                            v.tensor_tensor(decay[:, 1:P], run[:, 0, 0:P - 1], run[:, 0, 1:P], ALU.subtract)
                            step(v, v.tensor_tensor(weight[:, :], bank[0][0:width, 0:P], run[:, 0, :], ALU.subtract), vec, 2)
                            v.tensor_tensor(decay[:, :], decay[:, :], negrow[0:width, :], ALU.add).then_inc(vec.sem, 1)
                            v.wait_ge(act.sem, act.base + 1)
                            step(v, v.tensor_tensor(term[:, :, :], bank[0][0:width, P:(k + 1) * P].rearrange("p (n c) -> p n c", c=P),
                                                    along(weight[:, :], k), ALU.mult), vec, 4)
                            for n in range(k):
                                last = v.tensor_tensor_scan(run[:, n + 1, :], decay[:, :], term[:, n, :], 0.0, ALU.mult, ALU.add)
                            last.then_inc(vec.sem, 1)
                        else:
                            step(v, v.tensor_copy(term[:, 0, :], bank[0][0:width, P:2 * P]), vec, 1)
                            v.tensor_tensor_scan(run[:, 1, :], controw[0:width, :], term[:, 0, :], 0.0, ALU.mult, ALU.add).then_inc(vec.sem, 1)
                        v.wait_ge(mm.sem, mm.base + 2)
                        for to, first, every, count in pieces:
                            last = v.tensor_copy(chain[:, to:to + count], bank[1][:, first:first + (count - 1) * every + 1:every])
                        last.then_inc(vec.sem, 1)
                        for n, (j0, j1) in enumerate(SEVENTHS):
                            v.wait_ge(records[n].sem, records[n].base + 16 * (j1 - j0))
                            v.wait_ge(act.sem, act.base + online + j1)
                            join_vector(v, slice(j0, j1), (6 if online else 3) + n * vec_steps, online + NT + n * act_steps)

                    @block.scalar
                    def _(s):
                        if online:
                            s.wait_ge(vec.sem, vec.base + 3)
                            s.activation(decay[:, :], decay[:, :], ACT.Exp)
                            s.activation(weight[:, :], weight[:, :], ACT.Exp).then_inc(act.sem, 1)
                        for j in range(NT):
                            s.wait_ge(mm2.sem, mm2.base + j + 1)
                            s.activation(carried[:, j, :], bank[2 + j % 4][:, 0:length], ACT.Copy).then_inc(act.sem, 1)
                        if join_scalar is not None:
                            for n, (j0, j1) in enumerate(SEVENTHS):
                                join_scalar(s, slice(j0, j1), (6 if online else 3) + n * vec_steps)
                mm.base += 2
                mm2.base += NT
                vec.base += (6 if online else 3) + len(SEVENTHS) * vec_steps
                act.base += NT + online + len(SEVENTHS) * act_steps
                loaded.base += 16
                for k, (j0, j1) in enumerate(SEVENTHS):
                    records[k].base += 16 * (j1 - j0)

        def start_count(sp, kept):
            for b in range(2):
                sp.dma_start(spare[b], holder[:, 0:1]).then_inc(kept[b].sem, 16)

        def hold(g):
            return g.tensor_tensor(holder[:, 1:2], holder[:, 0:1], holder[:, 0:1], ALU.add)

        def next_index(v, index, i, b):
            v.tensor_copy(index, src_i[:, bass.ds((i * 2 + b + 2) * T, T)])

        def gathers(g, index, where, filled, source):
            for t in range(where.shape[1]):
                nc.gpsimd.indirect_dma_start(where[:, t, :], None, source,
                                             bass.IndirectOffsetOnAxis(ap=index[:, t:t + 1], axis=0)).then_inc(filled, 16)

        def edges_logsumexp(l, rec, net):
            tag = f"lse{l}"
            c0, c1 = NET_COLUMNS[l]
            n_net = c1 - c0
            w1, w2, b1, b2 = net
            HI, LO = NT, P
            counts = bank[0][0:HI, 0:LO]
            n_cols = 2 * PAIRS * n_net
            with ExitStack() as st:
                ea = sb(st, "ea", [D, n_net, P])
                hid = [sb(st, f"hid{k}", [P, P]) for k in range(2)]
                net_out = sb(st, "net_out", [P, n_net, 2 * O])
                if l == 0:
                    iota_i = sb(st, "iota_i", [P, P], I32)
                    iota_f = sb(st, "iota_f", [P, P])
                    digits_i = sb(st, "digits_i", [P, 2, T], I32)
                    digits = sb(st, "digits", [P, 2, T])
                    hot_hi = sb(st, "hot_hi", [P, T, HI], BF16)
                    hot_lo = sb(st, "hot_lo", [P, T, LO], BF16)
                    zero = sb(st, "zero", [P, P], BF16)
                got = [sb(st, f"got{b}", [P, T, D]) for b in range(2)]
                fall = sb(st, "fall", [P, T, D])
                index = sb(st, "index", [P, 2, T], I32)
                neg_t = sb(st, "neg_t", [P, T])
                filled = [signal(f"{tag}_rows_here{b}") for b in range(2)]
                done = [signal(f"{tag}_record_ready{b}") for b in range(2)]
                kept = [signal(f"{tag}_record_stored{b}") for b in range(2)]

                def column(i, b, c):
                    return i * (2 * n_net) + (b * n_net + c + 4)

                with nc.Block() as block:
                    @block.gpsimd
                    def _(g):
                        if l == 0:
                            step(g, g.iota(iota_i[:, :], pattern=[[1, P]], base=0, channel_multiplier=0), pool, 1)
                            pool.base += 1
                        with g.Fori(0, PAIRS) as i:
                            for b in range(2):
                                g.wait_ge(pool.sem, pool.base + 2 * i + b)
                                g.wait_ge(done[b].sem, i + 1)
                                hold(g).then_inc(pool.sem, 1)
                                gathers(g, index[:, b, :], got[b], filled[b].sem, table)

                    @block.tensor
                    def _(pe):
                        pe.wait_ge(hot.sem, hot.base + 1)
                        for k in range(3):
                            for bk, sig in ((1, net_hid), (3, net_done)):
                                nc.tensor.matmul(bank[bk][:, 0:P], ident[:, :], ident[:, :], start=True, stop=True).then_inc(sig.sem, 1)
                        if l == 0:
                            nc.tensor.matmul(counts, zero[:, 0:HI], zero[:, 0:LO], start=True, stop=False).then_inc(counted.sem, 1)

                        def hidden(i, b, c):
                            if c == 0:
                                pe.wait_ge(net_here.sem, i * 32 + (net_here.base + 16 * (b + 1)))
                            pe.wait_ge(net_relu.sem, column(i, b, c - 2) + net_relu.base)
                            nc.tensor.matmul(bank[1 + c % 2][:, 0:P], w1[:, :], ea[:, c, :], start=True, stop=True).then_inc(net_hid.sem, 1)

                        with pe.Fori(0, PAIRS) as i:
                            for b in range(2):
                                if l == 0:
                                    pe.wait_ge(hot.sem, i * 2 + (b + 2))
                                    for t in range(T):
                                        last = nc.tensor.matmul(counts, hot_hi[:, t, :], hot_lo[:, t, :], start=False, stop=False)
                                    last.then_inc(counted.sem, 1)
                                hidden(i, b, 0)
                                for c in range(n_net):
                                    if c + 1 < n_net:
                                        hidden(i, b, c + 1)
                                    pe.wait_ge(net_relu.sem, column(i, b, c) + net_relu.base)
                                    pe.wait_ge(net_out_ready.sem, column(i, b, c - 2) + net_out_ready.base)
                                    to = bank[3 + c % 2][:, 0:2 * O]
                                    for m in range(3):
                                        nc.tensor.matmul(to, net_ones[:, :], b2[:, m, :], start=m == 0, stop=False)
                                    nc.tensor.matmul(to, hid[c % 2][:, :], w2[:, :], start=False, stop=True).then_inc(net_done.sem, 1)
                        if l == 0:
                            nc.tensor.matmul(counts, zero[:, 0:HI], zero[:, 0:LO], start=False, stop=True)

                    @block.vector
                    def _(v):
                        if l == 0:
                            v.memset(zero[:, :], 0.0)
                            v.wait_ge(pool.sem, pool.base)
                            v.tensor_copy(iota_f[:, :], iota_i[:, :])
                        v.memset(fall[:, 0, 0:1], 0.0).then_inc(hot.sem, 1)
                        v.tensor_copy(index[:, :, :], src_i[:, 0:2 * T].rearrange("p (b t) -> p b t", t=T))
                        v.memset(rec[1][:, T - 1, 0:D], 0.0).then_inc(done[0].sem, 1)
                        v.memset(rec[1][:, T - 1, D:2 * D], 0.0).then_inc(done[1].sem, 1)
                        with v.Fori(0, PAIRS) as i:
                            for b in range(2):
                                now, past = rec[b], rec[1 - b]
                                at = vec.base + 8 * i + 4 * b
                                v.wait_ge(done[1 - b].sem, i + b + 1)
                                v.tensor_copy(neg_t[:, :], neg[:, bass.ds((i * 2 + b) * T, T)]).then_inc(vec.sem, 1)
                                v.wait_ge(vec.sem, at + 1)
                                if l == 0:
                                    some = dst_i[:, bass.ds((i * 2 + b) * T, T)]
                                    v.tensor_scalar(digits_i[:, 0, :], some, 7, None, ALU.logical_shift_right)
                                    v.tensor_scalar(digits_i[:, 1, :], some, P - 1, None, ALU.bitwise_and).then_inc(digit.sem, 1)
                                    v.wait_ge(digit.sem, i * 4 + (2 * b + 1))
                                    v.tensor_copy(digits[:, :, :], digits_i[:, :, :]).then_inc(digit.sem, 1)
                                    v.wait_ge(digit.sem, i * 4 + (2 * b + 2))
                                    v.wait_ge(counted.sem, i * 2 + (b + 1))
                                    v.tensor_tensor(hot_hi[:, :, :], over(digits[:, 0, :], HI), along(iota_f[:, 0:HI], T), ALU.is_equal)
                                    v.tensor_tensor(hot_lo[:, :, :], over(digits[:, 1, :], LO), along(iota_f[:, :], T), ALU.is_equal).then_inc(hot.sem, 1)
                                v.wait_ge(filled[b].sem, 16 * T * (i + 1))
                                next_index(v, index[:, b, :], i, b)
                                v.wait_ge(kept[b].sem, 16 * i + 16)
                                for f in range(D):
                                    last = v.tensor_tensor_scan(now[:, :, f], neg_t[:, :], got[b][:, :, f], past[:, T - 1, f:f + 1], ALU.add, ALU.max)
                                last.then_inc(vec.sem, 1)
                                v.wait_ge(vec.sem, at + 2)
                                v.tensor_tensor(fall[:, 0, :], past[:, T - 1, 0:D], now[:, 0, 0:D], ALU.subtract)
                                v.tensor_tensor(fall[:, 1:T, :], now[:, 0:T - 1, 0:D], now[:, 1:T, 0:D], ALU.subtract)
                                v.tensor_tensor(got[b][:, :, :], got[b][:, :, :], now[:, :, 0:D], ALU.subtract).then_inc(vec.sem, 1)
                                v.wait_ge(vec.sem, at + 3)
                                v.tensor_tensor(fall[:, :, :], fall[:, :, :], over(neg_t[:, :], D), ALU.add).then_inc(vec.sem, 1)
                                v.wait_ge(act.sem, act.base + 2 * i + b + 1)
                                for f in range(D):
                                    last = v.tensor_tensor_scan(now[:, :, D + f], fall[:, :, f], got[b][:, :, f], past[:, T - 1, D + f:D + f + 1], ALU.mult, ALU.add)
                                last.then_inc(done[b].sem, 1)

                    @block.scalar
                    def _(s):
                        for k in range(3):
                            for m, sig in enumerate((net_relu, net_out_ready)):
                                s.activation(primes[:, 2 * k + m:2 * k + m + 1], holder[:, 0:1], ACT.Copy).then_inc(sig.sem, 1)
                        s.dma_start(spare_net[:, :], holder[:, 0:1]).then_inc(net_kept.sem, 16)

                        def relu(i, b, c):
                            s.wait_ge(net_hid.sem, column(i, b, c) + net_hid.base)
                            s.wait_ge(net_done.sem, column(i, b, c - 2) + net_done.base)
                            s.activation(hid[c % 2][:, :], bank[1 + c % 2][:, 0:P], ACT.Relu, bias=b1[:, 0:1]).then_inc(net_relu.sem, 1)

                        def exponentials(i, b):
                            s.wait_ge(vec.sem, vec.base + 8 * i + 4 * b + 4)
                            s.activation(fall[:, :, :], fall[:, :, :], ACT.Exp)
                            s.activation(got[b][:, :, :], got[b][:, :, :], ACT.Exp).then_inc(act.sem, 1)

                        with s.Fori(0, PAIRS) as i:
                            for b in range(2):
                                if l == 0:
                                    exponentials(i, b)
                                relu(i, b, 0)
                                s.wait_ge(net_kept.sem, i * 32 + (net_kept.base + 16 * (b + 1)))
                                for c in range(n_net):
                                    if c + 1 < n_net:
                                        relu(i, b, c + 1)
                                    s.wait_ge(net_done.sem, column(i, b, c) + net_done.base)
                                    s.activation(net_out[:, c, :], bank[3 + c % 2][:, 0:2 * O], ACT.Copy).then_inc(net_out_ready.sem, 1)
                                s.wait_ge(net_out_ready.sem, column(i, b, n_net - 1) + net_out_ready.base)
                                s.dma_start(edges(edge_net)[:, bass.ds((i * 2 + b) * T + c0, n_net), :], net_out[:, :, :]).then_inc(net_kept.sem, 16)
                                if l > 0:
                                    exponentials(i, b)
                        s.wait_ge(net_kept.sem, net_kept.base + 16 * (2 * PAIRS + 1))

                    @block.sync
                    def _(sp):
                        start_count(sp, kept)
                        sp.dma_start(ea[:, :, :], a["edge64"][:, c0:c1, :]).then_inc(net_here.sem, 16)
                        with sp.Fori(0, PAIRS) as i:
                            for b in range(2):
                                sp.wait_ge(net_hid.sem, column(i, b, n_net - 1) + net_hid.base)
                                sp.dma_start(ea[:, :, :], a["edge64"][:, bass.ds((i * 2 + b + 1) * T + c0, n_net), :]).then_inc(net_here.sem, 16)
                                sp.wait_ge(done[b].sem, i + 2)
                                sp.dma_start(edges(record128)[:, bass.ds((i * 2 + b) * T, T), :], rec[b][:, :, :]).then_inc(kept[b].sem, 16)
                        for b in range(2):
                            sp.wait_ge(kept[b].sem, 16 * PAIRS + 16)
                        sp.wait_ge(net_here.sem, net_here.base + 16 * (2 * PAIRS + 1))
                pool.base += 2 * PAIRS
                vec.base += 8 * PAIRS
                act.base += 2 * PAIRS
                hot.base += 1 + (2 * PAIRS if l == 0 else 0)
                for sig in (net_hid, net_done, net_relu, net_out_ready):
                    sig.base += 3 + n_cols
                net_here.base += 16 * (2 * PAIRS + 1)
                net_kept.base += 16 * (2 * PAIRS + 1)

        def logsumexp_layers():
            with ExitStack() as st:
                w_in = sb(st, "w_in", [D, D])
                w1 = sb(st, "w1", [D, P])
                w2 = sb(st, "w2", [P, 2 * O])
                b1 = sb(st, "b1", [P, 1])
                b2 = sb(st, "b2", [1, 2 * O])
                b2_parts = sb(st, "b2_parts", [1, 3, 2 * O], BF16)
                w_l = sb(st, "w_l", [2 * D, 3, D])
                vecs = sb(st, "vecs", [P, 10, D])
                with nc.Block() as block:
                    @block.vector
                    def _(v):
                        v.memset(w2[:, :], 0.0)
                        v.memset(net_ones[:, :], 1.0)
                load_weights([(w1[:, 0:D], a["L2_gnn_k_w1"]), (w1[:, D:P], a["L2_gnn_v_w1"]),
                              (b1[0:D, :], a["L2_gnn_k_b1"].unsqueeze(1)), (b1[D:P, :], a["L2_gnn_v_b1"].unsqueeze(1)),
                              (b2[:, 0:O], a["L2_gnn_k_b2"].unsqueeze(0)), (b2[:, O:2 * O], a["L2_gnn_v_b2"].unsqueeze(0)),
                              (w2[0:D, 0:O], a["L2_gnn_k_w2"]), (w2[D:P, O:2 * O], a["L2_gnn_v_w2"]),
                              (w_in[:, :], a["L0_gnn_W_inT"]), (w_l[:, :, :], a["L0_gnn_W_lT"].rearrange("l k m -> k l m")),
                              (vecs[:, 0, :], spread(a["L0_gnn_b_in"]))]
                             + [(vecs[:, 1 + 3 * l + n, :], spread(a[name][l]))
                                for l in range(3) for n, name in enumerate(("L0_gnn_b_l", "L0_gnn_gamma_l", "L0_gnn_beta_l"))])
                with nc.Block() as block:
                    @block.vector
                    def _(v):
                        step(v, v.tensor_copy(b2_parts[:, 0, :], b2[:, :]), vec, 1)
                        step(v, v.tensor_tensor(b2[:, :], b2[:, :], b2_parts[:, 0, :], ALU.subtract), vec, 2)
                        step(v, v.tensor_copy(b2_parts[:, 1, :], b2[:, :]), vec, 3)
                        step(v, v.tensor_tensor(b2[:, :], b2[:, :], b2_parts[:, 1, :], ALU.subtract), vec, 4)
                        v.tensor_copy(b2_parts[:, 2, :], b2[:, :])
                vec.base += 4
                with ExitStack() as s2:
                    tmp = sb(s2, "tmp", [P, NT, D])
                    stat = sb(s2, "stat", [P, 2, NT])
                    layer_norm_relu(agg, x_sb[:, :, :], tmp[:, :, :], stat)
                    linear(h_sb, agg, w_in[:, :], D, D, bias=vecs[:, 0, :])
                for l in range(3):
                    store_nodes([(table, h_sb)])
                    with ExitStack() as s2:
                        rec = [sb(s2, f"rec{b}", [P, T, 2 * D]) for b in range(2)]
                        edges_logsumexp(l, rec, (w1, w2, b1, b2_parts))
                        if l == 0:
                            index_nodes()
                        with ExitStack() as s3:
                            tail = rec[1][:, T - 1, :]
                            collected = sb(s3, "collected", [P, NT, 2 * D])
                            carried = sb(s3, "carried", [P, NT, 2 * D])
                            chain = sb(s3, "chain", [P, 2 * D])
                            collect(D, tail[:, 0:D], [tail[:, D:2 * D]], [(0, 0, 1, 2 * D)], chain, carried, collected, record128, last_i,
                                    join_logsumexp(collected, carried))
                    with ExitStack() as s2:
                        new = sb(s2, "new", [P, NT, D])
                        tmp = sb(s2, "tmp2", [P, NT, D])
                        stat = sb(s2, "stat2", [P, 2, NT])
                        linear(new[:, :, :], hc, w_l[:, l, :], 2 * D, D, bias=vecs[:, 1 + 3 * l, :])
                        layer_norm_relu(agg, new[:, :, :], tmp[:, :, :], stat, vecs[:, 2 + 3 * l, :], vecs[:, 3 + 3 * l, :],
                                        blend=h_sb, add_to=x_sb[:, :, :] if l == 2 else None)

        def join_logsumexp(collected, carried):
            def join_vector(v, j, k, ka):
                m1, s1, m2, s2 = (t[:, j, f:f + D] for t in (collected, carried) for f in (0, D))
                top = agg[:, j, :]
                step(v, v.tensor_tensor(m2, m2, over(nocarry[:, j], D), ALU.add), vec, k + 1)
                step(v, v.tensor_tensor(top, m1, m2, ALU.max), vec, k + 2)
                v.tensor_tensor(m1, m1, top, ALU.subtract)
                v.tensor_tensor(m2, m2, top, ALU.subtract).then_inc(vec.sem, 1)
                v.wait_ge(act.sem, act.base + ka + 1)
                v.tensor_tensor(s1, s1, m1, ALU.mult)
                step(v, v.tensor_tensor(s2, s2, m2, ALU.mult), vec, k + 4)
                step(v, v.tensor_tensor(s1, s1, s2, ALU.add), vec, k + 5)
                v.tensor_scalar(s1, s1, 1e-30, None, ALU.max).then_inc(vec.sem, 1)
                v.wait_ge(act.sem, act.base + ka + 2)
                step(v, v.tensor_tensor(top, top, s1, ALU.add), vec, k + 7)
                v.tensor_tensor(top, top, over(has[:, j], D), ALU.mult)

            def join_scalar(s, j, k):
                m1, s1, m2 = collected[:, j, 0:D], collected[:, j, D:2 * D], carried[:, j, 0:D]
                s.wait_ge(vec.sem, vec.base + k + 3)
                s.activation(m1, m1, ACT.Exp)
                s.activation(m2, m2, ACT.Exp).then_inc(act.sem, 1)
                s.wait_ge(vec.sem, vec.base + k + 6)
                s.activation(s1, s1, ACT.Ln).then_inc(act.sem, 1)

            return 7, 2, join_vector, join_scalar

        def batch_norm(dst, src, tmp, gamma, beta, relu):
            with ExitStack() as st:
                mean = sb(st, "mean", [P, D])
                scale = sb(st, "scale", [P, 2, D])
                with nc.Block() as block:
                    @block.tensor
                    def _(pe):
                        for k, what in enumerate((src, dst)):
                            if k == 1:
                                pe.wait_ge(vec.sem, vec.base + 3)
                            for j in range(NT):
                                last = nc.tensor.matmul(bank[k][:, 0:D], (ones_last if j == NT - 1 else ones)[:, :], what[:, j, :],
                                                        start=j == 0, stop=j == NT - 1)
                            last.then_inc(mm.sem, 1)

                    @block.vector
                    def _(v):
                        v.wait_ge(mm.sem, mm.base + 1)
                        step(v, v.tensor_scalar(mean[:, :], bank[0][:, 0:D], 1.0 / N, None, ALU.mult), vec, 1)
                        step(v, v.tensor_tensor(tmp, src, along(mean[:, :], NT), ALU.subtract), vec, 2)
                        v.tensor_tensor(dst, tmp, tmp, ALU.mult).then_inc(vec.sem, 1)
                        v.wait_ge(mm.sem, mm.base + 2)
                        v.tensor_scalar(scale[:, 0, :], bank[1][:, 0:D], 1.0 / N, 1e-5, ALU.mult, ALU.add).then_inc(vec.sem, 1)
                        v.wait_ge(act.sem, act.base + 1)
                        step(v, v.reciprocal(scale[:, 0, :], scale[:, 1, :]), vec, 5)
                        step(v, v.tensor_tensor(scale[:, 0, :], scale[:, 0, :], gamma, ALU.mult), vec, 6)
                        step(v, v.tensor_tensor(tmp, tmp, along(scale[:, 0, :], NT), ALU.mult), vec, 7)
                        step(v, v.tensor_tensor(dst, tmp, along(beta, NT), ALU.add), vec, 8)
                        if relu:
                            v.tensor_scalar(dst, dst, 0.0, None, ALU.max)

                    @block.scalar
                    def _(s):
                        s.wait_ge(vec.sem, vec.base + 4)
                        s.activation(scale[:, 1, :], scale[:, 0, :], ACT.Sqrt).then_inc(act.sem, 1)
                mm.base += 2
                vec.base += 8
                act.base += 1

        def edges_weighted_sum(rec, weight):
            n_sh = S * EP // (2 * PAIRS * P)
            sh_from = a["edge9"].rearrange("s t c -> (s t c)").rearrange("(g p n) -> p g n", p=P, n=n_sh)
            sh_to = sh_parts.rearrange("m s t c -> m (s t c)").rearrange("m (g p n) -> m p g n", p=P, n=n_sh)
            with ExitStack() as st:
                full = sb(st, "full", [P, 2, n_sh])
                part = sb(st, "part", [P, 3, n_sh], BF16)
                sh_here = [signal("harmonics_here0"), signal("harmonics_here1")]
                sh_step, sh_kept = signal("harmonics_split"), signal("harmonics_stored")
                got = [sb(st, f"got{b}", [P, T, D]) for b in range(2)]
                index = sb(st, "index", [P, 2, T], I32)
                cont_t = sb(st, "cont_t", [P, T])
                filled = [signal(f"sum_rows_here{b}") for b in range(2)]
                done = [signal(f"sum_record_ready{b}") for b in range(2)]
                kept = [signal(f"sum_record_stored{b}") for b in range(2)]
                with nc.Block() as block:
                    @block.gpsimd
                    def _(g):
                        with g.Fori(0, PAIRS) as i:
                            for b in range(2):
                                g.wait_ge(pool.sem, pool.base + 2 * i + b)
                                g.wait_ge(done[b].sem, i + 1)
                                hold(g).then_inc(pool.sem, 1)
                                gathers(g, index[:, b, :], got[b], filled[b].sem, table)

                    @block.vector
                    def _(v):
                        v.memset(part[:, 0, 0:1], 0.0).then_inc(sh_step.sem, 1)
                        v.tensor_copy(index[:, :, :], src_i[:, 0:2 * T].rearrange("p (b t) -> p b t", t=T))
                        v.memset(rec[1][:, T - 1, 0:D // 2], 0.0).then_inc(done[0].sem, 1)
                        v.memset(rec[1][:, T - 1, D // 2:D], 0.0).then_inc(done[1].sem, 1)
                        with v.Fori(0, PAIRS) as i:
                            for b in range(2):
                                v.wait_ge(done[1 - b].sem, i + b + 1)
                                f = full[:, b, :]

                                def link(k, ins):
                                    ins.then_inc(sh_step.sem, 1)
                                    v.wait_ge(sh_step.sem, i * 10 + (5 * b + k + 1))

                                v.wait_ge(sh_here[b].sem, i * 16 + 16)
                                v.wait_ge(sh_kept.sem, i * 96 + (48 * b + 16))
                                link(1, v.tensor_copy(part[:, 0, :], f))
                                link(2, v.tensor_tensor(f, f, part[:, 0, :], ALU.subtract))
                                link(3, v.tensor_copy(part[:, 1, :], f))
                                link(4, v.tensor_tensor(f, f, part[:, 1, :], ALU.subtract))
                                link(5, v.tensor_copy(part[:, 2, :], f))
                                v.tensor_scalar(cont_t[:, :], neg[:, bass.ds((i * 2 + b) * T, T)], 0.0, None, ALU.is_equal)
                                v.wait_ge(filled[b].sem, 16 * T * (i + 1))
                                next_index(v, index[:, b, :], i, b)
                                v.tensor_tensor(got[b][:, :, :], got[b][:, :, :], over(weight[:, bass.ds((i * 2 + b) * T, T)], D), ALU.mult).then_inc(vec.sem, 1)
                                v.wait_ge(vec.sem, vec.base + 2 * i + b + 1)
                                v.wait_ge(kept[b].sem, 16 * i + 16)
                                for f in range(D):
                                    last = v.tensor_tensor_scan(rec[b][:, :, f], cont_t[:, :], got[b][:, :, f], rec[1 - b][:, T - 1, f:f + 1], ALU.mult, ALU.add)
                                last.then_inc(done[b].sem, 1)

                    @block.scalar
                    def _(s):
                        s.dma_start(spare_net[:, :], holder[:, 0:1]).then_inc(sh_kept.sem, 16)
                        with s.Fori(0, PAIRS) as i:
                            for b in range(2):
                                s.wait_ge(sh_step.sem, i * 10 + (5 * b + 1))
                                s.dma_start(full[:, b, :], sh_from[:, bass.ds(i * 2 + b, 1), :].rearrange("p g n -> p (g n)")).then_inc(sh_here[b].sem, 16)
                                s.wait_ge(sh_step.sem, i * 10 + (5 * b + 6))
                                for m in range(3):
                                    s.dma_start(sh_to[m][:, bass.ds(i * 2 + b, 1), :].rearrange("p g n -> p (g n)"), part[:, m, :]).then_inc(sh_kept.sem, 16)
                        s.wait_ge(sh_kept.sem, 16 + 96 * PAIRS)

                    @block.sync
                    def _(sp):
                        start_count(sp, kept)
                        with sp.Fori(0, PAIRS) as i:
                            for b in range(2):
                                sp.wait_ge(done[b].sem, i + 2)
                                sp.dma_start(edges(record64)[:, bass.ds((i * 2 + b) * T, T), :], rec[b][:, :, :]).then_inc(kept[b].sem, 16)
                        for b in range(2):
                            sp.wait_ge(kept[b].sem, 16 * PAIRS + 16)
                pool.base += 2 * PAIRS
                vec.base += 2 * PAIRS

        def weighted_sum_layer():
            with ExitStack() as st:
                w = sb(st, "w", [D, 2, D])
                vecs = sb(st, "vecs", [P, 6, D])
                weight = sb(st, "weight_e", [P, CHUNK])
                load_weights([(w[:, 0, :], a["L1_gnn_W1"]), (w[:, 1, :], a["L1_gnn_W2"]),
                              (weight[:, :], a["edge_weight"].rearrange("(c t) -> c t", c=P))]
                             + [(vecs[:, n, :], spread(a[f"L1_gnn_{name}"]))
                                for n, name in enumerate(("b1", "gamma1", "beta1", "b2", "gamma2", "beta2"))])
                with ExitStack() as s2:
                    tmp = sb(s2, "tmp", [P, NT, D])
                    stat = sb(s2, "stat", [P, 2, NT])
                    layer_norm_relu(h_sb, x_sb[:, :, :], tmp[:, :, :], stat)
                store_nodes([(table, h_sb)])
                with ExitStack() as s2:
                    rec = [sb(s2, f"rec{b}", [P, T, D]) for b in range(2)]
                    edges_weighted_sum(rec, weight)
                    collected = sb(s2, "collected", [P, NT, D])
                    carried = sb(s2, "carried", [P, NT, D])
                    chain = sb(s2, "chain", [P, D])

                    def join_vector(v, j, k, ka):
                        step(v, v.tensor_tensor(collected[:, j, :], collected[:, j, :], over(has[:, j], D), ALU.mult), vec, k + 1)
                        step(v, v.tensor_tensor(collected[:, j, :], collected[:, j, :], carried[:, j, :], ALU.add), vec, k + 2)
                        v.tensor_tensor(agg[:, j, :], collected[:, j, :], h_sb[:, j, :], ALU.add)

                    collect(D, None, [rec[1][:, T - 1, :]], [(0, 0, 1, D)], chain, carried, collected, record64, last_i,
                            (2, 0, join_vector, None))
                with ExitStack() as s2:
                    mid = sb(s2, "mid", [P, NT, D])
                    tmp = sb(s2, "tmp", [P, NT, D])
                    for k in range(2):
                        linear(mid[:, :, :], agg, w[:, k, :], D, D, bias=vecs[:, 3 * k, :])
                        batch_norm(agg, mid[:, :, :], tmp[:, :, :], vecs[:, 3 * k + 1, :], vecs[:, 3 * k + 2, :], True)
                    with nc.Block() as block:
                        @block.vector
                        def _(v):
                            v.tensor_tensor(x_sb[:, :, :], x_sb[:, :, :], agg, ALU.add)

        def edges_attention(rec):
            C = 2 * T2
            W = O + 2 * H
            K5 = 5
            with ExitStack() as st:
                c_w = sb(st, "c_w", [P, K5, 2 * O])
                pick = sb(st, "pick", [3 * S, K5, 2, D], BF16)
                xg = [sb(st, f"xg{b}", [P, G, 2 * D]) for b in range(2)]
                qg = [sb(st, f"qg{b}", [P, G, O]) for b in range(2)]
                wg = [sb(st, f"wg{b}", [P, G, 2 * O]) for b in range(2)]
                sh = [sb(st, f"sh{b}", [3 * S, G, P], BF16) for b in range(2)]
                vv = [sb(st, f"vv{b}", [P, T2, O]) for b in range(2)]
                logit = [sb(st, f"logit{b}", [P, T2, H]) for b in range(2)]
                neg_t = [sb(st, f"neg_t{b}", [P, T2]) for b in range(2)]
                fall = sb(st, "fall", [P, T2, H])
                xt = [sb(st, f"xt{k}", [P, P]) for k in range(2)]
                zt = [sb(st, f"zt{k}", [P, K5, P]) for k in range(2)]
                kk = [sb(st, f"kk{k}", [P, O]) for k in range(2)]
                index = sb(st, "index", [P, 2, 2, G], I32)
                filled = [signal(f"att_rows_here{b}") for b in range(2)]
                inputs = [signal(f"att_edges_here{b}") for b in range(2)]
                kept = [signal(f"att_record_stored{b}") for b in range(2)]
                tails = [signal(f"att_record_ready{b}") for b in range(2)]
                left = [signal(f"att_rows_used{b}") for b in range(2)]
                primed = sb(st, "primed", [P, 32])
                turned, xt_ready, z_ready = signal("x_turned_sh_spread"), signal("xt_ready"), signal("z_ready")
                products, joined = signal("products_done"), signal("kv_joined")
                tail_v, tail_a = signal("tail_vec"), signal("tail_exp")
                chain_v = signal("column_vec")

                def done(i, c):
                    return i * C + (c + 4)

                load_weights([(c_w[:, 0:4, 0:O], a["L2_gnn_Cqk_s"][0:512, :].rearrange("(k p) o -> p k o", p=P)),
                              (c_w[:, 0:4, O:2 * O], a["L2_gnn_Cv_s"][0:512, :].rearrange("(k p) o -> p k o", p=P)),
                              (c_w[0:D, 4, 0:O], a["L2_gnn_Cqk_s"][512:576, :]), (c_w[0:D, 4, O:2 * O], a["L2_gnn_Cv_s"][512:576, :]),
                              ])

                with nc.Block() as block:
                    @block.gpsimd
                    def _(g):
                        step(g, g.memset(pick[:, :, :, :], 0.0), pool, 1)
                        for part in range(3):
                            step(g, g.affine_select(out=pick[:, :, :, :], in_=pick[:, :, :, :], compare_op=ALU.not_equal, fill=1.0,
                                                    base=-S * part, pattern=[[-2, K5], [-1, 2], [0, D]], channel_multiplier=1), pool, 2 + part)
                        pool.base += 4
                        with g.Fori(0, PAIRS2) as i:
                            for u in range(4):
                                b = u % 2
                                g.wait_ge(left[b].sem, i * 2 + (u // 2 + 1))
                                g.tensor_copy(index[:, b, 0, :], src_i[:, bass.ds((i * 4 + u) * G, G)])
                                g.tensor_copy(index[:, b, 1, :], dst_i[:, bass.ds((i * 4 + u) * G, G)]).then_inc(pool.sem, 1)
                                g.wait_ge(pool.sem, i * 4 + (pool.base + u + 1))
                                hold(g)
                                gathers(g, index[:, b, 0, :], xg[b], filled[b].sem, table_hh)
                                gathers(g, index[:, b, 1, :], qg[b], filled[b].sem, table_q)

                    @block.sync
                    def _(sp):
                        def load(g, b, used):
                            sp.wait_ge(left[b].sem, used)
                            sp.dma_start(wg[b][:, :, :], edges(edge_net)[:, bass.ds(g * G, G), :]).then_inc(inputs[b].sem, 16)
                            sp.dma_start(sh[b][:, :, :], sh_parts.rearrange("k s t c -> (k s) t c")[:, bass.ds(g * G, G), :]).then_inc(inputs[b].sem, 16)

                        def store(g, b, ready):
                            sp.wait_ge(tails[b].sem, ready)
                            sp.dma_start(edges(record144)[:, bass.ds(g * T2, T2), :], rec[b][:, :, :]).then_inc(kept[b].sem, 16)

                        def ahead(i, b, more):
                            for u in range(2 * more):
                                load(i * 4 + (2 * b + 2 + u), u, i * 2 + (b + 2))
                            store(i * 2 + b, 1 - b, i + 2)

                        start_count(sp, kept)
                        load(0, 0, 1)
                        load(1, 1, 1)
                        with sp.Fori(0, PAIRS2 - 1) as i:
                            ahead(i, 0, 1)
                            ahead(i, 1, 1)
                        ahead(PAIRS2 - 1, 0, 1)
                        ahead(PAIRS2 - 1, 1, 0)
                        store(2 * PAIRS2, 1, PAIRS2 + 2)
                        sp.wait_ge(kept[0].sem, 16 * (PAIRS2 + 1))
                        sp.wait_ge(kept[1].sem, 16 * (PAIRS2 + 2))

                    @block.tensor
                    def _(pe):
                        for k in range(3):
                            for bk, sem in ((0, turned), (6, products)):
                                nc.tensor.matmul(bank[bk][:, 0:P], ident[:, :], ident[:, :], start=True, stop=True).then_inc(sem.sem, 1)
                        pe.wait_ge(pool.sem, pool.base)

                        def turn(i, c):
                            u, t = c // G, c % G
                            b, w = u % 2, wide[c % 2]
                            if t == 0:
                                pe.wait_ge(filled[b].sem, i * (64 * G) + 32 * G * (u // 2 + 1))
                                pe.wait_ge(inputs[b].sem, i * 64 + 32 * (u // 2 + 1))
                            pe.wait_ge(z_ready.sem, done(i, c - 2))
                            for k in range(K5):
                                nc.tensor.matmul(w[:, k * P:(k + 1) * P], pick[:, k, :, :].rearrange("r a d -> r (a d)"), sh[b][:, t, :], start=True, stop=True)
                            nc.tensor.transpose(w[:, K5 * P:(K5 + 1) * P], xg[b][:, t, :], ident[:, :]).then_inc(turned.sem, 1)

                        with pe.Fori(0, PAIRS2) as i:
                            for c in range(C):
                                b, t, q = (c // G) % 2, c % G, c % 2
                                if c == 0:
                                    turn(i, 0)
                                if c + 1 < C:
                                    turn(i, c + 1)
                                pe.wait_ge(z_ready.sem, done(i, c))
                                pe.wait_ge(joined.sem, done(i, c - 2))
                                for k in range(K5):
                                    last = nc.tensor.matmul(bank[6 + q][:, 0:2 * O], zt[q][:, k, :], c_w[:, k, :], start=k == 0, stop=k == K5 - 1)
                                last.then_inc(products.sem, 1)

                    @block.scalar
                    def _(s):
                        for k in range(3):
                            s.activation(primed[:, k:k + 1], holder[:, 0:1], ACT.Copy).then_inc(xt_ready.sem, 1)

                        def keep_xt(i, c):
                            s.wait_ge(turned.sem, done(i, c))
                            s.wait_ge(z_ready.sem, done(i, c - 2))
                            s.activation(xt[c % 2][:, :], wide[c % 2][:, K5 * P:(K5 + 1) * P], ACT.Copy).then_inc(xt_ready.sem, 1)

                        with s.Fori(0, PAIRS2) as i:
                            for c in range(C):
                                b, t, q = c // T2, c % T2, c % 2
                                if c == 0:
                                    keep_xt(i, 0)
                                if c + 1 < C:
                                    keep_xt(i, c + 1)
                                if t == 2:
                                    s.wait_ge(tail_v.sem, i * 8 + (4 * b + 3))
                                    s.activation(fall[:, :, :], fall[:, :, :], ACT.Exp)
                                    s.activation(logit[1 - b][:, :, :], logit[1 - b][:, :, :], ACT.Exp).then_inc(tail_a.sem, 1)
                        s.wait_ge(tail_v.sem, 4 * 2 * PAIRS2 + 3)
                        s.activation(fall[:, :, :], fall[:, :, :], ACT.Exp)
                        s.activation(logit[1][:, :, :], logit[1][:, :, :], ACT.Exp).then_inc(tail_a.sem, 1)

                    @block.vector
                    def _(v):
                        v.memset(vv[1][:, :, :], 0.0)
                        v.memset(logit[1][:, :, :], 0.0)
                        v.memset(neg_t[1][:, :], 0.0)
                        v.memset(rec[0][:, T2 - 1, :], 0.0).then_inc(tails[0].sem, 1)
                        v.memset(rec[1][:, T2 - 1, :], 0.0).then_inc(tails[1].sem, 1)
                        v.memset(c_w[D:P, 4, :], 0.0)
                        for k in range(3):
                            v.memset(primed[:, 16 + k:17 + k], 0.0).then_inc(z_ready.sem, 1)
                            v.memset(primed[:, 20 + k:21 + k], 0.0).then_inc(joined.sem, 1)
                        for b in range(2):
                            v.memset(primed[:, 24 + b:25 + b], 0.0).then_inc(left[b].sem, 1)

                        def outer(i, c):
                            v.wait_ge(xt_ready.sem, done(i, c))
                            v.wait_ge(products.sem, done(i, c - 2))
                            v.tensor_tensor(zt[c % 2][:, :, :], wide[c % 2][:, 0:K5 * P].rearrange("p (k e) -> p k e", e=P),
                                            along(xt[c % 2][:, :], K5), ALU.mult).then_inc(z_ready.sem, 1)

                        def tail(n, pb, t, before, free, columns):
                            now, past = rec[pb], rec[1 - pb]
                            p, m_now, m_past = logit[pb], now[:, :, O:O + H], past[:, T2 - 1, O:O + H]
                            if t == 0:
                                v.wait_ge(joined.sem, columns)
                                v.wait_ge(tails[1 - pb].sem, before)
                                v.wait_ge(kept[pb].sem, free)
                                for h in range(H):
                                    last = v.tensor_tensor_scan(now[:, :, O + h], neg_t[pb][:, :], p[:, :, h], past[:, T2 - 1, O + h:O + h + 1], ALU.add, ALU.max)
                                last.then_inc(tail_v.sem, 1)
                            elif t == 1:
                                v.wait_ge(tail_v.sem, n * 4 + 1)
                                v.tensor_tensor(fall[:, 0, :], m_past, now[:, 0, O:O + H], ALU.subtract)
                                v.tensor_tensor(fall[:, 1:T2, :], now[:, 0:T2 - 1, O:O + H], now[:, 1:T2, O:O + H], ALU.subtract)
                                v.tensor_tensor(p[:, :, :], p[:, :, :], m_now, ALU.subtract).then_inc(tail_v.sem, 1)
                                v.wait_ge(tail_v.sem, n * 4 + 2)
                                v.tensor_tensor(fall[:, :, :], fall[:, :, :], over(neg_t[pb][:, :], H), ALU.add).then_inc(tail_v.sem, 1)
                            elif t == 4:
                                v.wait_ge(tail_a.sem, n + 1)
                                for h in range(H):
                                    v.tensor_tensor_scan(now[:, :, O + H + h], fall[:, :, h], p[:, :, h], past[:, T2 - 1, O + H + h:O + H + h + 1], ALU.mult, ALU.add)
                            elif 5 <= t < 9:
                                t0 = (t - 5) * (T2 // 4)
                                part = vv[pb][:, t0:t0 + T2 // 4, :].rearrange("p t (h d) -> p t h d", d=DH)
                                pr = p[:, t0:t0 + T2 // 4, :]
                                last = v.tensor_tensor(part, part, pr.unsqueeze(3).to_broadcast([P, T2 // 4, H, DH]), ALU.mult)
                                if t == 8:
                                    last.then_inc(tail_v.sem, 1)
                            elif t >= 10:
                                if t == 10:
                                    v.wait_ge(tail_v.sem, n * 4 + 4)
                                slots = T2 - 10
                                for o in range((t - 10) * O // slots, (t - 9) * O // slots):
                                    last = v.tensor_tensor_scan(now[:, :, o], fall[:, :, o // DH], vv[pb][:, :, o], past[:, T2 - 1, o:o + 1], ALU.mult, ALU.add)
                                if t == T2 - 1:
                                    last.then_inc(tails[pb].sem, 1)

                        with v.Fori(0, PAIRS2) as i:
                            for c in range(C):
                                b, t, q = c // T2, c % T2, c % 2
                                if c == 0:
                                    outer(i, 0)
                                if c + 1 < C:
                                    outer(i, c + 1)
                                tail(i * 2 + b, 1 - b, t, i + (b + 1), i * 16 + 16, i * C + (b * T2 + 3))
                                if t == 0:
                                    v.tensor_copy(neg_t[b][:, :], neg[:, bass.ds((i * 2 + b) * T2, T2)])
                                v.wait_ge(products.sem, done(i, c))
                                u, w = (c // G) % 2, wg[(c // G) % 2][:, c % G, :]
                                v.tensor_tensor(kk[q][:, :], bank[6 + q][:, 0:O], w[:, 0:O], ALU.mult).then_inc(chain_v.sem, 1)
                                v.wait_ge(chain_v.sem, i * (2 * C) + (2 * c + 1))
                                v.tensor_tensor(kk[q][:, :], kk[q][:, :], qg[u][:, c % G, :], ALU.mult).then_inc(chain_v.sem, 1)
                                last = v.tensor_tensor(vv[b][:, t, :], bank[6 + q][:, O:2 * O], w[:, O:2 * O], ALU.mult)
                                if c % G == G - 1:
                                    last.then_inc(left[(c // G) % 2].sem, 1)
                                v.wait_ge(chain_v.sem, i * (2 * C) + (2 * c + 2))
                                v.tensor_reduce(logit[b][:, t, :], kk[q][:, :].rearrange("p (h d) -> p h d", d=DH), X, ALU.add).then_inc(joined.sem, 1)
                        for t in range(T2):
                            tail(2 * PAIRS2, 1, t, PAIRS2 + 1, 16 * (PAIRS2 + 1), PAIRS2 * C + 3)
                pool.base += 4 * PAIRS2

        def join_softmax(top, collected, carried, heads, width, own=None):
            O1 = heads * width
            parts_all = [collected, carried] + ([own] if own is not None else [])
            vec_steps = 10 if own is None else 12

            def join_vector(v, j, k, ka):
                n = [k]

                def link(ins):
                    n[0] += 1
                    step(v, ins, vec, n[0])

                tiles = j.stop - j.start
                parts = [(t[:, j, 0:O1], t[:, j, O1:O1 + heads], t[:, j, O1 + heads:O1 + 2 * heads]) for t in parts_all]
                (u1, m1, s1), (_, m2, _) = parts[0:2]
                tp = top[:, j, :]
                link(v.tensor_tensor(m2, m2, over(nocarry[:, j], heads), ALU.add))
                link(v.tensor_scalar(tp, over(has[:, j], heads), 0.0, NEG, ALU.is_equal, ALU.mult))
                link(v.tensor_tensor(m1, m1, over(has[:, j], heads), ALU.mult))
                link(v.tensor_tensor(m1, m1, tp, ALU.add))
                link(v.tensor_tensor(tp, m1, m2, ALU.max))
                if own is not None:
                    link(v.tensor_tensor(tp, tp, parts[2][1], ALU.max))
                for _, m, _ in parts:
                    last = v.tensor_tensor(m, m, tp, ALU.subtract)
                link(last)
                v.wait_ge(act.sem, act.base + ka + 1)
                for u, m, s in parts:
                    v.tensor_tensor(s, s, m, ALU.mult)
                    uh = u.rearrange("p j (h d) -> p j h d", d=width)
                    last = v.tensor_tensor(uh, uh, m.unsqueeze(3).to_broadcast([P, tiles, heads, width]), ALU.mult)
                link(last)
                for u, _, s in parts[1:]:
                    v.tensor_tensor(s1, s1, s, ALU.add)
                    link(v.tensor_tensor(u1, u1, u, ALU.add))
                link(v.tensor_scalar(s1, s1, 1e-16, None, ALU.add))
                link(v.reciprocal(m1, s1))
                uh = u1.rearrange("p j (h d) -> p j h d", d=width)
                v.tensor_tensor(uh, uh, m1.unsqueeze(3).to_broadcast([P, tiles, heads, width]), ALU.mult)

            def join_scalar(s, j, k):
                s.wait_ge(vec.sem, vec.base + k + (6 if own is None else 7))
                for t in parts_all:
                    m = t[:, j, O1:O1 + heads]
                    last = s.activation(m, m, ACT.Exp)
                last.then_inc(act.sem, 1)

            return vec_steps, 1, join_vector, join_scalar

        def attention_layer():
            W = O + 2 * H
            with ExitStack() as s2:
                tmp = sb(s2, "tmp", [P, NT, D])
                stat = sb(s2, "stat", [P, 2, NT])
                wq = sb(s2, "wq", [D, O])
                q = sb(s2, "q_nodes", [P, NT, O])
                load_weights([(wq[:, :], a["L2_gnn_Wq"])])
                layer_norm_relu(h_sb, x_sb[:, :, :], tmp[:, :, :], stat)
                linear(q[:, :, :], h_sb, wq[:, :], D, O)
                store_nodes([(table_hh[:, 0:D], h_sb), (table_hh[:, D:2 * D], h_sb), (table_q, q[:, :, :])])
            with ExitStack() as s1:
                last_rec = sb(s1, "last_rec", [P, W])
                with ExitStack() as s2:
                    rec = [sb(s2, f"rec{b}", [P, T2, W]) for b in range(2)]
                    edges_attention(rec)
                    with nc.Block() as block:
                        @block.vector
                        def _(v):
                            v.tensor_copy(last_rec[:, :], rec[1][:, T2 - 1, :])
                upd = sb(s1, "collected", [P, NT, W])
                with ExitStack() as s2:
                    tail_m = sb(s2, "tail_m", [P, O])
                    tail_s = sb(s2, "tail_s", [P, O])
                    chain = sb(s2, "chain", [P, W])
                    carried = sb(s2, "carried", [P, NT, W])
                    top = sb(s2, "top", [P, NT, H])
                    with nc.Block() as block:
                        @block.vector
                        def _(v):
                            v.tensor_copy(tail_m[:, :].rearrange("p (h d) -> p h d", d=DH), over(last_rec[:, O:O + H], DH))
                            v.tensor_copy(tail_s[:, :].rearrange("p (h d) -> p h d", d=DH), over(last_rec[:, O + H:W], DH))
                    collect(O, tail_m[:, :], [last_rec[:, 0:O], tail_s[:, :]],
                            [(0, O, 1, O), (O, 0, DH, H), (O + H, 2 * O, DH, H)], chain, carried, upd, record144, last144_i,
                            join_softmax(top, upd, carried, H, DH))
                w_out = sb(s1, "w_out", [O, D])
                w_self = sb(s1, "w_self", [D, D])
                vecs = sb(s1, "vecs", [P, 2, D])
                total = sb(s1, "total", [P, NT, D])
                tmp = sb(s1, "tmp", [P, NT, D])
                load_weights([(w_out[:, :], a["L2_gnn_W_out"]), (w_self[:, :], a["L2_gnn_W_self"]),
                              (vecs[:, 0, :], spread(a["L2_gnn_gamma"])), (vecs[:, 1, :], spread(a["L2_gnn_beta"]))])
                linear(tmp[:, :, :], upd[:, :, 0:O], w_out[:, :], O, D)
                linear(total[:, :, :], h_sb, w_self[:, :], D, D, add_to=tmp[:, :, :])
                batch_norm(agg, total[:, :, :], tmp[:, :, :], vecs[:, 0, :], vecs[:, 1, :], False)
                with nc.Block() as block:
                    @block.vector
                    def _(v):
                        v.tensor_tensor(x_sb[:, :, :], x_sb[:, :, :], agg, ALU.add)

        def edges_graph(tag, rec, own, alphas, a_src, a_dst):
            before = vec.base
            hw, alpha_s, alpha_d, own_logit = own[:, :, 0:D], alphas[:, 0, :], alphas[:, 1, :], alphas[:, 2, :]
            with ExitStack() as st:
                ade = sb(st, "ade", [P, CHUNK])
                cont = sb(st, "cont", [P, CHUNK])
                firsts = sb(st, "firsts", [P, CHUNK])
                chunk_row = sb(st, "chunk_row", [P, D + 2])
                got = [sb(st, f"got{b}", [P, T, D + 2]) for b in range(2)]
                index = sb(st, "index", [P, 2, T], I32)
                neg_t = sb(st, "neg_t", [P, T])
                p = sb(st, "p", [P, T])
                raw = sb(st, "raw", [P, T])
                fall = sb(st, "fall", [P, T])
                M, Z = D, D + 1
                filled = [signal(f"{tag}_rows_here{b}") for b in range(2)]
                done = [signal(f"{tag}_record_ready{b}") for b in range(2)]
                kept = [signal(f"{tag}_record_stored{b}") for b in range(2)]
                with nc.Block() as block:
                    @block.gpsimd
                    def _(g):
                        g.wait_ge(vec.sem, before + 2)
                        step(g, hold(g), pool, 1)
                        for j in range(NT):
                            nc.gpsimd.indirect_dma_start(by_first, bass.IndirectOffsetOnAxis(ap=first_i[:, j:j + 1], axis=0),
                                                         alpha_d[:, j:j + 1], None).then_inc(rows.sem, 16)
                        g.wait_ge(stored.sem, stored.base + 16)
                        step(g, hold(g), pool, 2)
                        pool.base += 2
                        nc.gpsimd.indirect_dma_start(chunk_row[:, :], None, table_a,
                                                     bass.IndirectOffsetOnAxis(ap=chunk_dst[:, 0:1], axis=0)).then_inc(chunk_rows.sem, 16)
                        with g.Fori(0, PAIRS) as i:
                            for b in range(2):
                                g.wait_ge(pool.sem, pool.base + 2 * i + b)
                                g.wait_ge(done[b].sem, i + 1)
                                hold(g).then_inc(pool.sem, 1)
                                gathers(g, index[:, b, :], got[b], filled[b].sem, table_a)

                    @block.vector
                    def _(v):
                        v.tensor_copy(index[:, :, :], src_i[:, 0:2 * T].rearrange("p (b t) -> p b t", t=T))
                        v.memset(rec[1][:, T - 1, 0:D], 0.0).then_inc(done[0].sem, 1)
                        v.memset(rec[1][:, T - 1, D:D + 2], 0.0).then_inc(done[1].sem, 1)
                        step(v, v.tensor_tensor(agg, hw, along(a_dst, NT), ALU.mult), vec, 1)
                        step(v, v.tensor_reduce(alpha_d, agg, X, ALU.add), vec, 2)
                        step(v, v.tensor_tensor(agg, hw, along(a_src, NT), ALU.mult), vec, 3)
                        step(v, v.tensor_reduce(alpha_s, agg, X, ALU.add), vec, 4)
                        v.tensor_copy(own[:, :, D], alpha_s)
                        v.tensor_copy(own[:, :, D + 1], alpha_d).then_inc(vec.sem, 1)
                        v.wait_ge(vec.sem, before + 5)
                        step(v, v.tensor_tensor(own_logit, alpha_s, alpha_d, ALU.add), vec, 6)
                        v.wait_ge(stored.sem, stored.base + 16)
                        v.scalar_tensor_tensor(own[:, :, D], own_logit, 0.2, own_logit, ALU.mult, ALU.max)
                        v.memset(own[:, :, D + 1], 1.0)
                        v.tensor_scalar(cont[:, :], neg[:, :], 0.0, None, ALU.is_equal).then_inc(vec.sem, 1)
                        v.wait_ge(chunk_rows.sem, chunk_rows.base + 16)
                        v.wait_ge(loaded.sem, loaded.base + 16)
                        v.tensor_copy(firsts[:, 0:1], chunk_row[:, D + 1:D + 2]).then_inc(vec.sem, 1)
                        v.wait_ge(vec.sem, vec.base + 8)
                        step(v, v.tensor_tensor_scan(ade[:, :], cont[:, :], firsts[:, :], 0.0, ALU.mult, ALU.add), vec, 9)
                        vec.base += 9
                        with v.Fori(0, PAIRS) as i:
                            for b in range(2):
                                now, past = rec[b], rec[1 - b]

                                def link(k, ins):
                                    ins.then_inc(vec.sem, 1)
                                    v.wait_ge(vec.sem, i * 14 + (vec.base + 7 * b + k))

                                v.wait_ge(done[1 - b].sem, i + b + 1)
                                v.tensor_copy(neg_t[:, :], neg[:, bass.ds((i * 2 + b) * T, T)])
                                v.wait_ge(filled[b].sem, 16 * T * (i + 1))
                                next_index(v, index[:, b, :], i, b)
                                link(1, v.tensor_tensor(raw[:, :], got[b][:, :, D], ade[:, bass.ds((i * 2 + b) * T, T)], ALU.add))
                                link(2, v.scalar_tensor_tensor(p[:, :], raw[:, :], 0.2, raw[:, :], ALU.mult, ALU.max))
                                v.wait_ge(kept[b].sem, 16 * i + 16)
                                link(3, v.tensor_tensor_scan(now[:, :, M], neg_t[:, :], p[:, :], past[:, T - 1, M:M + 1], ALU.add, ALU.max))
                                v.tensor_tensor(fall[:, 0:1], past[:, T - 1, M:M + 1], now[:, 0, M:M + 1], ALU.subtract)
                                v.tensor_tensor(fall[:, 1:T], now[:, 0:T - 1, M], now[:, 1:T, M], ALU.subtract)
                                link(4, v.tensor_tensor(p[:, :], p[:, :], now[:, :, M], ALU.subtract))
                                link(5, v.tensor_tensor(fall[:, :], fall[:, :], neg_t[:, :], ALU.add))
                                v.wait_ge(act.sem, act.base + 2 * i + b + 1)
                                link(6, v.tensor_tensor(got[b][:, :, 0:D], got[b][:, :, 0:D], over(p[:, :], D), ALU.mult))
                                link(7, v.tensor_tensor_scan(now[:, :, Z], fall[:, :], p[:, :], past[:, T - 1, Z:Z + 1], ALU.mult, ALU.add))
                                for f in range(D):
                                    last = v.tensor_tensor_scan(now[:, :, f], fall[:, :], got[b][:, :, f], past[:, T - 1, f:f + 1], ALU.mult, ALU.add)
                                last.then_inc(done[b].sem, 1)

                    @block.scalar
                    def _(s):
                        with s.Fori(0, PAIRS) as i:
                            for b in range(2):
                                s.wait_ge(vec.sem, i * 14 + (vec.base + 7 * b + 5))
                                s.activation(fall[:, :], fall[:, :], ACT.Exp)
                                s.activation(p[:, :], p[:, :], ACT.Exp).then_inc(act.sem, 1)

                    @block.sync
                    def _(sp):
                        sp.wait_ge(vec.sem, before + 5)
                        sp.dma_start(nodes(table_a), own[:, :, :]).then_inc(stored.sem, 16)
                        sp.wait_ge(rows.sem, rows.base + 16 * NT)
                        sp.dma_start(firsts[:, :], by_first[0:EP, :].rearrange("(c t) o -> c (t o)", c=P)).then_inc(loaded.sem, 16)
                        start_count(sp, kept)
                        with sp.Fori(0, PAIRS) as i:
                            for b in range(2):
                                sp.wait_ge(done[b].sem, i + 2)
                                sp.dma_start(edges(record66)[:, bass.ds((i * 2 + b) * T, T), :], rec[b][:, :, :]).then_inc(kept[b].sem, 16)
                        for b in range(2):
                            sp.wait_ge(kept[b].sem, 16 * PAIRS + 16)
                pool.base += 2 * PAIRS
                vec.base += 14 * PAIRS
                act.base += 2 * PAIRS
                rows.base += 16 * NT
                loaded.base += 16
                stored.base += 16
                chunk_rows.base += 16

        def graph_attention_layers():
            W = D + 2
            with ExitStack() as st:
                w = sb(st, "w", [D, 3, D])
                vecs = sb(st, "vecs", [P, 9, D])
                alphas = sb(st, "alphas", [P, 3, NT])
                own = sb(st, "own", [P, NT, W])
                load_weights([(w[:, l, :], a[f"L3_gnn_W{l + 1}"]) for l in range(3)]
                             + [(vecs[:, 3 * l + n, :], spread(a[f"L3_gnn_{name}"]))
                                for l in range(3) for n, name in enumerate((f"a{l + 1}s", f"a{l + 1}d", f"b{l + 1}"))])
                with ExitStack() as s2:
                    tmp = sb(s2, "tmp", [P, NT, D])
                    stat = sb(s2, "stat", [P, 2, NT])
                    layer_norm_relu(h_sb, x_sb[:, :, :], tmp[:, :, :], stat)
                for l in range(3):
                    linear(own[:, :, 0:D], h_sb, w[:, l, :], D, D)
                    with ExitStack() as s2:
                        rec = [sb(s2, f"rec{b}", [P, T, W]) for b in range(2)]
                        edges_graph(f"gat{l}", rec, own, alphas, vecs[:, 3 * l, :], vecs[:, 3 * l + 1, :])
                        collected = sb(s2, "collected", [P, NT, W])
                        carried = sb(s2, "carried", [P, NT, W])
                        chain = sb(s2, "chain", [P, W])
                        tail_m = sb(s2, "tail_m", [P, D])
                        tail_s = sb(s2, "tail_s", [P, D])
                        top = sb(s2, "top", [P, NT, 1])
                        with nc.Block() as block:
                            @block.vector
                            def _(v):
                                v.tensor_copy(tail_m[:, :], rec[1][:, T - 1, D:D + 1].to_broadcast([P, D]))
                                v.tensor_copy(tail_s[:, :], rec[1][:, T - 1, D + 1:D + 2].to_broadcast([P, D]))
                        collect(D, tail_m[:, :], [rec[1][:, T - 1, 0:D], tail_s[:, :]],
                                [(0, D, 1, D), (D, 0, 1, 1), (D + 1, 2 * D, 1, 1)], chain, carried, collected, record66, last_i,
                                join_softmax(top, collected, carried, 1, D, own=own))
                        u = collected[:, :, 0:D]
                        with nc.Block() as block:
                            @block.vector
                            def _(v):
                                if l < 2:
                                    step(v, v.tensor_tensor(u, u, along(vecs[:, 3 * l + 2, :], NT), ALU.add), vec, 1)
                                    v.tensor_scalar(h_sb, u, 0.0, None, ALU.max)
                                else:
                                    step(v, v.tensor_tensor(u, u, along(vecs[:, 3 * l + 2, :], NT), ALU.add), vec, 1)
                                    v.tensor_tensor(x_sb[:, :, :], x_sb[:, :, :], u, ALU.add)
                        vec.base += 1

        load_and_flags()
        logsumexp_layers()
        weighted_sum_layer()
        attention_layer()
        clear_by_first()
        graph_attention_layers()

        with nc.Block() as block:
            @block.sync
            def _(sp):
                sp.dma_start(out[0:P * (NT - 1), :].rearrange("(j p) f -> p j f", p=P), x_sb[:, 0:NT - 1, :]).then_inc(stored.sem, 16)
                sp.dma_start(out[P * (NT - 1):N, :], x_sb[0:LAST, NT - 1, :]).then_inc(stored.sem, 16)
                sp.wait_ge(stored.sem, stored.base + 32)


def kernel(**inputs):
    import numpy as np
    import concourse.bacc as bacc
    from concourse.bass_utils import run_bass_kernel_spmd as run

    def padded(v, length, value, front=0):
        r = np.full((length,) + v.shape[1:], value, v.dtype)
        r[front:front + v.shape[0]] = v
        return r

    lay = {k: np.ascontiguousarray(v) for k, v in inputs.items()}
    arrays = {
        "x": lay["x"],
        "src_pad": padded(lay["src"], EP, 0),
        "dst_ext": padded(lay["dst"], EP + 1, N, front=1),
        "edge64": padded(np.ascontiguousarray(padded(lay["edge_attr_64"], EP, 0).reshape(P, CHUNK, D).transpose(1, 2, 0)),
                         CHUNK + T, 0).transpose(1, 0, 2).copy(),
        "edge9": np.ascontiguousarray(padded(lay["edge_attr_9"], EP, 0).reshape(P, CHUNK, S).transpose(2, 1, 0)),
        "edge_weight": padded(lay["edge_weight"], EP, 0),
        "L0_gnn_W_inT": np.ascontiguousarray(lay["L0_gnn_W_in"].T),
        "L0_gnn_W_lT": np.ascontiguousarray(lay["L0_gnn_W_l"].transpose(0, 2, 1)),
    }
    for name in ("Cqk", "Cv"):
        arrays[f"L2_gnn_{name}_s"] = np.ascontiguousarray(lay[f"L2_gnn_{name}"].transpose(1, 0, 2).reshape(S * D, O))
    arrays["dst_ext"][0] = -1
    for name, v in lay.items():
        if name[:3] in ("L0_", "L1_", "L2_", "L3_") and name not in ("L0_gnn_W_in", "L0_gnn_W_l", "L2_gnn_Cqk", "L2_gnn_Cv"):
            arrays[name] = v
    nc = bacc.Bacc("TRN2", target_bir_lowering=False, num_devices=1)
    aps = {name: nc.dram_tensor(f"in_{name}", v.shape, mybir.dt.from_np(v.dtype), kind="ExternalInput").ap()
           for name, v in arrays.items()}
    out = nc.dram_tensor("out_0", (N, D), F32, kind="ExternalOutput").ap()
    build_program(nc, aps, out)
    r = run(nc, [{f"in_{name}": v for name, v in arrays.items()}], core_ids=[0])
    return r.results[0]["out_0"]
```
